# Optimizing a Trainium2 kernel written in Bass

```python
import numpy as np
import jax
import jax.numpy as jnp

def _softmax(x, axis=-1):
    return jax.nn.softmax(x, axis=axis)

def _gelu(x):
    return jax.nn.gelu(x, approximate=True)

def _silu(x):
    return jax.nn.silu(x)

def _sigmoid(x):
    return jax.nn.sigmoid(x)

def _layernorm(x, axis=-1, eps=1e-05):
    m = jnp.mean(x, axis=axis, keepdims=True)
    v = jnp.var(x, axis=axis, keepdims=True)
    return (x - m) / jnp.sqrt(v + eps)

def _scatter_add(tgt, idx, src, axis=0):
    return tgt.at[idx].add(src)

def _segment_sum(src, seg, n):
    return jax.ops.segment_sum(src, seg, n)
kernel_name = 'mk_decoder_postln_d1_seqx_r4_52bd6b'

def setup_inputs(seed: int=0):
    np.random.seed(seed)
    _w = jnp.asarray

    def _rec_inputs():
        import jax
        import jax.numpy as jnp
        _rk = jax.random.key(seed)
        x = 0.0002417 + 0.9998 * jax.random.normal(jax.random.fold_in(_rk, 1), (16, 100, 256), jnp.float32)
        _lenS = 100 - jax.random.randint(jax.random.fold_in(_rk, 7), (16,), 0, max(1, 100 // 4) + 1, jnp.int32)
        _lenS2 = 361 - jax.random.randint(jax.random.fold_in(_rk, 8), (16,), 0, max(1, 361 // 4) + 1, jnp.int32)
        _ctx_1024P = jax.random.normal(jax.random.fold_in(_rk, 11), (16, 16, 256), jnp.float32)
        _ctx_1024c = jax.random.dirichlet(jax.random.fold_in(_rk, 511), 0.3 * jnp.ones((16,), jnp.float32), (16, 361))
        _ctx_1024t = jnp.einsum('bsk,bkd->bsd', _ctx_1024c, _ctx_1024P)
        _ctx_1024t = _ctx_1024t * jax.lax.rsqrt(jnp.mean(jnp.square(_ctx_1024t)) + 1e-12) * 0.953939
        ctx_1024 = 7.22013e-05 + 1.00017 * (_ctx_1024t + 0.3 * jax.random.normal(jax.random.fold_in(_rk, 611), (16, 361, 256), jnp.float32))
        _validS = jnp.arange(100)[None, :] < _lenS[:, None]
        _validS2 = jnp.arange(361)[None, :] < _lenS2[:, None]
        _causal = jnp.tril(jnp.ones((100, 100), dtype=bool))
        mask_1x1xSxS2_fk1 = jnp.where(jnp.broadcast_to(_validS2[0:1, None, None, :], (1, 1, 100, 361)), 1.0, 0.0).astype(jnp.float32)
        return (x, ctx_1024, mask_1x1xSxS2_fk1)
    x, ctx_1024, mask_1x1xSxS2_fk1 = _rec_inputs()

    def _L0_attn_setup():
        import jax, jax.numpy as jnp
        import numpy as np
        D_MODEL = 256
        D_INNER = 512
        D_STATE = 16
        D_CONV = 4
        DT_RANK = 64
        RANK = 16
        LORA_SCALING = 2.0
        BATCH = 2
        SEQLEN = 512

        def _lora_linear(x, w, a, b, mask, scaling):
            base = x @ w.T
            lora = x @ a.T @ b.T * mask * scaling
            return base + lora

        def _selective_scan(u, delta, A, Bm, Cm, Dp):

            def step(h, inp):
                d_t, b_t, c_t, u_t = inp
                dA = jnp.exp(d_t[..., None] * A)
                h = dA * h + (d_t * u_t)[..., None] * b_t[:, None, :]
                y = jnp.sum(h * c_t[:, None, :], axis=-1)
                return (h, y)
            Bsz, L, Dd = u.shape
            h0 = jnp.zeros((Bsz, Dd, A.shape[1]), u.dtype)
            xs = (jnp.moveaxis(delta, 1, 0), jnp.moveaxis(Bm, 1, 0), jnp.moveaxis(Cm, 1, 0), jnp.moveaxis(u, 1, 0))
            _, ys = jax.lax.scan(step, h0, xs)
            return jnp.moveaxis(ys, 0, 1) + u * Dp
        key = jax.random.key(seed)
        ks = jax.random.split(key, 14)
        s = lambda i, shape, sc=1.0: jax.random.normal(ks[i], shape, dtype=jnp.float32) * sc
        return {'x': s(0, (BATCH, SEQLEN, D_MODEL)), 'w_in': s(1, (2 * D_INNER, D_MODEL), 0.02), 'lora_A_in': s(2, (RANK, D_MODEL), 0.01), 'lora_B_in': s(3, (2 * D_INNER, RANK), 0.01), 'mask_in': jnp.ones((2 * D_INNER,), jnp.float32), 'conv_w': s(4, (D_INNER, 1, D_CONV), 0.1), 'conv_b': s(5, (D_INNER,), 0.1), 'w_xproj': s(6, (DT_RANK + 2 * D_STATE, D_INNER), 0.02), 'w_dt': s(7, (D_INNER, DT_RANK), 0.02), 'b_dt': s(8, (D_INNER,), 0.1), 'A_log': jnp.log(jnp.tile(jnp.arange(1, D_STATE + 1, dtype=jnp.float32), (D_INNER, 1))), 'Dp': s(9, (D_INNER,), 0.1) + 1.0, 'w_out': s(10, (D_MODEL, D_INNER), 0.02), 'lora_A_out': s(11, (RANK, D_INNER), 0.01), 'lora_B_out': s(12, (D_MODEL, RANK), 0.01), 'mask_out': jnp.ones((D_MODEL,), jnp.float32)}
    _L0_attn_all = _L0_attn_setup()
    _L0_attn_in = {k: v for k, v in _L0_attn_all.items() if k in ('w_in', 'lora_A_in', 'lora_B_in', 'mask_in', 'conv_w', 'conv_b', 'w_xproj', 'w_dt', 'b_dt', 'A_log', 'Dp', 'w_out', 'lora_A_out', 'lora_B_out', 'mask_out')}
    del _L0_attn_all

    def _L0_xattn_setup():
        import jax, jax.numpy as jnp
        import numpy as np
        B, S, D, H = (4, 512, 256, 16)
        DEPTH = D // H

        def _split_heads(x):
            b, s, _ = x.shape
            return x.reshape(b, s, H, DEPTH).transpose(0, 2, 1, 3)
        key = jax.random.key(seed)
        ks = jax.random.split(key, 11)
        scale = 1.0 / np.sqrt(D)
        inp = {'v': jax.random.normal(ks[0], (B, S, D), jnp.float32), 'k': jax.random.normal(ks[1], (B, S, D), jnp.float32), 'q': jax.random.normal(ks[2], (B, S, D), jnp.float32), 'mask': jnp.triu(jnp.ones((S, S), jnp.float32), k=1)[None, None, :, :], 'wq': jax.random.normal(ks[3], (D, D), jnp.float32) * scale, 'bq': jnp.zeros((D,), jnp.float32), 'wk': jax.random.normal(ks[4], (D, D), jnp.float32) * scale, 'bk': jnp.zeros((D,), jnp.float32), 'wv': jax.random.normal(ks[5], (D, D), jnp.float32) * scale, 'bv': jnp.zeros((D,), jnp.float32), 'wo': jax.random.normal(ks[6], (D, D), jnp.float32) * scale, 'bo': jnp.zeros((D,), jnp.float32)}
        return inp
    _L0_xattn_all = _L0_xattn_setup()
    _L0_xattn_in = {k: v for k, v in _L0_xattn_all.items() if k in ('wq', 'bq', 'wk', 'bk', 'wv', 'bv', 'wo', 'bo')}
    del _L0_xattn_all

    def _L0_ffn_setup():
        import jax, jax.numpy as jnp
        import numpy as np
        B, S, D, F, E, K = (2, 512, 256, 1024, 8, 2)
        key = jax.random.key(seed)
        ks = jax.random.split(key, 5)
        x = jax.random.normal(ks[0], (B, S, D), dtype=jnp.float32)
        Wg = jax.random.normal(ks[1], (D, E), dtype=jnp.float32) * 0.02
        W1 = jax.random.normal(ks[2], (E, D, F), dtype=jnp.float32) * 0.02
        b1 = jnp.zeros((E, F), dtype=jnp.float32)
        W2 = jax.random.normal(ks[3], (E, F, D), dtype=jnp.float32) * 0.02
        b2 = jnp.zeros((E, D), dtype=jnp.float32)
        return {'x': x, 'Wg': Wg, 'W1': W1, 'b1': b1, 'W2': W2, 'b2': b2}
    _L0_ffn_all = _L0_ffn_setup()
    _L0_ffn_in = {k: v for k, v in _L0_ffn_all.items() if k in ('Wg', 'W1', 'b1', 'W2', 'b2')}
    del _L0_ffn_all
    return {'x': x, 'ctx_1024': ctx_1024, 'mask_1x1xSxS2_fk1': mask_1x1xSxS2_fk1, 'L0_attn_w_in': _L0_attn_in['w_in'], 'L0_attn_lora_A_in': _L0_attn_in['lora_A_in'], 'L0_attn_lora_B_in': _L0_attn_in['lora_B_in'], 'L0_attn_mask_in': _L0_attn_in['mask_in'], 'L0_attn_conv_w': _L0_attn_in['conv_w'], 'L0_attn_conv_b': _L0_attn_in['conv_b'], 'L0_attn_w_xproj': _L0_attn_in['w_xproj'], 'L0_attn_w_dt': _L0_attn_in['w_dt'], 'L0_attn_b_dt': _L0_attn_in['b_dt'], 'L0_attn_A_log': _L0_attn_in['A_log'], 'L0_attn_Dp': _L0_attn_in['Dp'], 'L0_attn_w_out': _L0_attn_in['w_out'], 'L0_attn_lora_A_out': _L0_attn_in['lora_A_out'], 'L0_attn_lora_B_out': _L0_attn_in['lora_B_out'], 'L0_attn_mask_out': _L0_attn_in['mask_out'], 'L0_xattn_wq': _L0_xattn_in['wq'], 'L0_xattn_bq': _L0_xattn_in['bq'], 'L0_xattn_wk': _L0_xattn_in['wk'], 'L0_xattn_bk': _L0_xattn_in['bk'], 'L0_xattn_wv': _L0_xattn_in['wv'], 'L0_xattn_bv': _L0_xattn_in['bv'], 'L0_xattn_wo': _L0_xattn_in['wo'], 'L0_xattn_bo': _L0_xattn_in['bo'], 'L0_ffn_Wg': _L0_ffn_in['Wg'], 'L0_ffn_W1': _L0_ffn_in['W1'], 'L0_ffn_b1': _L0_ffn_in['b1'], 'L0_ffn_W2': _L0_ffn_in['W2'], 'L0_ffn_b2': _L0_ffn_in['b2']}

def reference(x, ctx_1024, mask_1x1xSxS2_fk1, L0_attn_w_in, L0_attn_lora_A_in, L0_attn_lora_B_in, L0_attn_mask_in, L0_attn_conv_w, L0_attn_conv_b, L0_attn_w_xproj, L0_attn_w_dt, L0_attn_b_dt, L0_attn_A_log, L0_attn_Dp, L0_attn_w_out, L0_attn_lora_A_out, L0_attn_lora_B_out, L0_attn_mask_out, L0_xattn_wq, L0_xattn_bq, L0_xattn_wk, L0_xattn_bk, L0_xattn_wv, L0_xattn_bv, L0_xattn_wo, L0_xattn_bo, L0_ffn_Wg, L0_ffn_W1, L0_ffn_b1, L0_ffn_W2, L0_ffn_b2):
    import jax
    import jax.numpy as jnp

    def _L0_attn_ref(x, w_in, lora_A_in, lora_B_in, mask_in, conv_w, conv_b, w_xproj, w_dt, b_dt, A_log, Dp, w_out, lora_A_out, lora_B_out, mask_out):
        import jax, jax.numpy as jnp
        import numpy as np
        D_MODEL = 256
        D_INNER = 512
        D_STATE = 16
        D_CONV = 4
        DT_RANK = 64
        RANK = 16
        LORA_SCALING = 2.0
        BATCH = 2
        SEQLEN = 512

        def _lora_linear(x, w, a, b, mask, scaling):
            base = x @ w.T
            lora = x @ a.T @ b.T * mask * scaling
            return base + lora

        def _selective_scan(u, delta, A, Bm, Cm, Dp):

            def step(h, inp):
                d_t, b_t, c_t, u_t = inp
                dA = jnp.exp(d_t[..., None] * A)
                h = dA * h + (d_t * u_t)[..., None] * b_t[:, None, :]
                y = jnp.sum(h * c_t[:, None, :], axis=-1)
                return (h, y)
            Bsz, L, Dd = u.shape
            h0 = jnp.zeros((Bsz, Dd, A.shape[1]), u.dtype)
            xs = (jnp.moveaxis(delta, 1, 0), jnp.moveaxis(Bm, 1, 0), jnp.moveaxis(Cm, 1, 0), jnp.moveaxis(u, 1, 0))
            _, ys = jax.lax.scan(step, h0, xs)
            return jnp.moveaxis(ys, 0, 1) + u * Dp
        B, L, _ = x.shape
        xz = _lora_linear(x, w_in, lora_A_in, lora_B_in, mask_in, LORA_SCALING)
        xs, z = jnp.split(xz, 2, axis=-1)
        xc = jnp.moveaxis(xs, 1, 2)
        xc = jax.lax.conv_general_dilated(xc, conv_w, window_strides=(1,), padding=[(D_CONV - 1, 0)], feature_group_count=D_INNER, dimension_numbers=('NCH', 'OIH', 'NCH')) + conv_b[None, :, None]
        xs = jax.nn.silu(jnp.moveaxis(xc, 1, 2))
        x_dbl = xs @ w_xproj.T
        dt, Bm, Cm = jnp.split(x_dbl, [DT_RANK, DT_RANK + D_STATE], axis=-1)
        delta = jax.nn.softplus(dt @ w_dt.T + b_dt)
        A = -jnp.exp(A_log)
        y = _selective_scan(xs, delta, A, Bm, Cm, Dp)
        y = y * jax.nn.silu(z)
        return _lora_linear(y, w_out, lora_A_out, lora_B_out, mask_out, LORA_SCALING)

    def _L0_xattn_ref(v, k, q, mask, wq, bq, wk, bk, wv, bv, wo, bo):
        import jax, jax.numpy as jnp
        import numpy as np
        B, S, D, H = (4, 512, 256, 16)
        DEPTH = D // H

        def _split_heads(x):
            b, s, _ = x.shape
            return x.reshape(b, s, H, DEPTH).transpose(0, 2, 1, 3)
        qh = _split_heads(q @ wq + bq)
        kh = _split_heads(k @ wk + bk)
        vh = _split_heads(v @ wv + bv)
        logits = jnp.einsum('bhqd,bhkd->bhqk', qh, kh) / jnp.sqrt(jnp.asarray(DEPTH, jnp.float32))
        logits = logits + mask * -1000000000.0
        attn = jax.nn.softmax(logits, axis=-1)
        out = jnp.einsum('bhqk,bhkd->bhqd', attn, vh)
        out = out.transpose(0, 2, 1, 3).reshape(q.shape[0], -1, D)
        return out @ wo + bo

    def _L0_ffn_ref(x, Wg, W1, b1, W2, b2):
        import jax, jax.numpy as jnp
        import numpy as np
        B, S, D, F, E, K = (2, 512, 256, 1024, 8, 2)
        b, s, d = x.shape
        e = Wg.shape[1]
        T = b * s
        C = 2 * K * T // e
        xt = x.reshape(T, d)
        logits = xt.astype(jnp.float32) @ Wg.astype(jnp.float32)
        gates = jax.nn.softmax(logits, axis=-1)
        idx1 = jnp.argmax(gates, axis=-1)
        mask1 = jax.nn.one_hot(idx1, e, dtype=gates.dtype)
        gate1 = jnp.sum(gates * mask1, axis=-1)
        logits2 = jnp.where(mask1 > 0, -jnp.inf, logits)
        idx2 = jnp.argmax(logits2, axis=-1)
        mask2 = jax.nn.one_hot(idx2, e, dtype=gates.dtype)
        gate2 = jnp.sum(gates * mask2, axis=-1)
        denom = gate1 + gate2 + 1e-09
        w1 = gate1 / denom
        w2 = gate2 / denom
        p1 = jnp.cumsum(mask1, axis=0) - mask1
        pos1 = jnp.sum(p1 * mask1, axis=-1).astype(jnp.int32)
        off = jnp.sum(mask1, axis=0)
        p2 = jnp.cumsum(mask2, axis=0) - mask2 + off[None, :]
        pos2 = jnp.sum(p2 * mask2, axis=-1).astype(jnp.int32)
        keep1 = (pos1 < C).astype(xt.dtype)
        keep2 = (pos2 < C).astype(xt.dtype)
        pos1 = jnp.clip(pos1, 0, C - 1)
        pos2 = jnp.clip(pos2, 0, C - 1)
        xe = jnp.zeros((e, C, d), dtype=xt.dtype)
        xe = xe.at[idx1, pos1].add(xt * keep1[:, None])
        xe = xe.at[idx2, pos2].add(xt * keep2[:, None])
        h = jax.nn.gelu(jnp.einsum('ecd,edf->ecf', xe, W1) + b1[:, None, :], approximate=False)
        ye = jnp.einsum('ecf,efd->ecd', h, W2) + b2[:, None, :]
        out = ye[idx1, pos1] * (w1 * keep1)[:, None] + ye[idx2, pos2] * (w2 * keep2)[:, None]
        return out.reshape(b, s, d)
    x = _layernorm(x + _L0_attn_ref(x, L0_attn_w_in, L0_attn_lora_A_in, L0_attn_lora_B_in, L0_attn_mask_in, L0_attn_conv_w, L0_attn_conv_b, L0_attn_w_xproj, L0_attn_w_dt, L0_attn_b_dt, L0_attn_A_log, L0_attn_Dp, L0_attn_w_out, L0_attn_lora_A_out, L0_attn_lora_B_out, L0_attn_mask_out), axis=-1)
    x = _layernorm(x + _L0_xattn_ref(ctx_1024, ctx_1024, x, mask_1x1xSxS2_fk1, L0_xattn_wq, L0_xattn_bq, L0_xattn_wk, L0_xattn_bk, L0_xattn_wv, L0_xattn_bv, L0_xattn_wo, L0_xattn_bo), axis=-1)
    x = _layernorm(x + _L0_ffn_ref(x, L0_ffn_Wg, L0_ffn_W1, L0_ffn_b1, L0_ffn_W2, L0_ffn_b2), axis=-1)
    return x

_drawn_inputs = setup_inputs


def setup_inputs(seed=0):
    import zlib

    import numpy as np

    out = dict(_drawn_inputs(seed))
    spreads = {'L0_attn_mask_in': (1.0, 0.6),
     'L0_attn_mask_out': (1.0, 0.6),
     'L0_xattn_bq': (0.0, 0.286),
     'L0_xattn_bk': (0.0, 0.8),
     'L0_xattn_bv': (0.0, 0.1),
     'L0_xattn_bo': (0.0, 0.1),
     'L0_ffn_b1': (0.0, 0.305),
     'L0_ffn_b2': (0.0, 0.1)}
    factors = {'L0_attn_w_in': 7.188,
     'L0_attn_lora_A_in': 8.0,
     'L0_attn_lora_B_in': 8.0,
     'L0_attn_conv_w': 8.0,
     'L0_attn_conv_b': 7.331,
     'L0_attn_w_xproj': 8.0,
     'L0_attn_w_dt': 8.0,
     'L0_attn_b_dt': 8.0,
     'L0_attn_A_log': 8.0,
     'L0_attn_Dp': 8.0,
     'L0_attn_w_out': 6.625,
     'L0_attn_lora_A_out': 8.0,
     'L0_attn_lora_B_out': 8.0}
    for name, (base, spread) in spreads.items():
        noise = np.random.default_rng([zlib.crc32(name.encode()), seed]).standard_normal(out[name].shape)
        drawn = base * np.exp(spread * noise) if base else spread * noise
        out[name] = jnp.asarray(drawn.astype(out[name].dtype))
    for name, factor in factors.items():
        out[name] = (out[name] * factor).astype(out[name].dtype)
    return out
```

```python
from contextlib import ExitStack

import concourse.bass as bass
from concourse import mybir

F32 = mybir.dt.float32
F32R = mybir.dt.float32r
I32 = mybir.dt.int32
U32 = mybir.dt.uint32
ALU = mybir.AluOpType
ACT = mybir.ActivationFunctionType
AX_X = mybir.AxisListType.X

P = 128
SEQS, STEPS, D = 16, 100, 256
TOKENS = SEQS * STEPS
DC = D // P
INNER, STATES, TAPS, RANK, LORA = 512, 16, 4, 64, 16
G = INNER // P
QS = 4
QUADS = SEQS // QS
QT = QS * STEPS
PAD = STEPS + TAPS - 1
LORA_SCALING = 2.0
EPS = 1e-5
UNITS = QUADS * STATES
HB_RING, DA_RING = 4, 3
SERIES = [(-1.0) ** (k + 1) / k for k in range(5, 0, -1)]
SERIES_BELOW = 2.0 ** -5


class Program:

    def __init__(self, nc, dram):
        self.nc, self.dram = nc, dram

    def sb(self, ctx, name, shape, dt=F32):
        return ctx.enter_context(self.nc.sbuf_tensor(name, shape, dt))

    def psum(self, ctx, name, shape, dt=F32):
        return ctx.enter_context(self.nc.psum_tensor(name, shape, dt))

    def sem(self, ctx, name):
        return ctx.enter_context(self.nc.semaphore(name))


def misc_schedule():
    slots = {}

    def put(q, n, *task):
        slots.setdefault((q, n), []).append(task)

    for j in range(G):
        put(-1, 0, "xz", 0, j)
    put(-1, 0, "bcdt", 0)
    for g in range(G):
        put(-1, 0, "delta", 0, g)
        put(0, g, "xz", 0, G + g)
    for q in range(QUADS + 1):
        if q:
            for s in range(QS):
                put(q, 3 + s // 2, "proj", q - 1, s)
            for c in range(DC):
                put(q, 7, "x1T", q - 1, c)
            for o in range(DC):
                put(q, 8, "q", q - 1, o)
        if q + 1 < QUADS:
            for j, n in enumerate((1, 1, 2, 2, 9, 9, 10, 11)):
                put(q, n, "xz", q + 1, j)
            put(q, 5, "bcdt", q + 1)
            for g in range(G):
                put(q, 6 + g // 2, "delta", q + 1, g)
    order = sorted(slots)
    number, m = {}, 0
    for key in order:
        for task in slots[key]:
            number[task] = m
            m += 1
    return slots, number


def stage_a(pr, x1, qT, ident, xe, xe_cleared):
    nc, dram = pr.nc, pr.dram
    slots, number = misc_schedule()
    with ExitStack() as ctx:
        def sb(*a):
            return pr.sb(ctx, *a)

        def sem(name):
            return pr.sem(ctx, name)

        w_in = sb("w_in", [P, DC, 2 * INNER])
        w_x = sb("w_x", [P, G, RANK + 4 * STATES])
        w_dt = sb("w_dt", [P, INNER])
        w_out = sb("w_out", [P, G, D])
        wq = sb("wq", [P, DC, D])
        bq = sb("bq", [P, DC])
        conv_w = sb("conv_w", [P, G, TAPS])
        conv_b = sb("conv_b", [P, G])
        b_dt = sb("b_dt", [P, G])
        skip = sb("skip", [P, G])
        decay = sb("decay", [P, G, STATES])
        eps = sb("eps", [P, 1])
        sel = sb("sel", [P, 2 * STATES], F32R)

        zeros = sb("zeros", [P, D])
        xT = sb("xT", [P, 2, DC, QT])
        xrow = sb("xrow", [STEPS, QS, D])
        xpad = sb("xpad", [P, G, QS, PAD])
        u = sb("u", [P, 2, G, QT])
        zs = sb("zs", [P, 2, G, QT])
        delta = sb("delta", [P, 2, G, QT])
        du = sb("du", [P, 2, G, QT])
        tmp = sb("tmp", [P, G, QT])
        logs = sb("logs", [P, G, QT])
        small = sb("small", [P, G, QT], mybir.dt.uint8)
        dtT = sb("dtT", [P, QT])
        bcs = sb("bcs", [P, 2, QT], F32R)
        Bs = sb("Bs", [P, 3, QT])
        Cs = sb("Cs", [P, 3, QT])
        dA = sb("dA", [P, DA_RING, G, QS, STEPS])
        hb = sb("hb", [P, HB_RING, G, QT])
        yz, x1T = tmp, logs[:, 0:DC]
        stat = sb("stat", [STEPS, QS, 6])
        mv = sb("mv", [STEPS, QS, 2])
        lnv = sb("lnv", [STEPS, QS])
        rstd = sb("rstd", [STEPS, QS])

        y_ps = [pr.psum(ctx, f"y_ps{g}", [P, 512]) for g in range(G)]
        b_ps = pr.psum(ctx, "b_ps", [P, 512])
        c_ps = pr.psum(ctx, "c_ps", [P, 512])
        misc = [pr.psum(ctx, f"misc{i}", [P, 512]) for i in range(2)]

        w_in_loaded, w_loaded, lora_loaded = sem("w_in_loaded"), sem("w_loaded"), sem("lora_loaded")
        xT_loaded = [sem(f"xT_loaded{i}") for i in range(2)]
        xrow_loaded = sem("xrow_loaded")
        consts = sem("consts")
        zeroed = sem("zeroed")
        lora_scaled, lora_product, w_folded = sem("lora_scaled"), sem("lora_product"), sem("w_folded")
        decay_exp, decay_ready = sem("decay_exp"), sem("decay_ready")
        misc_full = sem("misc_full")
        misc_free = [sem(f"misc_free{i}") for i in range(2)]
        xs_copied, z_copied, conv_step, conv_done = sem("xs_copied"), sem("z_copied"), sem("conv_step"), sem("conv_done")
        u_ready, zs_ready, dt_ready = sem("u_ready"), sem("zs_ready"), sem("dt_ready")
        bc_high, bc_ready = sem("bc_high"), sem("bc_ready")
        v_ready, sp_step, log_ready, delta_ready, du_ready = (
            sem("v_ready"), sem("sp_step"), sem("log_ready"), sem("delta_ready"), sem("du_ready"))
        series_step, log_patched = sem("series_step"), sem("log_patched")
        b_full, b_copied, c_full, c_copied = sem("b_full"), sem("b_copied"), sem("c_full"), sem("c_copied")
        dA_ready, dbu_ready, scan_done, hc_done, added = (
            sem("dA_ready"), sem("dbu_ready"), sem("scan_done"), sem("hc_done"), sem("added"))
        y_taken, yz_ready = sem("y_taken"), sem("yz_ready")
        stat_ready, mv_ready, ln_ready, rstd_ready, x1_ready = (
            sem("stat_ready"), sem("mv_ready"), sem("ln_ready"), sem("rstd_ready"), sem("x1_ready"))
        x1T_ready = sem("x1T_ready")
        q_ready = sem("q_ready")

        lora_a = hb[0:LORA, 0, 0:2, :].rearrange("p g t -> p (g t)")[:, 0:D + INNER]
        lora_b = hb[0:LORA, 1, :, :].rearrange("p g t -> p (g t)")[:, 0:2 * INNER + D]
        lora_m = hb[0:LORA, 2, :, :].rearrange("p g t -> p (g t)")[:, 0:2 * INNER + D]
        A_IN, A_OUT = lora_a[:, 0:D], lora_a[:, D:]
        B_IN, B_OUT = lora_b[:, 0:2 * INNER], lora_b[:, 2 * INNER:]
        folds = [(w_in[:, c, f * 512:(f + 1) * 512], A_IN[:, c * P:(c + 1) * P], B_IN[:, f * 512:(f + 1) * 512])
                 for c in range(DC) for f in range(2)]
        folds += [(w_out[:, g, :], A_OUT[:, g * P:(g + 1) * P], B_OUT) for g in range(G)]
        NUM_W = 11

        def misc_bank(task):
            return misc[number[task] % 2]

        def wait_full(eng, task):
            eng.wait_ge(misc_full, len(folds) + number[task] + 1)

        def free_bank(ins, task):
            return ins.then_inc(misc_free[number[task] % 2], 1)

        block = ctx.enter_context(nc.Block())

        @block.sync
        def _(sp):
            sp.dma_start(lora_a[:, 0:D], dram["L0_attn_lora_A_in"]).then_inc(lora_loaded, 16)
            sp.dma_start(A_OUT, dram["L0_attn_lora_A_out"]).then_inc(lora_loaded, 16)
            sp.dma_start(B_IN, dram["lora_B_inT"]).then_inc(lora_loaded, 16)
            sp.dma_start(B_OUT, dram["lora_B_outT"]).then_inc(lora_loaded, 16)
            sp.dma_start(lora_m[:, 0:2 * INNER], dram["L0_attn_mask_in"].rearrange("(a n) -> a n", a=1)
                         .partition_broadcast(LORA)).then_inc(lora_loaded, 16)
            sp.dma_start(lora_m[:, 2 * INNER:], dram["L0_attn_mask_out"].rearrange("(a n) -> a n", a=1)
                         .partition_broadcast(LORA)).then_inc(lora_loaded, 16)
            sp.dma_start(w_in[:], dram["w_inT"].rearrange("(c p) n -> p c n", p=P)).then_inc(w_in_loaded, 16)

            def load_xT(q):
                if q >= 2:
                    sp.wait_ge(misc_full, len(folds) + number[("xz", q - 2, 2 * G - 1)] + 1)
                sp.dma_start(xT[:, q % 2], dram["xT"][:, q * QT:(q + 1) * QT].rearrange("(c p) t -> p c t", p=P)
                             ).then_inc(xT_loaded[q % 2], 16)

            def load_xrow(q):
                if q >= 1:
                    sp.wait_ge(x1_ready, QS * q)
                sp.dma_start(xrow[:], dram["x"][q * QS:(q + 1) * QS].rearrange("s t d -> t s d")
                             ).then_inc(xrow_loaded, 16)

            load_xT(0)
            sp.dma_start(conv_w[:], dram["conv_w"]).then_inc(w_loaded, 16)
            sp.dma_start(conv_b[:], dram["conv_b"]).then_inc(w_loaded, 16)
            sp.dma_start(b_dt[:], dram["b_dt"]).then_inc(w_loaded, 16)
            sp.dma_start(skip[:], dram["Dp"]).then_inc(w_loaded, 16)
            sp.dma_start(decay[:], dram["A_log"]).then_inc(w_loaded, 16)
            wx = dram["w_xprojT"].rearrange("(g p) n -> p g n", p=P)
            sp.dma_start(w_x[:, :, 0:RANK + 2 * STATES], wx).then_inc(w_loaded, 16)
            sp.dma_start(w_x[:, :, RANK + 2 * STATES:], wx[:, :, RANK:]).then_inc(w_loaded, 16)
            sp.dma_start(w_dt[0:RANK, :], dram["w_dtT"]).then_inc(w_loaded, 16)
            sp.dma_start(w_out[:], dram["w_outT"].rearrange("(g p) n -> p g n", p=P)).then_inc(w_loaded, 16)
            sp.dma_start(wq[:], dram["L0_xattn_wq"].rearrange("(c p) n -> p c n", p=P)).then_inc(w_loaded, 16)
            sp.dma_start(bq[:], dram["bq"]).then_inc(w_loaded, 16)
            load_xT(1)
            load_xrow(0)
            sp.wait_ge(consts, 1)
            sp.dma_start(xe[0:SLOTS + P].rearrange("(n p) d -> p n d", p=P),
                         zeros[:].unsqueeze(1).to_broadcast([P, TILES + 1, D])).then_inc(xe_cleared, 16)
            for q in range(1, QUADS):
                if q + 1 < QUADS:
                    load_xT(q + 1)
                load_xrow(q)

        @block.gpsimd
        def _(pool):
            pool.memset(ident[:], 0.0).then_inc(zeroed, 1)
            pool.memset(zeros[:], 0.0).then_inc(consts, 1)
            pool.memset(dtT[:], 0.0).then_inc(consts, 1)
            pool.wait_ge(consts, 2)
            pool.memset(w_dt[RANK:, :], 0.0).then_inc(consts, 1)
            pool.wait_ge(consts, 3)
            pool.memset(xpad[:, :, :, 0:TAPS - 1], 0.0).then_inc(consts, 1)
            pool.memset(dA[:, :, :, :, 0:1], 0.0).then_inc(consts, 1)
            pool.memset(eps[:], EPS).then_inc(consts, 1)
            pool.wait_ge(zeroed, 1)
            pool.affine_select(out=ident[:], in_=ident[:], compare_op=ALU.not_equal, fill=1.0, base=0,
                               pattern=[[-1, P]], channel_multiplier=1).then_inc(zeroed, 1)
            for q in range(QUADS):
                for n in range(STATES):
                    U = q * STATES + n
                    if n == 0:
                        pool.wait_ge(delta_ready, q + 1)
                        pool.tensor_tensor(du[:, q % 2], delta[:, q % 2], u[:, q % 2], ALU.mult).then_inc(du_ready, 1)
                        pool.wait_ge(du_ready, q + 1)
                    pool.wait_ge(b_copied, U + 1)
                    if U >= HB_RING:
                        pool.wait_ge(added, U - HB_RING + 1)
                    pool.tensor_tensor(hb[:, U % HB_RING], du[:, q % 2],
                                       Bs[:, U % 3].unsqueeze(1).to_broadcast([P, G, QT]),
                                       ALU.mult).then_inc(dbu_ready, 1)

        @block.scalar
        def _(act):
            act.wait_ge(w_loaded, 16 * NUM_W)
            act.activation(decay[:], decay[:], ACT.Exp).then_inc(decay_exp, 1)

            def copy_xz(q, j):
                task = ("xz", q, j)
                wait_full(act, task)
                if j < G:
                    if q >= 1:
                        act.wait_ge(conv_done, G * (q - 1) + j + 1)
                    act.copy(xpad[:, j, :, TAPS - 1:],
                             misc_bank(task)[:, 0:QT].rearrange("p (s t) -> p s t", s=QS)).then_inc(xs_copied, 1)
                    if q >= 2:
                        act.wait_ge(y_taken, G * (q - 1))
                    free_bank(act.activation(u[:, q % 2, j], misc_bank(task)[:, 0:QT], ACT.Identity,
                                             scale=conv_w[:, j, TAPS - 1:TAPS], bias=conv_b[:, j:j + 1]), task)
                else:
                    if q >= 2 and j == G:
                        act.wait_ge(yz_ready, q - 1)
                    free_bank(act.copy(zs[:, q % 2, j - G], misc_bank(task)[:, 0:QT]), task)

            def silu_u(q):
                act.wait_ge(conv_done, G * (q + 1))
                act.activation(u[:, q % 2], u[:, q % 2], ACT.Silu).then_inc(u_ready, 1)

            def silu_z(q):
                for j in (2 * G - 2, 2 * G - 1):
                    last = number[("xz", q, j)]
                    act.wait_ge(misc_free[last % 2], last // 2 + 1)
                act.activation(zs[:, q % 2], zs[:, q % 2], ACT.Silu).then_inc(zs_ready, 1)

            def exp_table():
                act.preload_act_table_set("natural_log_exp_and_others")

            def split_bc(q):
                task = ("bcdt", q)
                wait_full(act, task)
                act.copy(bcs[RANK:, q % 2], misc_bank(task)[RANK:, 0:QT]).then_inc(bc_high, 1)
                act.copy(dtT[0:RANK, :], misc_bank(task)[0:RANK, 0:QT]).then_inc(dt_ready, 1)

            def copy_v(q, g):
                task = ("delta", q, g)
                wait_full(act, task)
                free_bank(act.activation(delta[:, q % 2, g], misc_bank(task)[:, 0:QT], ACT.Identity,
                                         bias=b_dt[:, g:g + 1]), task)

            def softplus_exp(q):
                for g in range(2):
                    last = number[("delta", q, G - 1 - g)]
                    act.wait_ge(misc_free[last % 2], last // 2 + 1)
                if q >= 1:
                    act.wait_ge(delta_ready, q)
                act.activation(tmp[:], delta[:, q % 2], ACT.Abs).then_inc(sp_step, 1)
                act.wait_ge(sp_step, 2 * q + 1)
                act.activation(tmp[:], tmp[:], ACT.Exp, scale=-1.0).then_inc(sp_step, 1)

            def softplus_log(q):
                act.wait_ge(sp_step, 2 * q + 2)
                act.activation(logs[:], tmp[:], ACT.Ln, bias=1.0).then_inc(log_ready, 1)

            def inverse_deviation(q):
                act.wait_ge(mv_ready, QS * (q + 1))
                if q >= 1:
                    act.wait_ge(x1_ready, QS * q)
                act.activation(lnv[:], mv[:, :, 1], ACT.Ln, bias=eps[0:STEPS, :]).then_inc(ln_ready, 1)
                act.wait_ge(ln_ready, q + 1)
                act.activation(rstd[:], lnv[:], ACT.Exp, scale=-0.5).then_inc(rstd_ready, 1)

            def copy_q(q):
                for o in range(DC):
                    task = ("q", q, o)
                    wait_full(act, task)
                    ins = act.activation(qT[:, o, q * QT:(q + 1) * QT], misc_bank(task)[:, 0:QT], ACT.Identity,
                                         scale=0.25, bias=bq[:, o:o + 1])
                    free_bank(ins, task)

            def copy_b(U):
                act.wait_ge(b_full, U + 1)
                if U >= 3:
                    act.wait_ge(dbu_ready, U - 2)
                act.copy(Bs[:, U % 3], b_ps[:, 0:QT]).then_inc(b_copied, 1)

            def copy_c(U):
                act.wait_ge(c_full, U + 1)
                if U >= 3:
                    act.wait_ge(hc_done, U - 2)
                act.copy(Cs[:, U % 3], c_ps[:, 0:QT]).then_inc(c_copied, 1)

            def exps(U):
                q, n = divmod(U, STATES)
                if n == 0:
                    act.wait_ge(delta_ready, q + 1)
                if U >= DA_RING:
                    act.wait_ge(scan_done, U - DA_RING + 1)
                for g in range(G):
                    ins = act.activation(dA[:, U % DA_RING, g, :, 1:],
                                         delta[:, q % 2, g].rearrange("p (s t) -> p s t", s=QS)[:, :, 1:],
                                         ACT.Exp, scale=decay[:, g, n:n + 1])
                ins.then_inc(dA_ready, 1)

            act.wait_ge(consts, 6)
            for j in range(G):
                copy_xz(0, j)
            silu_u(0)
            exp_table()
            split_bc(0)
            for g in range(G):
                copy_v(0, g)
            softplus_exp(0)
            softplus_log(0)
            act.wait_ge(decay_ready, 1)
            for U in range(2):
                copy_b(U)
                copy_c(U)
                exps(U)
            copy_b(2)
            for q in range(QUADS + 1):
                for n in range(STATES):
                    if q == QUADS and n > 9:
                        break
                    U = q * STATES + n
                    if U + 2 < UNITS:
                        exps(U + 2)
                    if U + 3 < UNITS:
                        copy_b(U + 3)
                    if U + 2 < UNITS:
                        copy_c(U + 2)
                    if q >= 1:
                        if n == 5:
                            inverse_deviation(q - 1)
                        if n == 8:
                            copy_q(q - 1)
                    for task in slots.get((q, n), ()):
                        if task[0] == "xz":
                            copy_xz(*task[1:])
                        if task[0] == "delta":
                            copy_v(*task[1:])
                    if q == 0 and n == 4:
                        silu_z(0)
                    if q + 1 < QUADS:
                        if n == 4:
                            silu_u(q + 1)
                            exp_table()
                        if n == 5:
                            split_bc(q + 1)
                        if n == 8:
                            softplus_exp(q + 1)
                        if n == 9:
                            softplus_log(q + 1)
                        if n == 12:
                            silu_z(q + 1)
                            exp_table()

        @block.vector
        def _(dve):
            dve.wait_ge(lora_loaded, 16 * 6)
            dve.scalar_tensor_tensor(out=lora_b, in0=lora_b, scalar=LORA_SCALING, in1=lora_m,
                                     op0=ALU.mult, op1=ALU.mult).then_inc(lora_scaled, 1)
            dve.wait_ge(zeroed, 2)
            for part in range(2):
                r = RANK + 2 * STATES * part
                dve.tensor_copy(sel[r:r + 2 * STATES, :], ident[r:r + 2 * STATES, r:r + 2 * STATES]).then_inc(consts, 1)
            dve.wait_ge(w_in_loaded, 16)
            dve.wait_ge(w_loaded, 16 * NUM_W)
            for i, (w, _, _) in enumerate(folds):
                dve.wait_ge(misc_full, i + 1)
                dve.tensor_tensor(w, w, misc[i % 2][:, 0:w.shape[-1]], ALU.add).then_inc(w_folded, 1)
            dve.wait_ge(decay_exp, 1)
            dve.tensor_scalar(decay[:], decay[:], -1.0, None, ALU.mult).then_inc(decay_ready, 1)
            dve.tensor_scalar(bq[:], bq[:], 0.25, None, ALU.mult).then_inc(decay_ready, 1)

            def conv(q, g):
                last = number[("xz", q, g)]
                dve.wait_ge(misc_free[last % 2], last // 2 + 1)
                out = u[:, q % 2, g].rearrange("p (s t) -> p s t", s=QS)
                step = (TAPS - 2) * (G * q + g)
                for k in range(TAPS - 1):
                    if k:
                        dve.wait_ge(conv_step, step + k)
                    ins = dve.scalar_tensor_tensor(out=out, in0=xpad[:, g, :, k:k + STEPS],
                                                   scalar=conv_w[:, g, k:k + 1], in1=out,
                                                   op0=ALU.mult, op1=ALU.add)
                    ins.then_inc(conv_step if k < TAPS - 2 else conv_done, 1)

            def low_bc(q):
                task = ("bcdt", q)
                dve.wait_ge(bc_high, q + 1)
                dve.wait_ge(dt_ready, q + 1)
                rows = slice(RANK + 2 * STATES, P)
                ins = dve.tensor_tensor(bcs[rows, q % 2], misc_bank(task)[rows, 0:QT],
                                        bcs[rows, q % 2].bitcast(F32), ALU.subtract)
                free_bank(ins, task)

            def softplus(q, parts):
                series = du[:, q % 2]
                steps = len(SERIES) + 1
                for k in parts:
                    if k == 0:
                        dve.wait_ge(log_ready, q + 1)
                        dve.tensor_scalar(small[:], tmp[:], SERIES_BELOW, None, ALU.is_lt).then_inc(series_step, 1)
                        dve.tensor_scalar(series, tmp[:], SERIES[0], None, ALU.mult).then_inc(series_step, 1)
                    elif k < len(SERIES):
                        dve.wait_ge(series_step, steps * q + k + 1)
                        dve.scalar_tensor_tensor(out=series, in0=series, scalar=SERIES[k], in1=tmp[:],
                                                 op0=ALU.add, op1=ALU.mult).then_inc(series_step, 1)
                    elif k == len(SERIES):
                        dve.wait_ge(series_step, steps * (q + 1))
                        dve.copy_predicated(logs[:], small[:], series).then_inc(log_patched, 1)
                    else:
                        dve.wait_ge(log_patched, q + 1)
                        dve.scalar_tensor_tensor(out=delta[:, q % 2], in0=delta[:, q % 2], scalar=0.0, in1=logs[:],
                                                 op0=ALU.max, op1=ALU.add).then_inc(delta_ready, 1)

            def scan(U):
                dve.wait_ge(dA_ready, U + 1)
                dve.wait_ge(dbu_ready, U + 1)
                flat = hb[:, U % HB_RING].rearrange("p g t -> p (g t)")
                dve.tensor_tensor_scan(flat, dA[:, U % DA_RING].rearrange("p g s t -> p (g s t)"), flat, 0.0,
                                       ALU.mult, ALU.add).then_inc(scan_done, 1)

            def times_c(U):
                dve.wait_ge(scan_done, U + 1)
                dve.wait_ge(c_copied, U + 1)
                dve.tensor_tensor(hb[:, U % HB_RING], hb[:, U % HB_RING],
                                  Cs[:, U % 3].unsqueeze(1).to_broadcast([P, G, QT]), ALU.mult).then_inc(hc_done, 1)

            def take_y(q):
                dve.wait_ge(added, STATES * (q + 1))
                if q >= 1:
                    dve.wait_ge(misc_full, len(folds) + number[("proj", q - 1, QS - 1)] + 1)
                for g in range(G):
                    ins = dve.scalar_tensor_tensor(out=yz[:, g], in0=u[:, q % 2, g], scalar=skip[:, g:g + 1],
                                                   in1=y_ps[g][:, 0:QT], op0=ALU.mult, op1=ALU.add)
                    ins.then_inc(y_taken, 1)
                dve.wait_ge(y_taken, G * (q + 1))
                dve.wait_ge(zs_ready, q + 1)
                dve.tensor_tensor(yz[:], yz[:], zs[:, q % 2], ALU.mult).then_inc(yz_ready, 1)

            def residual(q, part):
                dve.wait_ge(xrow_loaded, 16 * (q + 1))
                for s in range(2 * part, 2 * part + 2):
                    task = ("proj", q, s)
                    wait_full(dve, task)
                    ins = dve.tensor_tensor(xrow[:, s], misc_bank(task)[0:STEPS, 0:D], xrow[:, s],
                                            ALU.add)
                    free_bank(ins, task)
                for s in range(2 * part, 2 * part + 2):
                    last = number[("proj", q, s)]
                    dve.wait_ge(misc_free[last % 2], last // 2 + 1)
                    dve.bn_stats(stat[:, s], xrow[:, s]).then_inc(stat_ready, 1)
                for s in range(2 * part, 2 * part + 2):
                    dve.wait_ge(stat_ready, QS * q + s + 1)
                    dve.bn_aggr(mv[:, s], stat[:, s]).then_inc(mv_ready, 1)

            def normalise(q):
                dve.wait_ge(rstd_ready, q + 1)
                for s in range(QS):
                    dve.tensor_scalar(x1[:, QS * q + s], xrow[:, s], mv[:, s, 0:1], rstd[:, s:s + 1],
                                      ALU.subtract, ALU.mult).then_inc(x1_ready, 1)

            def copy_x1T(q):
                for c in range(DC):
                    task = ("x1T", q, c)
                    wait_full(dve, task)
                    free_bank(dve.tensor_copy(x1T[:, c], misc_bank(task)[:, 0:QT]), task)

            convs = {1: (0,), 2: (1, 2), 3: (3,)}
            softplus_parts = {10: (0, 1), 11: (2, 3), 12: (4, 5), 13: (6,)}
            for g in range(G):
                conv(0, g)
            low_bc(0)
            softplus(0, range(len(SERIES) + 2))
            scan(0)
            for q in range(QUADS + 1):
                for n in range(STATES):
                    if q == QUADS and n > 9:
                        break
                    U = q * STATES + n
                    if U + 1 < UNITS:
                        scan(U + 1)
                    if U < UNITS:
                        times_c(U)
                    if q >= 1:
                        if n == 0:
                            take_y(q - 1)
                        if n in (3, 4):
                            residual(q - 1, n - 3)
                        if n == 6:
                            normalise(q - 1)
                        if n == 7:
                            copy_x1T(q - 1)
                    if q + 1 < QUADS:
                        for g in convs.get(n, ()):
                            conv(q + 1, g)
                        if n == 5:
                            low_bc(q + 1)
                        softplus(q + 1, softplus_parts.get(n, ()))

        @block.tensor
        def _(pe):
            pe.wait_ge(lora_scaled, 1)
            for i, (w, left, right) in enumerate(folds):
                if i >= 2:
                    pe.wait_ge(w_folded, i - 1)
                pe.matmul(misc[i % 2][:, 0:w.shape[-1]], left, right, start=True, stop=True).then_inc(misc_full, 1)
            pe.wait_ge(w_folded, len(folds))

            def run(task):
                name, q = task[0], task[1]
                m = number[task]
                if m >= 2:
                    pe.wait_ge(misc_free[m % 2], m // 2)
                bank = misc_bank(task)
                if name == "xz":
                    j = task[2]
                    if j == 0:
                        pe.wait_ge(xT_loaded[q % 2], 16 * (q // 2 + 1))
                    for c in range(DC):
                        ins = pe.matmul(bank[:, 0:QT], w_in[:, c, j * P:(j + 1) * P], xT[:, q % 2, c],
                                        start=(c == 0), stop=(c == DC - 1))
                elif name == "bcdt":
                    pe.wait_ge(u_ready, q + 1)
                    for g in range(G):
                        ins = pe.matmul(bank[:, 0:QT], w_x[:, g], u[:, q % 2, g],
                                        start=(g == 0), stop=(g == G - 1))
                elif name == "delta":
                    pe.wait_ge(dt_ready, q + 1)
                    g = task[2]
                    ins = pe.matmul(bank[:, 0:QT], w_dt[:, g * P:(g + 1) * P], dtT[:], start=True, stop=True)
                elif name == "proj":
                    pe.wait_ge(yz_ready, q + 1)
                    s = task[2]
                    for g in range(G):
                        ins = pe.matmul(bank[0:STEPS, 0:D], yz[:, g, s * STEPS:(s + 1) * STEPS], w_out[:, g],
                                        start=(g == 0), stop=(g == G - 1))
                elif name == "x1T":
                    c = task[2]
                    pe.wait_ge(x1_ready, QS * (q + 1))
                    for s in range(QS):
                        ins = pe.transpose(bank[:, s * STEPS:(s + 1) * STEPS], x1[:, QS * q + s, c * P:(c + 1) * P],
                                           ident[0:STEPS, 0:STEPS])
                elif name == "q":
                    for c in range(DC):
                        last = number[("x1T", q, c)]
                        pe.wait_ge(misc_free[last % 2], last // 2 + 1)
                    o = task[2]
                    for c in range(DC):
                        ins = pe.matmul(bank[:, 0:QT], wq[:, c, o * P:(o + 1) * P], x1T[:, c],
                                        start=(c == 0), stop=(c == DC - 1))
                ins.then_inc(misc_full, 1)

            def spread(U, bank, row, full):
                q = U // STATES
                if U % STATES == 0:
                    last = number[("bcdt", q)]
                    pe.wait_ge(misc_free[last % 2], last // 2 + 1)
                n = row + U % STATES
                pe.matmul(bank[:, 0:QT], sel[RANK:, n:n + 1].to_broadcast([P - RANK, P]), bcs[RANK:, q % 2],
                          start=True, stop=True).then_inc(full, 1)

            def spread_b(U):
                if U >= 1:
                    pe.wait_ge(b_copied, U)
                spread(U, b_ps, 0, b_full)

            def spread_c(U):
                if U >= 1:
                    pe.wait_ge(c_copied, U)
                spread(U, c_ps, STATES, c_full)

            pe.wait_ge(consts, 8)
            for task in slots[(-1, 0)]:
                run(task)
            for U in range(2):
                spread_b(U)
                spread_c(U)
            spread_b(2)
            for q in range(QUADS + 1):
                for n in range(STATES):
                    U = q * STATES + n
                    if U + 3 < UNITS:
                        spread_b(U + 3)
                    if U + 2 < UNITS:
                        spread_c(U + 2)
                    for task in slots.get((q, n), ()):
                        run(task)
                    if U < UNITS:
                        pe.wait_ge(hc_done, U + 1)
                        for g in range(G):
                            if n == 0 and q >= 1:
                                pe.wait_ge(y_taken, G * (q - 1) + g + 1)
                            ins = pe.matmul(y_ps[g][:, 0:QT], ident[:], hb[:, U % HB_RING, g],
                                            start=(n == 0), stop=(n == STATES - 1))
                        ins.then_inc(added, 1)


HEADS = 16
HD = D // HEADS
KEYS = 361
KCH = [(0, 128), (128, 128), (256, KEYS - 256)]
HG = 4
SPS = HEADS // HG
MASKED = -1e9


def wait(eng, semaphore, value):
    if not isinstance(value, int) or value > 0:
        eng.wait_ge(semaphore, value)


def stage_b(pr, x1, qT, ident, lg, w1, w1_loaded):
    nc, dram = pr.nc, pr.dram
    with ExitStack() as ctx:
        def sb(*a):
            return pr.sb(ctx, *a)

        def sem(name):
            return pr.sem(ctx, name)

        wk = sb("wk", [P, DC, D])
        wv = sb("wv", [P, DC, D])
        wo = sb("wo", [P, HG, D])
        bk = sb("bk", [P, DC])
        bv = sb("bv", [P, D])
        bo = sb("bo", [P, D])
        wg = sb("wg", [P, DC, 8])
        mask = sb("mask", [STEPS, KEYS])
        head_rows = sb("head_rows", [P, P // HD])
        eps = sb("eps_b", [P, 1])
        ctxT = sb("ctxT", [P, 2, DC, KEYS])
        kT = sb("kT", [P, 2, DC, KEYS])
        v = sb("v", [P, 2, len(KCH), D + HD])
        qm = sb("qm", [P, 2, HEADS, STEPS])
        prob = sb("prob", [STEPS, 2, HG, KEYS])
        pT = sb("pT", [P, 2, len(KCH), HG * STEPS])
        mx = sb("mx", [STEPS, 2, HG])
        nmx = sb("nmx", [STEPS, 2, HG])
        rsum = sb("rsum", [STEPS, 2, HEADS])
        inv = sb("inv", [STEPS, HEADS])
        inv_wide = sb("inv_wide", [STEPS, HEADS, 32])
        inv_sb = sb("inv_sb", [P, HG * STEPS])
        oT = sb("oT", [P, HG, STEPS])
        x1b = sb("x1b", [STEPS, D])
        res = sb("res", [STEPS, D])
        stat = sb("stat_b", [STEPS, 6])
        mv = sb("mv_b", [STEPS, 2])
        lnv = sb("lnv_b", [STEPS, 1])
        rstd = sb("rstd_b", [STEPS, 1])
        x2 = sb("x2_b", [STEPS, D])
        x2T = sb("x2T_b", [P, DC, STEPS])

        s_ps = [pr.psum(ctx, f"s_ps{i}", [P, 512]) for i in range(2)]
        t_ps = [pr.psum(ctx, f"t_ps{i}", [P, 512]) for i in range(3)]
        o_ps = pr.psum(ctx, "o_ps", [P, 512])
        misc = [pr.psum(ctx, f"misc_b{i}", [P, 512]) for i in range(2)]

        w_loaded, wo_zero, consts = sem("wb_loaded"), sem("wo_zero"), sem("consts_b")
        mask_ready = sem("mask_ready")
        ctx_loaded = [sem(f"ctx_loaded{i}") for i in range(2)]
        qm_ready = sem("qm_ready")
        misc_full = sem("misc_b_full")
        misc_free = [sem(f"misc_b_free{i}") for i in range(2)]
        s_full, s_taken, nmx_ready, p_ready = sem("s_full"), sem("s_taken"), sem("nmx_ready"), sem("p_ready")
        t_full, pt_vector, pt_scalar, pv_done = sem("t_full"), sem("pt_vector"), sem("pt_scalar"), sem("pv_done")
        inv_ready, wide_ready, o_ready = sem("inv_ready"), sem("wide_ready"), sem("o_ready")
        x1b_ready, stat_ready, mv_ready = sem("x1b_ready"), sem("stat_b_ready"), sem("mv_b_ready")
        ln_ready, rstd_ready, x2_ready, x2_kept = (
            sem("ln_b_ready"), sem("rstd_b_ready"), sem("x2_ready"), sem("x2_kept"))

        ORDER = ["K0", "K1", "R", "V0", "proj", "V1", "V2", "xT", "lg"]
        FIRST = ["K0", "K1", "V0", "V1", "V2"]
        LAST = ["R", "proj", "xT", "lg"]
        SHIFT = 2 * len(FIRST) - len(ORDER)

        class Seq:

            def __init__(self, it, s):
                self.it, self.s = it, s

            def count(self, per_seq, more=0):
                return self.it * (2 * per_seq) + (self.s * per_seq + more)

            def use(self, name):
                b = 2 * self.it + self.s if isinstance(self.it, int) else None
                if b is not None and (b <= 0 or b == SEQS):
                    m = (len(FIRST) * (b + 1) + FIRST.index(name) if b <= 0 else
                         SEQS * len(ORDER) + SHIFT + LAST.index(name))
                    return m, m % 2, m // 2
                n = self.s * len(ORDER) + SHIFT + ORDER.index(name)
                return self.it * (2 * len(ORDER)) + n, n % 2, self.it * len(ORDER) + n // 2

            def bank(self, name):
                return misc[self.use(name)[1]]

            def wait_full(self, eng, name):
                eng.wait_ge(misc_full, self.use(name)[0] + 1)

            def free(self, ins, name):
                return ins.then_inc(misc_free[self.use(name)[1]], 1)

            def wait_freed(self, eng, name):
                _, i, before = self.use(name)
                eng.wait_ge(misc_free[i], before + 1)

        def sequences(eng, lead, body, tail):
            lead(Seq(0, -1))
            for s in range(2):
                body(Seq(0, s), s)
            with eng.Fori(1, SEQS // 2) as it:
                for s in range(2):
                    body(Seq(it, s), s)
            tail(Seq(SEQS // 2, 0))

        def first(seq):
            return isinstance(seq.it, int) and 2 * seq.it + seq.s == 0

        def alone(eng):
            eng.sem_inc(met[eng.engine], 1)

        NUM_W = 12
        met = {e.engine: sem(f"waits_met_{i}") for i, e in enumerate((nc.vector, nc.gpsimd))}
        block = ctx.enter_context(nc.Block())

        @block.sync
        def _(sp):
            def load(q, s):
                sp.dma_start(ctxT[:, s], dram["ctxT"][q].rearrange("(c p) t -> p c t", p=P)).then_inc(ctx_loaded[s], 16)

            load(0, 0)
            sp.dma_start(wk[:], dram["L0_xattn_wk"].rearrange("(c p) n -> p c n", p=P)).then_inc(w_loaded, 16)
            sp.dma_start(wv[:], dram["L0_xattn_wv"].rearrange("(c p) n -> p c n", p=P)).then_inc(w_loaded, 16)
            sp.dma_start(bk[:], dram["bk"]).then_inc(w_loaded, 16)
            for row, name in ((bv, "L0_xattn_bv"), (bo, "L0_xattn_bo")):
                sp.dma_start(row[:], dram[name].rearrange("(a n) -> a n", a=1).partition_broadcast(P)
                             ).then_inc(w_loaded, 16)
            sp.dma_start(mask[:], dram["mask_1x1xSxS2_fk1"].rearrange("a b q k -> (a b q) k")).then_inc(w_loaded, 16)
            sp.dma_start(wg[:], dram["L0_ffn_Wg"].rearrange("(c p) n -> p c n", p=P)).then_inc(w_loaded, 16)
            sp.dma_start(head_rows[:], dram["head_rows"]).then_inc(w_loaded, 16)
            sp.wait_ge(consts, 1)
            for h in range(HG):
                sp.dma_start(wo[32 * h:32 * h + HD], dram["L0_xattn_wo"].rearrange("(j h r) n -> h r j n", h=HG, r=HD)[h]
                             ).then_inc(w_loaded, 16)
            load(1, 1)
            for e in range(EXPERTS):
                sp.dma_start(w1[:, e], dram["L0_ffn_W1"][e].rearrange("(c p) f -> p c f", p=P)).then_inc(w1_loaded, 16)

            def body(seq, s):
                sp.wait_ge(misc_full, Seq(seq.it, seq.s - 1).use("V2")[0] + 1)
                load(seq.count(1, 2) % SEQS, s)

            sequences(sp, lambda seq: None, body, lambda seq: None)
            for s in range(2):
                sp.wait_ge(ctx_loaded[s], 16 * (SEQS // 2 + 1))

        @block.gpsimd
        def _(pool):
            pool.memset(wo[:], 0.0).then_inc(consts, 1)
            pool.memset(v[:, :, :, D:], 0.0).then_inc(consts, 1)
            pool.memset(eps[:], EPS).then_inc(consts, 1)
            pool.wait_ge(w_loaded, 16 * NUM_W)

            def masked_q(seq, s, b):
                wait(pool, s_full, seq.count(HEADS))
                for o in range(DC):
                    ins = pool.tensor_tensor(
                        qm[:, s, o * 8:(o + 1) * 8, :],
                        qT[:, o, bass.ds(b * STEPS, STEPS)].unsqueeze(1).to_broadcast([P, 8, STEPS]),
                        head_rows[:].unsqueeze(2).to_broadcast([P, 8, STEPS]), ALU.mult)
                ins.then_inc(qm_ready, 1)

            def after(seq):
                pool.wait_ge(inv_ready, seq.count(1))
                wait(pool, o_ready, seq.count(1, -1))
                alone(pool)
                pool.tensor_copy(inv_wide[:], inv[:].unsqueeze(2).to_broadcast([STEPS, HEADS, 32])).then_inc(wide_ready, 1)
                wait(pool, mv_ready, seq.count(1, -1))
                pool.tensor_tensor(x1b[:], x1[:, bass.ds(seq.count(1, -1), 1), :].rearrange("p a d -> p (a d)"),
                                   bo[0:STEPS], ALU.add).then_inc(x1b_ready, 1)

            def body(seq, s):
                if not first(seq):
                    after(seq)
                masked_q(seq, 1 - s, seq.count(1, 1) % SEQS)

            sequences(pool, lambda seq: masked_q(seq, 0, 0), body, after)

        @block.scalar
        def _(act):
            act.preload_act_table_set("natural_log_exp_and_others")
            act.wait_ge(w_loaded, 16 * NUM_W)
            act.wait_ge(consts, 3)

            def copy_k(seq, s):
                for o in range(DC):
                    name = f"K{o}"
                    seq.wait_full(act, name)
                    if o == 0:
                        wait(act, s_full, seq.count(HEADS))
                    ins = act.activation(kT[:, s, o], seq.bank(name)[:, 0:KEYS], ACT.Identity, bias=bk[:, o:o + 1])
                    seq.free(ins, name)

            def copy_pT(seq, j):
                n, rows = len(KCH) - 1, KCH[-1][1]
                act.wait_ge(t_full, seq.count(3 * SPS, 3 * j))
                wait(act, pv_done, seq.count(SPS, j - 2))
                act.copy(pT[0:rows, (j + 1) % 2, n], t_ps[n][0:rows, 0:HG * STEPS]).then_inc(pt_scalar, 1)

            def exps(seq, s, j):
                act.wait_ge(nmx_ready, seq.count(SPS, j + 1))
                for h in range(HG):
                    ins = act.activation(prob[:, j % 2, h], prob[:, j % 2, h], ACT.Exp, bias=nmx[:, j % 2, h:h + 1],
                                         accum_out=rsum[:, s, HG * j + h:HG * j + h + 1])
                ins.then_inc(p_ready, 1)

            def copy_inv(seq):
                seq.wait_full(act, "R")
                wait(act, o_ready, seq.count(1, -1))
                seq.free(act.copy(inv_sb[:], seq.bank("R")[:, 0:HG * STEPS]), "R")

            def deviation(seq):
                act.wait_ge(mv_ready, seq.count(1))
                act.activation(lnv[:], mv[:, 1:2], ACT.Ln, bias=eps[0:STEPS, :]).then_inc(ln_ready, 1)
                act.wait_ge(ln_ready, seq.count(1))
                act.activation(rstd[:], lnv[:], ACT.Exp, scale=-0.5).then_inc(rstd_ready, 1)

            def body(seq, s):
                before = not first(seq)
                for j in range(SPS):
                    if j or before:
                        copy_pT(seq, j)
                    exps(seq, s, j)
                    if j == 1 and before:
                        copy_inv(seq)
                    if j == 0:
                        copy_k(seq, 1 - s)
                    if j == 2 and before:
                        deviation(seq)

            def tail(seq):
                copy_pT(seq, 0)
                copy_inv(seq)
                deviation(seq)

            sequences(act, lambda seq: copy_k(seq, 0), body, tail)

        @block.vector
        def _(dve):
            dve.wait_ge(w_loaded, 16 * NUM_W)
            dve.wait_ge(consts, 3)
            dve.tensor_scalar(mask[:], mask[:], MASKED, None, ALU.mult).then_inc(mask_ready, 1)
            dve.wait_ge(mask_ready, 1)

            def copy_v(seq, s, n):
                name, rows = f"V{n}", KCH[n][1]
                seq.wait_full(dve, name)
                wait(dve, pv_done, seq.count(SPS))
                seq.free(dve.tensor_tensor(v[0:rows, s, n, 0:D], seq.bank(name)[0:rows, 0:D], bv[0:rows], ALU.add), name)

            def mask_and_max(seq, j, h):
                dve.wait_ge(s_full, seq.count(HEADS, HG * j + h + 1))
                if h == 0:
                    wait(dve, t_full, seq.count(3 * SPS, 3 * (j - 1)))
                alone(dve)
                dve.tensor_tensor_reduce(prob[:, j % 2, h], s_ps[h % 2][0:STEPS, 0:KEYS], mask[:], 1.0, -3.0e38,
                                         ALU.add, ALU.max, mx[:, j % 2, h:h + 1]).then_inc(s_taken, 1)

            def copy_pT(seq, j, n):
                dve.wait_ge(t_full, seq.count(3 * SPS, 3 * (j - 1) + n + 1))
                if n == 0:
                    wait(dve, pv_done, seq.count(SPS, j - 2))
                rows = KCH[n][1]
                dve.tensor_copy(pT[0:rows, (j + 1) % 2, n], t_ps[n][0:rows, 0:HG * STEPS]).then_inc(pt_vector, 1)

            def step(seq, j, before):
                for h in range(HG):
                    mask_and_max(seq, j, h)
                    if h in (1, 2) and (j or before):
                        copy_pT(seq, j, h - 1)
                dve.wait_ge(s_taken, seq.count(HEADS, HG * (j + 1)))
                wait(dve, p_ready, seq.count(SPS, j - 1))
                dve.tensor_scalar(nmx[:, j % 2], mx[:, j % 2], -1.0, None, ALU.mult).then_inc(nmx_ready, 1)

            def inverse_sums(seq, s):
                dve.wait_ge(p_ready, seq.count(SPS))
                wait(dve, wide_ready, seq.count(1, -1))
                dve.reciprocal(inv[:], rsum[:, s]).then_inc(inv_ready, 1)

            def normalise_o(seq):
                dve.wait_ge(pv_done, seq.count(SPS))
                seq.wait_freed(dve, "R")
                dve.tensor_tensor(oT[:].rearrange("p j t -> p (j t)"), o_ps[:, 0:HG * STEPS], inv_sb[:], ALU.mult
                                  ).then_inc(o_ready, 1)

            def residual(seq):
                seq.wait_full(dve, "proj")
                dve.wait_ge(x1b_ready, seq.count(1))
                ins = dve.tensor_tensor(res[:], seq.bank("proj")[0:STEPS, 0:D], x1b[:], ALU.add)
                seq.free(ins, "proj")
                seq.wait_freed(dve, "proj")
                dve.bn_stats(stat[:], res[:]).then_inc(stat_ready, 1)
                dve.wait_ge(stat_ready, seq.count(1))
                alone(dve)
                dve.bn_aggr(mv[:], stat[:]).then_inc(mv_ready, 1)

            def normalise(seq):
                dve.wait_ge(rstd_ready, seq.count(1))
                dve.tensor_scalar(x1[:, bass.ds(seq.count(1, -1), 1), :].rearrange("p a d -> p (a d)"), res[:],
                                  mv[:, 0:1], rstd[:], ALU.subtract, ALU.mult).then_inc(x2_kept, 1)
                dve.tensor_scalar(x2[:], res[:], mv[:, 0:1], rstd[:], ALU.subtract, ALU.mult).then_inc(x2_ready, 1)

            def copy_x2T(seq):
                seq.wait_full(dve, "xT")
                seq.free(dve.tensor_copy(x2T[:].rearrange("p c t -> p (c t)"), seq.bank("xT")[:, 0:DC * STEPS]), "xT")

            def copy_logits(seq):
                seq.wait_full(dve, "lg")
                seq.free(dve.tensor_copy(lg[:, bass.ds(seq.count(1, -1), 1), :].rearrange("p a e -> p (a e)"),
                                         seq.bank("lg")[0:STEPS, 0:8]), "lg")

            def lead(seq):
                for n in range(len(KCH)):
                    copy_v(seq, 0, n)

            def body(seq, s):
                before = not first(seq)
                for j in range(SPS):
                    step(seq, j, before)
                    if before:
                        if j == 0:
                            inverse_sums(seq, 1 - s)
                        if j == 1:
                            normalise_o(seq)
                            copy_v(seq, 1 - s, 0)
                        if j == 2:
                            residual(seq)
                            copy_v(seq, 1 - s, 1)
                        if j == 3:
                            normalise(seq)
                            copy_v(seq, 1 - s, 2)
                            copy_x2T(seq)
                            copy_logits(seq)
                    elif j:
                        copy_v(seq, 1 - s, j - 1)

            def tail(seq):
                for n in range(2):
                    copy_pT(seq, 0, n)
                inverse_sums(seq, 1)
                normalise_o(seq)
                residual(seq)
                normalise(seq)
                copy_x2T(seq)
                copy_logits(seq)

            sequences(dve, lead, body, tail)

        @block.tensor
        def _(pe):
            pe.wait_ge(w_loaded, 16 * NUM_W)
            pe.wait_ge(consts, 3)

            def acquire(seq, name):
                _, i, before = seq.use(name)
                wait(pe, misc_free[i], before)
                return seq.bank(name)

            def keys(seq, s, o):
                if o == 0:
                    pe.wait_ge(ctx_loaded[s], half_loads(seq, s))
                bank = acquire(seq, f"K{o}")
                for c in range(DC):
                    ins = pe.matmul(bank[:, 0:KEYS], wk[:, c, o * P:(o + 1) * P], ctxT[:, s, c],
                                    start=(c == 0), stop=(c == DC - 1))
                ins.then_inc(misc_full, 1)

            def half_loads(seq, s):
                return seq.it * 16 + 16 * ((seq.s + 1) // 2 + 1)

            def values(seq, s, n):
                at, rows = KCH[n]
                bank = acquire(seq, f"V{n}")
                for c in range(DC):
                    ins = pe.matmul(bank[0:rows, 0:D], ctxT[:, s, c, at:at + rows], wv[:, c],
                                    start=(c == 0), stop=(c == DC - 1))
                ins.then_inc(misc_full, 1)

            def scores(seq, s, j, h):
                wait(pe, s_taken, seq.count(HEADS, HG * j + h - 1))
                head = HG * j + h
                pe.matmul(s_ps[h % 2][0:STEPS, 0:KEYS], qm[:, s, head], kT[:, s, head // 8],
                          start=True, stop=True).then_inc(s_full, 1)

            def turn(seq, j, n):
                if n == 0:
                    pe.wait_ge(p_ready, seq.count(SPS, j))
                if n < len(KCH) - 1:
                    wait(pe, pt_vector, seq.count(2 * SPS, 2 * (j - 2) + n + 1))
                else:
                    wait(pe, pt_scalar, seq.count(SPS, j - 1))
                at, rows = KCH[n]
                for h in range(HG):
                    ins = pe.transpose(t_ps[n][0:rows, h * STEPS:(h + 1) * STEPS], prob[:, (j + 1) % 2, h, at:at + rows],
                                       ident[0:STEPS, 0:STEPS])
                ins.then_inc(t_full, 1)

            def times_v(seq, s, j):
                pe.wait_ge(pt_vector, seq.count(2 * SPS, 2 * (j - 1)))
                pe.wait_ge(pt_scalar, seq.count(SPS, j - 1))
                jj = (j - 2) % SPS
                if jj == 0:
                    wait(pe, o_ready, seq.count(1))
                for h in range(HG):
                    head = HG * jj + h
                    for n, (_, rows) in enumerate(KCH):
                        ins = pe.matmul(o_ps[32 * h:32 * h + 32, jj * STEPS:(jj + 1) * STEPS],
                                        v[0:rows, s, n, head * HD:head * HD + 32],
                                        pT[0:rows, j % 2, n, h * STEPS:(h + 1) * STEPS],
                                        start=(n == 0), stop=(n == len(KCH) - 1))
                ins.then_inc(pv_done, 1)

            def spread_inv(seq):
                pe.wait_ge(wide_ready, seq.count(1))
                bank = acquire(seq, "R")
                for j in range(HG):
                    ins = pe.matmul(bank[:, j * STEPS:(j + 1) * STEPS],
                                    inv_wide[:, HG * j:HG * (j + 1)].rearrange("p h r -> p (h r)"),
                                    ident[0:STEPS, 0:STEPS], start=True, stop=True)
                ins.then_inc(misc_full, 1)

            def project(seq):
                pe.wait_ge(o_ready, seq.count(1))
                bank = acquire(seq, "proj")
                for j in range(HG):
                    ins = pe.matmul(bank[0:STEPS, 0:D], oT[:, j], wo[:, j], start=(j == 0), stop=(j == HG - 1))
                ins.then_inc(misc_full, 1)

            def turn_x2(seq):
                pe.wait_ge(x2_ready, seq.count(1))
                bank = acquire(seq, "xT")
                for c in range(DC):
                    ins = pe.transpose(bank[:, c * STEPS:(c + 1) * STEPS], x2[:, c * P:(c + 1) * P],
                                       ident[0:STEPS, 0:STEPS])
                ins.then_inc(misc_full, 1)

            def logits(seq):
                seq.wait_freed(pe, "xT")
                bank = acquire(seq, "lg")
                for c in range(DC):
                    ins = pe.matmul(bank[0:STEPS, 0:8], x2T[:, c], wg[:, c], start=(c == 0), stop=(c == DC - 1))
                ins.then_inc(misc_full, 1)

            def lead(seq):
                for o in range(DC):
                    keys(seq, 0, o)
                for n in range(len(KCH)):
                    values(seq, 0, n)

            def body(seq, s):
                before = not first(seq)
                seq_before = Seq(seq.it, seq.s - 1)
                seq_before.wait_freed(pe, "K1")
                seq_before.wait_freed(pe, "V2")
                pe.wait_ge(qm_ready, seq.count(1, 1))
                for j in range(SPS):
                    for h in range(HG):
                        scores(seq, s, j, h)
                        if h < len(KCH) and (j or before):
                            turn(seq, j, h)
                    if j == 0:
                        keys(seq, 1 - s, 0)
                        keys(seq, 1 - s, 1)
                    if j >= 2:
                        times_v(seq, s, j)
                    elif before:
                        times_v(seq, 1 - s, j)
                    if j == 1:
                        if before:
                            spread_inv(seq)
                        values(seq, 1 - s, 0)
                    if j == 2:
                        if before:
                            project(seq)
                        values(seq, 1 - s, 1)
                    if j == 3:
                        values(seq, 1 - s, 2)
                        if before:
                            turn_x2(seq)
                            logits(seq)

            def tail(seq):
                for n in range(len(KCH)):
                    turn(seq, 0, n)
                times_v(seq, 1, 0)
                times_v(seq, 1, 1)
                spread_inv(seq)
                project(seq)
                turn_x2(seq)
                logits(seq)

            sequences(pe, lead, body, tail)


EXPERTS, WIDTH = 8, 1024
FC = WIDTH // P
CAPACITY = 2 * 2 * TOKENS // EXPERTS
TILES = (2 * TOKENS + EXPERTS * (P - 1)) // P
TILES_PER_EXPERT = -(-CAPACITY // P)
SLOTS = TILES * P
TRASH = SLOTS + P
XE_ROWS = TRASH + 2 * TOKENS


def stage_c(pr, x, lg, ident, w1, w1_loaded, scratch, xe, xe_cleared, ye, out):
    nc, dram = pr.nc, pr.dram
    with ExitStack() as ctx:
        def sb(*a):
            return pr.sb(ctx, *a)

        def sem(name):
            return pr.sem(ctx, name)

        w2 = sb("w2", [P, EXPERTS, FC, D])
        b1 = sb("b1", [P, FC, EXPERTS])
        b2 = sb("b2", [P, EXPERTS, D])
        R = [STEPS, SEQS, EXPERTS]
        tri = sb("tri", [STEPS, STEPS])
        ones = sb("ones", [STEPS, STEPS])
        rev = sb("rev", [STEPS, EXPERTS])
        tile_no = sb("tile_no", [STEPS, TILES + 1])
        token_no = sb("token_no", [STEPS, 2, SEQS])
        cont = sb("cont", [STEPS, EXPERTS, SEQS])
        gates = sb("gates", R)
        work = sb("work", R)
        mask = [sb(f"mask{i}", R) for i in range(2)]
        pos_all = [sb(f"pos_all{i}", R) for i in range(2)]
        total = [sb(f"total{i}", [STEPS, EXPERTS, SEQS]) for i in range(2)]
        running = [sb(f"running{i}", [STEPS, EXPERTS, SEQS]) for i in range(2)]
        top = sb("top", [STEPS, SEQS])
        row = sb("row", [STEPS, SEQS])
        gate = [sb(f"gate{i}", [STEPS, SEQS]) for i in range(2)]
        pos = sb("pos", [STEPS, 2, SEQS])
        base_of = sb("base_of", [STEPS, 2, SEQS])
        keep = sb("keep", [STEPS, 2, SEQS])
        weight = sb("weight", [STEPS, 2, SEQS])
        count = sb("count", [STEPS, EXPERTS])
        tiles = sb("tiles", [STEPS, EXPERTS])
        tile_end = sb("tile_end", [STEPS, EXPERTS])
        base = sb("base", [STEPS, EXPERTS])
        steps7 = sb("steps7", [STEPS, EXPERTS, TILES_PER_EXPERT])
        past = sb("past", [STEPS, TILES + 1, EXPERTS])
        expert_f = sb("expert_f", [STEPS, TILES + 1])
        expert = sb("expert", [STEPS, TILES + 1], I32)
        to_slot = sb("to_slot", [STEPS, 2, SEQS], U32)
        from_slot = sb("from_slot", [STEPS, 2, SEQS], U32)
        eps = sb("eps_c", [P, 1])
        b1c = sb("b1c", [P, 2, FC])
        hT = sb("hT", [P, 2, FC, P])
        flat = scratch.rearrange("p c t -> p (c t)")
        h_sb = flat[:, 0:2 * WIDTH].rearrange("p (i f) -> p i f", i=2)
        xs = flat[:, 2 * WIDTH:2 * WIDTH + 2 * D].rearrange("p (i d) -> p i d", i=2)
        xTt = flat[:, 2 * WIDTH + 2 * D:2 * WIDTH + 4 * D].rearrange("p (i c t) -> p i c t", i=2, c=DC)
        y_sb = sb("y_sb", [P, 2, D])
        picked = hT[0:STEPS].rearrange("p i c t -> p (i c t)").rearrange("p (s k d) -> p s k d", s=4, k=2)
        NPICK = 4

        x_ps = pr.psum(ctx, "x_ps", [P, 512])
        h_ps = [pr.psum(ctx, f"h_ps{i}", [P, 512]) for i in range(2)]
        hT_ps = [pr.psum(ctx, f"hT_ps{i}", [P, 512]) for i in range(2)]
        y_ps = pr.psum(ctx, "y_ps_c", [P, 512])

        w2_loaded, b_loaded, consts = sem("w2_loaded"), sem("b_loaded"), sem("consts_c")
        route_step, logit_max, gate_exp = sem("route_step"), sem("logit_max"), sem("gate_exp")
        masks_ready, prefix_full, routed = sem("masks_ready"), sem("prefix_full"), sem("routed")
        dispatched = sem("dispatched")
        xs_loaded = [sem(f"xs_loaded{i}") for i in range(2)]
        xt_full, xt_copied = sem("xt_full"), sem("xt_copied")
        h_full, h_scalar, h_vector = sem("h_full"), sem("h_scalar"), sem("h_vector")
        ht_full, bias_ready, gelu_done = sem("ht_full"), sem("bias_ready"), sem("gelu_done")
        y_full, y_ready = sem("y_full"), sem("y_ready")
        y_stored = [sem(f"y_stored{i}") for i in range(2)]
        picked_in = [sem(f"picked_in{i}") for i in range(NPICK)]
        mix_step, mixed, stat_ready, mv_ready = sem("mix_step"), sem("mixed"), sem("stat_c_ready"), sem("mv_c_ready")
        ln_ready, rstd_ready, out_ready, stored = sem("ln_c_ready"), sem("rstd_c_ready"), sem("out_ready"), sem("stored")

        class Tile:

            def __init__(self, it, s):
                self.it, self.s = it, s

            def count(self, per_tile, more=0):
                return self.it * (2 * per_tile) + (self.s * per_tile + more)

            def at(self, before=0):
                return self.count(1, -before)

        def tile_steps(eng, body):
            for s in range(2):
                body(Tile(0, s), s, (True, s == 1, False))
            with eng.Fori(1, TILES // 2) as it:
                for s in range(2):
                    body(Tile(it, s), s, (True, True, True))
            body(Tile(TILES // 2, 0), 0, (False, True, True))
            body(Tile(TILES // 2, 1), 1, (False, False, True))

        const_count = 9

        def finish(dve, s):
            dve.wait_ge(rstd_ready, s + 1)
            dve.tensor_scalar(x[:, s], x[:, s], pos_all[0][:, s, 0:1], row[:, s:s + 1],
                              ALU.subtract, ALU.mult).then_inc(out_ready, 1)

        block = ctx.enter_context(nc.Block())

        @block.sync
        def _(sp):
            sp.dma_start(b1[:], dram["b1T"]).then_inc(b_loaded, 16)
            sp.dma_start(b2[:].rearrange("p e d -> p (e d)"), dram["L0_ffn_b2"].rearrange("(a e) d -> a (e d)", a=1)
                         .partition_broadcast(P)).then_inc(b_loaded, 16)
            for e in range(EXPERTS):
                sp.dma_start(w2[:, e], dram["L0_ffn_W2"][e].rearrange("(c p) d -> p c d", p=P)).then_inc(w2_loaded, 16)

            def load(t, s):
                sp.dma_start(xs[:, s], xe[bass.ds(t * P, P), :]).then_inc(xs_loaded[s], 16)

            sp.wait_ge(dispatched, 16 * 2 * SEQS)
            load(0, 0)

            def body(tile, s, parts):
                first, _, last = parts
                if first:
                    wait(sp, xt_full, tile.count(1))
                    load(tile.at(-1), 1 - s)
                if last:
                    sp.wait_ge(y_ready, tile.count(1, -1))
                    sp.dma_start(ye[bass.ds(tile.at(2) * P, P), :], y_sb[:, s]).then_inc(y_stored[s], 16)

            tile_steps(sp, body)
            for s in range(2):
                sp.wait_ge(y_stored[s], 16 * (TILES // 2 + 1))
            sp.wait_ge(xs_loaded[TILES % 2], 16 * (TILES // 2 + 1))
            for s in range(SEQS):
                sp.wait_ge(out_ready, s + 1)
                sp.dma_start(out[s], x[:, s]).then_inc(stored, 16)
            sp.wait_ge(stored, 16 * SEQS)

        @block.gpsimd
        def _(pool):
            def const(ins):
                const.made += 1
                ins.then_inc(consts, 1)
                pool.wait_ge(consts, const.made)

            const.made = 0
            const(pool.memset(ones[:], 1.0))
            const(pool.affine_select(out=tri[:], in_=ones[:], compare_op=ALU.is_gt, fill=0.0, base=0,
                                     pattern=[[1, STEPS]], channel_multiplier=-1))
            const(pool.iota(rev[:], pattern=[[-1, EXPERTS]], base=EXPERTS, channel_multiplier=0,
                            allow_small_or_imprecise_dtypes=True))
            const(pool.iota(tile_no[:], pattern=[[1, TILES + 1]], base=0, channel_multiplier=0,
                            allow_small_or_imprecise_dtypes=True))
            const(pool.iota(token_no[:], pattern=[[TOKENS, 2], [STEPS, SEQS]], base=TRASH, channel_multiplier=1,
                            allow_small_or_imprecise_dtypes=True))
            const(pool.iota(steps7[:], pattern=[[0, EXPERTS], [P, TILES_PER_EXPERT]], base=0, channel_multiplier=0,
                            allow_small_or_imprecise_dtypes=True))
            const(pool.memset(cont[:], 1.0))
            const(pool.memset(cont[:, :, 0:1], 0.0))
            const(pool.memset(eps[:], EPS))
            for s in range(2):
                pool.sem_inc(y_stored[s], 16)
            pool.wait_ge(xe_cleared, 16)
            pool.wait_ge(routed, 2)
            for k in range(2):
                for s in range(SEQS):
                    pool.indirect_dma_start(
                        out=xe[:], out_offset=bass.IndirectOffsetOnAxis(ap=to_slot[:, k, s:s + 1], axis=0),
                        in_=x[:, s], in_offset=None).then_inc(dispatched, 16)
            for s in range(2):
                pool.wait_ge(y_stored[s], 16 * (TILES // 2 + 1))
            for s in range(SEQS):
                if s >= NPICK:
                    pool.wait_ge(mixed, s - NPICK + 1)
                for k in range(2):
                    pool.indirect_dma_start(
                        out=picked[:, s % NPICK, k], out_offset=None, in_=ye[:],
                        in_offset=bass.IndirectOffsetOnAxis(ap=from_slot[:, k, s:s + 1], axis=0)
                    ).then_inc(picked_in[s % NPICK], 16)

        @block.scalar
        def _(act):
            act.wait_ge(logit_max, 1)
            act.activation(gates[:], gates[:], ACT.Exp).then_inc(gate_exp, 1)

            def body(tile, s, parts):
                first, middle, _ = parts
                if first:
                    act.wait_ge(h_full, tile.count(2, 1))
                    wait(act, ht_full, tile.count(1, -1))
                    act.copy(h_sb[:, s, 0:512], h_ps[0][:]).then_inc(h_scalar, 1)
                if middle:
                    act.wait_ge(ht_full, tile.count(1))
                    act.wait_ge(bias_ready, tile.count(1))
                    wait(act, y_full, tile.count(1, -2))
                    for c in range(FC):
                        ins = act.activation(hT[:, 1 - s, c], hT_ps[c // 4][:, (c % 4) * P:(c % 4 + 1) * P], ACT.Gelu,
                                             bias=b1c[:, 1 - s, c:c + 1])
                    ins.then_inc(gelu_done, 1)

            tile_steps(act, body)
            act.preload_act_table_set("natural_log_exp_and_others")
            act.wait_ge(consts, const_count)
            for s in range(SEQS):
                act.wait_ge(mv_ready, s + 1)
                act.activation(top[:, s:s + 1], pos_all[0][:, s, 1:2], ACT.Ln, bias=eps[0:STEPS, :]).then_inc(ln_ready, 1)
                act.wait_ge(ln_ready, s + 1)
                act.activation(row[:, s:s + 1], top[:, s:s + 1], ACT.Exp, scale=-0.5).then_inc(rstd_ready, 1)

        @block.vector
        def _(dve):
            done = [0]

            def link(ins):
                done[0] += 1
                ins.then_inc(route_step, 1)
                dve.wait_ge(route_step, done[0])

            def over_e(a):
                return a.unsqueeze(2).to_broadcast(R)

            def over_s(a):
                return a.unsqueeze(1).to_broadcast(R)

            def by_seq(a):
                return a.rearrange("p e s -> p s e")

            def first_hot(values, largest, onehot):
                link(dve.tensor_tensor(work[:], values[:], over_e(largest[:]), ALU.is_equal))
                link(dve.tensor_tensor(work[:], work[:], over_s(rev[:]), ALU.mult))
                link(dve.tensor_reduce(row[:], work[:], AX_X, ALU.max))
                link(dve.tensor_tensor(onehot[:], over_s(rev[:]), over_e(row[:]), ALU.is_equal))

            def pick(result, onehot, values):
                link(dve.tensor_tensor(work[:], onehot[:], values, ALU.mult))
                link(dve.tensor_reduce(result, work[:], AX_X, ALU.add))

            dve.wait_ge(consts, const_count)
            link(dve.tensor_reduce(top[:], lg[:], AX_X, ALU.max))
            dve.tensor_tensor(gates[:], lg[:], over_e(top[:]), ALU.subtract).then_inc(logit_max, 1)
            dve.wait_ge(gate_exp, 1)
            link(dve.tensor_reduce(top[:], gates[:], AX_X, ALU.add))
            link(dve.reciprocal(top[:], top[:]))
            link(dve.tensor_tensor(gates[:], gates[:], over_e(top[:]), ALU.mult))
            link(dve.tensor_reduce(gate[0][:], gates[:], AX_X, ALU.max))
            first_hot(gates, gate[0], mask[0])
            link(dve.scalar_tensor_tensor(out=lg[:], in0=mask[0][:], scalar=-3.0e38, in1=lg[:],
                                          op0=ALU.mult, op1=ALU.add))
            link(dve.tensor_reduce(top[:], lg[:], AX_X, ALU.max))
            first_hot(lg, top, mask[1])
            dve.sem_inc(masks_ready, 1)
            pick(gate[1][:], mask[1], gates[:])
            link(dve.scalar_tensor_tensor(out=top[:], in0=gate[0][:], scalar=1e-9, in1=gate[1][:],
                                          op0=ALU.add, op1=ALU.add))
            link(dve.reciprocal(top[:], top[:]))
            for k in range(2):
                link(dve.tensor_tensor(weight[:, k], gate[k][:], top[:], ALU.mult))
            dve.wait_ge(prefix_full, 1)
            for k in range(2):
                tot = h_ps[k][0:STEPS, SEQS * EXPERTS:2 * SEQS * EXPERTS].rearrange("p (s e) -> p e s", e=EXPERTS)
                link(dve.tensor_copy(total[k][:], tot))
                link(dve.tensor_tensor_scan(running[k][:].rearrange("p e s -> p (e s)"),
                                            cont[:].rearrange("p e s -> p (e s)"),
                                            total[k][:].rearrange("p e s -> p (e s)"), 0.0, ALU.mult, ALU.add))
                within = h_ps[k][0:STEPS, 0:SEQS * EXPERTS].rearrange("p (s e) -> p s e", e=EXPERTS)
                link(dve.tensor_tensor(pos_all[k][:], within, by_seq(running[k][:]), ALU.add))
                link(dve.tensor_tensor(pos_all[k][:], pos_all[k][:], by_seq(total[k][:]), ALU.subtract))
            all_first = running[0][:, :, SEQS - 1]
            link(dve.tensor_tensor(pos_all[1][:], pos_all[1][:], over_s(all_first), ALU.add))
            link(dve.tensor_tensor(count[:], all_first, running[1][:, :, SEQS - 1], ALU.add))
            link(dve.tensor_scalar(count[:], count[:], float(CAPACITY), None, ALU.min))
            link(dve.tensor_tensor(steps7[:], count[:].unsqueeze(2).to_broadcast([STEPS, EXPERTS, TILES_PER_EXPERT]),
                                   steps7[:], ALU.is_gt))
            link(dve.tensor_reduce(tiles[:], steps7[:], AX_X, ALU.add))
            link(dve.tensor_tensor_scan(tile_end[:], ones[:, 0:EXPERTS], tiles[:], 0.0, ALU.mult, ALU.add))
            link(dve.tensor_tensor(base[:], tile_end[:], tiles[:], ALU.subtract))
            link(dve.tensor_scalar(base[:], base[:], float(P), None, ALU.mult))
            for k in range(2):
                pick(pos[:, k], mask[k], pos_all[k][:])
                pick(base_of[:, k], mask[k], over_s(base[:]))
            link(dve.tensor_scalar(keep[:], pos[:], float(CAPACITY), None, ALU.is_lt))
            link(dve.tensor_tensor(weight[:], weight[:], keep[:], ALU.mult))
            link(dve.tensor_tensor(pos[:], pos[:], base_of[:], ALU.add))
            link(dve.tensor_tensor(pos[:], pos[:], token_no[:], ALU.subtract))
            link(dve.tensor_tensor(base_of[:], pos[:], keep[:], ALU.mult))
            link(dve.tensor_tensor(base_of[:], base_of[:], token_no[:], ALU.add))
            dve.tensor_copy(to_slot[:], base_of[:]).then_inc(routed, 1)
            link(dve.tensor_tensor(pos[:], pos[:], token_no[:], ALU.add))
            link(dve.tensor_tensor(pos[:], pos[:], keep[:], ALU.mult))
            dve.tensor_copy(from_slot[:], pos[:]).then_inc(routed, 1)
            shape = [STEPS, TILES + 1, EXPERTS]
            link(dve.tensor_tensor(past[:], tile_end[:].unsqueeze(1).to_broadcast(shape),
                                   tile_no[:].unsqueeze(2).to_broadcast(shape), ALU.is_le))
            link(dve.tensor_reduce(expert_f[:], past[:], AX_X, ALU.add))
            link(dve.tensor_scalar(expert_f[:], expert_f[:], float(EXPERTS - 1), None, ALU.min))
            dve.tensor_copy(expert[:], expert_f[:]).then_inc(routed, 1)
            dve.wait_ge(routed, 3)
            dve.wait_ge(b_loaded, 32)

            def copy_xT(tile, s):
                dve.wait_ge(xt_full, tile.count(1, 1))
                wait(dve, h_full, tile.count(2, -2))
                dve.tensor_copy(xTt[:, s].rearrange("p c t -> p (c t)"), x_ps[:, 0:DC * P]).then_inc(xt_copied, 1)

            copy_xT(Tile(0, 0), 0)

            def body(tile, s, parts):
                first, _, last = parts
                if first:
                    e = dve.value_load(expert[0:1, bass.ds(tile.at(), 1)], min_val=0, max_val=EXPERTS - 1)
                    wait(dve, gelu_done, tile.count(1, -1))
                    dve.tensor_copy(b1c[:, s], b1[:, :, bass.ds(e, 1)].rearrange("p c a -> p (c a)")
                                    ).then_inc(bias_ready, 1)
                    dve.wait_ge(h_full, tile.count(2, 2))
                    wait(dve, ht_full, tile.count(1, -1))
                    dve.tensor_copy(h_sb[:, s, 512:], h_ps[1][:]).then_inc(h_vector, 1)
                    copy_xT(Tile(tile.it, tile.s + 1), 1 - s)
                if last:
                    e = dve.value_load(expert[0:1, bass.ds(tile.at(2), 1)], min_val=0, max_val=EXPERTS - 1)
                    dve.wait_ge(y_full, tile.count(1, -1))
                    dve.wait_ge(y_stored[s], (tile.it + tile.s // 2) * 16)
                    dve.tensor_tensor(y_sb[:, s], y_ps[:, 0:D], b2[:, bass.ds(e, 1)].rearrange("p a d -> p (a d)"),
                                      ALU.add).then_inc(y_ready, 1)

            tile_steps(dve, body)

            for s in range(SEQS):
                dve.wait_ge(picked_in[s % NPICK], 32 * (s // NPICK + 1))
                dve.scalar_tensor_tensor(out=x[:, s], in0=picked[:, s % NPICK, 0], scalar=weight[:, 0, s:s + 1],
                                         in1=x[:, s], op0=ALU.mult, op1=ALU.add).then_inc(mix_step, 1)
                dve.wait_ge(mix_step, s + 1)
                dve.scalar_tensor_tensor(out=x[:, s], in0=picked[:, s % NPICK, 1], scalar=weight[:, 1, s:s + 1],
                                         in1=x[:, s], op0=ALU.mult, op1=ALU.add).then_inc(mixed, 1)
                dve.wait_ge(mixed, s + 1)
                dve.bn_stats(gates[:, s, 0:6], x[:, s]).then_inc(stat_ready, 1)
                dve.wait_ge(stat_ready, s + 1)
                dve.bn_aggr(pos_all[0][:, s, 0:2], gates[:, s, 0:6]).then_inc(mv_ready, 1)
                if s:
                    finish(dve, s - 1)
            finish(dve, SEQS - 1)

        @block.tensor
        def _(pe):
            pe.wait_ge(masks_ready, 1)
            for k in range(2):
                flat_mask = mask[k][:].rearrange("p s e -> p (s e)")
                pe.matmul(h_ps[k][0:STEPS, 0:SEQS * EXPERTS], tri[:], flat_mask, start=True, stop=True)
                ins = pe.matmul(h_ps[k][0:STEPS, SEQS * EXPERTS:2 * SEQS * EXPERTS], ones[:], flat_mask,
                                start=True, stop=True)
            ins.then_inc(prefix_full, 1)
            pe.wait_ge(routed, 3)
            pe.wait_ge(w1_loaded, 16 * EXPERTS)

            def turn_x(tile, s):
                pe.wait_ge(xs_loaded[s], tile.it * 16 + 16 * (tile.s // 2 + 1))
                wait(pe, xt_copied, tile.count(1))
                for c in range(DC):
                    ins = pe.transpose(x_ps[:, c * P:(c + 1) * P], xs[:, s, c * P:(c + 1) * P], ident[:])
                ins.then_inc(xt_full, 1)

            turn_x(Tile(0, 0), 0)

            def body(tile, s, parts):
                first, middle, last = parts
                if first:
                    e = pe.value_load(expert[0:1, bass.ds(tile.at(), 1)], min_val=0, max_val=EXPERTS - 1)
                    pe.wait_ge(xt_copied, tile.count(1, 1))
                    wait(pe, h_scalar, tile.count(1))
                    wait(pe, h_vector, tile.count(1))
                    for half in range(2):
                        for c in range(DC):
                            ins = pe.matmul(h_ps[half][:], xTt[:, s, c],
                                            w1[:, bass.ds(e, 1), c, half * 512:(half + 1) * 512].rearrange("p a f -> p (a f)"),
                                            start=(c == 0), stop=(c == DC - 1))
                        ins.then_inc(h_full, 1)
                    turn_x(Tile(tile.it, tile.s + 1), 1 - s)
                if middle:
                    pe.wait_ge(h_scalar, tile.count(1))
                    pe.wait_ge(h_vector, tile.count(1))
                    wait(pe, gelu_done, tile.count(1, -1))
                    for c in range(FC):
                        ins = pe.transpose(hT_ps[c // 4][:, (c % 4) * P:(c % 4 + 1) * P],
                                           h_sb[:, 1 - s, c * P:(c + 1) * P], ident[:])
                    ins.then_inc(ht_full, 1)
                if last:
                    e = pe.value_load(expert[0:1, bass.ds(tile.at(2), 1)], min_val=0, max_val=EXPERTS - 1)
                    pe.wait_ge(gelu_done, tile.count(1, -1))
                    wait(pe, y_ready, tile.count(1, -2))
                    for c in range(FC):
                        ins = pe.matmul(y_ps[:, 0:D], hT[:, s, c],
                                        w2[:, bass.ds(e, 1), c, :].rearrange("p a d -> p (a d)"),
                                        start=(c == 0), stop=(c == FC - 1))
                    ins.then_inc(y_full, 1)

            pe.wait_ge(w2_loaded, 16 * EXPERTS)
            tile_steps(pe, body)


def program(nc, dram, out):
    pr = Program(nc, dram)
    with ExitStack() as ctx:
        ident = pr.sb(ctx, "ident", [P, P])
        x1 = pr.sb(ctx, "x1", [STEPS, SEQS, D])
        qT = pr.sb(ctx, "qT", [P, DC, TOKENS])
        lg = pr.sb(ctx, "lg", [STEPS, SEQS, EXPERTS])
        xe = nc.dram_tensor("xe", (XE_ROWS, D), F32, kind="Internal").ap()
        ye = nc.dram_tensor("ye", (SLOTS, D), F32, kind="Internal").ap()
        xe_cleared, w1_loaded = pr.sem(ctx, "xe_cleared"), pr.sem(ctx, "w1_loaded")
        stage_a(pr, x1, qT, ident, xe, xe_cleared)
        w1 = pr.sb(ctx, "w1", [P, EXPERTS, DC, WIDTH])
        stage_b(pr, x1, qT, ident, lg, w1, w1_loaded)
        stage_c(pr, x1, lg, ident, w1, w1_loaded, qT[:], xe, xe_cleared, ye, out)


def kernel(**inputs):
    import numpy as np
    import concourse.bacc as bacc
    from concourse.bass_utils import run_bass_kernel_spmd

    a = {k: np.asarray(v) for k, v in inputs.items()}

    def columns(v):
        return v.reshape(-1, P, *v.shape[1:]).swapaxes(0, 1)

    laid = dict(
        xT=a["x"].reshape(TOKENS, D).T,
        ctxT=a["ctx_1024"].transpose(0, 2, 1),
        w_inT=a["L0_attn_w_in"].T,
        lora_B_inT=a["L0_attn_lora_B_in"].T,
        lora_B_outT=a["L0_attn_lora_B_out"].T,
        w_xprojT=a["L0_attn_w_xproj"].T,
        w_dtT=a["L0_attn_w_dt"].T,
        w_outT=a["L0_attn_w_out"].T,
        conv_w=columns(a["L0_attn_conv_w"].reshape(INNER, TAPS)),
        conv_b=columns(a["L0_attn_conv_b"]),
        b_dt=columns(a["L0_attn_b_dt"]),
        Dp=columns(a["L0_attn_Dp"]),
        A_log=columns(a["L0_attn_A_log"]),
        bq=columns(a["L0_xattn_bq"]),
        bk=columns(a["L0_xattn_bk"]),
        head_rows=(np.arange(P)[:, None] // HD == np.arange(P // HD)).astype(np.float32),
        b1T=columns(a["L0_ffn_b1"].T),
    )
    for name in ("x", "mask_1x1xSxS2_fk1", "L0_attn_lora_A_in", "L0_attn_lora_A_out", "L0_attn_mask_in",
                 "L0_attn_mask_out", "L0_xattn_wq", "L0_xattn_wk", "L0_xattn_wv", "L0_xattn_wo",
                 "L0_xattn_bv", "L0_xattn_bo", "L0_ffn_Wg", "L0_ffn_W1", "L0_ffn_W2", "L0_ffn_b2"):
        laid[name] = a[name]
    laid = {k: np.ascontiguousarray(v) for k, v in laid.items()}
    nc = bacc.Bacc("TRN2", target_bir_lowering=False, num_devices=1)
    dram = {k: nc.dram_tensor(f"in_{k}", v.shape, mybir.dt.from_np(v.dtype), kind="ExternalInput").ap()
            for k, v in laid.items()}
    out = nc.dram_tensor("out_0", (SEQS, STEPS, D), F32, kind="ExternalOutput").ap()
    program(nc, dram, out)
    r = run_bass_kernel_spmd(nc, [{f"in_{k}": v for k, v in laid.items()}], core_ids=[0])
    return r.results[0]["out_0"]
```

```python
from contextlib import ExitStack

import concourse.bass as bass
from concourse import mybir

F32 = mybir.dt.float32
F32R = mybir.dt.float32r
I32 = mybir.dt.int32
U32 = mybir.dt.uint32
ALU = mybir.AluOpType
ACT = mybir.ActivationFunctionType
AX_X = mybir.AxisListType.X

P = 128
SEQS, STEPS, D = 16, 100, 256
TOKENS = SEQS * STEPS
DC = D // P
INNER, STATES, TAPS, RANK, LORA = 512, 16, 4, 64, 16
G = INNER // P
QS = 4
QUADS = SEQS // QS
QT = QS * STEPS
PAD = STEPS + TAPS - 1
LORA_SCALING = 2.0
EPS = 1e-5
UNITS = QUADS * STATES
HB_RING, DA_RING = 4, 3
SERIES = [(-1.0) ** (k + 1) / k for k in range(4, 0, -1)]
SERIES_BELOW = 2.0 ** -6


class Program:

    def __init__(self, nc, dram):
        self.nc, self.dram = nc, dram

    def sb(self, ctx, name, shape, dt=F32):
        return ctx.enter_context(self.nc.sbuf_tensor(name, shape, dt))

    def psum(self, ctx, name, shape, dt=F32):
        return ctx.enter_context(self.nc.psum_tensor(name, shape, dt))

    def sem(self, ctx, name):
        return ctx.enter_context(self.nc.semaphore(name))


def misc_schedule():
    slots = {}

    def put(q, n, *task):
        slots.setdefault((q, n), []).append(task)

    for j in range(G):
        put(-1, 0, "xz", 0, j)
    put(-1, 0, "bcdt", 0)
    for g in range(G):
        put(-1, 0, "delta", 0, g)
        put(0, g, "xz", 0, G + g)
    for q in range(QUADS + 1):
        if q:
            for s in range(QS):
                put(q, 3 + s // 2, "proj", q - 1, s)
            for c in range(DC):
                put(q, 7, "x1T", q - 1, c)
            for o in range(DC):
                put(q, 8, "q", q - 1, o)
        if q + 1 < QUADS:
            for j, n in enumerate((1, 1, 2, 2, 9, 10, 11, 12)):
                put(q, n, "xz", q + 1, j)
            put(q, 5, "bcdt", q + 1)
            for g in range(G):
                put(q, 6, "delta", q + 1, g)
    order = sorted(slots)
    number, m = {}, 0
    for key in order:
        for task in slots[key]:
            number[task] = m
            m += 1
    return slots, number


def stage_a(pr, x1, q_parts, q_stored, ident, xe, xe_cleared):
    nc, dram = pr.nc, pr.dram
    slots, number = misc_schedule()
    with ExitStack() as ctx:
        def sb(*a):
            return pr.sb(ctx, *a)

        def sem(name):
            return pr.sem(ctx, name)

        w_in = sb("w_in", [P, DC, 2 * INNER])
        w_x = sb("w_x", [P, G, RANK + 4 * STATES])
        w_dt = sb("w_dt", [P, INNER])
        w_out = sb("w_out", [P, G, D])
        wq = sb("wq", [P, DC, D])
        bq = sb("bq", [P, DC])
        conv_w = sb("conv_w", [P, G, TAPS])
        conv_b = sb("conv_b", [P, G])
        b_dt = sb("b_dt", [P, G])
        skip = sb("skip", [P, G])
        decay = sb("decay", [P, G, STATES])
        eps = sb("eps", [P, 1])
        q_sb = sb("q_sb", [P, 2, DC, QT], F32R)
        sel = sb("sel", [P, 2 * STATES], F32R)

        zeros = sb("zeros", [P, D])
        xT = sb("xT", [P, 2, DC, QT])
        xrow = sb("xrow", [STEPS, QS, D])
        xpad = sb("xpad", [P, G, QS, PAD])
        u = sb("u", [P, 2, G, QT])
        zs = sb("zs", [P, 2, G, QT])
        delta = sb("delta", [P, 2, G, QT])
        du = sb("du", [P, 2, G, QT])
        tmp = sb("tmp", [P, G, QT])
        logs = sb("logs", [P, G, QT])
        small = sb("small", [P, G, QT], mybir.dt.uint8)
        dtT = sb("dtT", [P, QT])
        bcs = sb("bcs", [P, 2, QT], F32R)
        Bs = sb("Bs", [P, 3, QT])
        Cs = sb("Cs", [P, 3, QT])
        dA = sb("dA", [P, DA_RING, G, QS, STEPS])
        hb = sb("hb", [P, HB_RING, G, QT])
        yz, x1T = tmp, logs[:, 0:DC]
        stat = sb("stat", [STEPS, QS, 6])
        mv = sb("mv", [STEPS, QS, 2])
        lnv = sb("lnv", [STEPS, QS])
        rstd = sb("rstd", [STEPS, QS])

        y_ps = [pr.psum(ctx, f"y_ps{g}", [P, 512]) for g in range(G)]
        b_ps = pr.psum(ctx, "b_ps", [P, 512])
        c_ps = pr.psum(ctx, "c_ps", [P, 512])
        misc = [pr.psum(ctx, f"misc{i}", [P, 512]) for i in range(2)]

        small_loaded = sem("small_loaded")
        w_in_loaded, w_loaded, lora_loaded = sem("w_in_loaded"), sem("w_loaded"), sem("lora_loaded")
        xT_loaded = [sem(f"xT_loaded{i}") for i in range(2)]
        xrow_loaded = sem("xrow_loaded")
        consts = sem("consts")
        zeroed = sem("zeroed")
        lora_scaled, fold_full, w_folded = sem("lora_scaled"), sem("fold_full"), sem("w_folded")
        decay_exp, decay_ready = sem("decay_exp"), sem("decay_ready")
        misc_full = sem("misc_full")
        misc_free = [sem(f"misc_free{i}") for i in range(2)]
        xs_copied, z_copied, conv_step, conv_done = sem("xs_copied"), sem("z_copied"), sem("conv_step"), sem("conv_done")
        u_ready, zs_ready, dt_ready = sem("u_ready"), sem("zs_ready"), sem("dt_ready")
        bc_high, bc_ready = sem("bc_high"), sem("bc_ready")
        v_ready, sp_step, log_ready, delta_ready, du_ready = (
            sem("v_ready"), sem("sp_step"), sem("log_ready"), sem("delta_ready"), sem("du_ready"))
        series_step, log_patched = sem("series_step"), sem("log_patched")
        b_full, b_copied, c_full, c_copied = sem("b_full"), sem("b_copied"), sem("c_full"), sem("c_copied")
        dA_ready, dbu_ready, scan_done, hc_done, added = (
            sem("dA_ready"), sem("dbu_ready"), sem("scan_done"), sem("hc_done"), sem("added"))
        y_taken, yz_ready = sem("y_taken"), sem("yz_ready")
        stat_ready, mv_ready, ln_ready, rstd_ready, x1_ready = (
            sem("stat_ready"), sem("mv_ready"), sem("ln_ready"), sem("rstd_ready"), sem("x1_ready"))
        q_scaled = sem("q_scaled")
        q_high, q_ready = sem("q_high"), sem("q_ready")

        lora_a = hb[0:LORA, 0, 0:2, :].rearrange("p g t -> p (g t)")[:, 0:D + INNER]
        lora_b = hb[0:LORA, 1, :, :].rearrange("p g t -> p (g t)")[:, 0:2 * INNER + D]
        lora_m = hb[0:LORA, 2, :, :].rearrange("p g t -> p (g t)")[:, 0:2 * INNER + D]
        A_IN, A_OUT = lora_a[:, 0:D], lora_a[:, D:]
        B_IN, B_OUT = lora_b[:, 0:2 * INNER], lora_b[:, 2 * INNER:]
        folds = [(w_in[:, c, f * 512:(f + 1) * 512], A_IN[:, c * P:(c + 1) * P], B_IN[:, f * 512:(f + 1) * 512])
                 for f in range(2) for c in range(DC)]
        folds += [(w_out[:, g, :], A_OUT[:, g * P:(g + 1) * P], B_OUT) for g in range(G)]
        NUM_SMALL, NUM_W = 8, 3

        def misc_bank(task):
            return misc[number[task] % 2]

        def wait_full(eng, task):
            eng.wait_ge(misc_full, number[task] + 1)

        def free_bank(ins, task):
            return ins.then_inc(misc_free[number[task] % 2], 1)

        block = ctx.enter_context(nc.Block())

        @block.sync
        def _(sp):
            sp.dma_start(lora_a[:, 0:D], dram["L0_attn_lora_A_in"]).then_inc(lora_loaded, 16)
            sp.dma_start(A_OUT, dram["L0_attn_lora_A_out"]).then_inc(lora_loaded, 16)
            sp.dma_start(B_IN, dram["lora_B_inT"]).then_inc(lora_loaded, 16)
            sp.dma_start(B_OUT, dram["lora_B_outT"]).then_inc(lora_loaded, 16)
            sp.dma_start(lora_m[:, 0:2 * INNER], dram["L0_attn_mask_in"].rearrange("(a n) -> a n", a=1)
                         .partition_broadcast(LORA)).then_inc(lora_loaded, 16)
            sp.dma_start(lora_m[:, 2 * INNER:], dram["L0_attn_mask_out"].rearrange("(a n) -> a n", a=1)
                         .partition_broadcast(LORA)).then_inc(lora_loaded, 16)
            sp.dma_start(w_in[:], dram["w_inT"].rearrange("(c p) n -> p c n", p=P)).then_inc(w_in_loaded, 16)

            def load_xT(q):
                if q >= 2:
                    sp.wait_ge(misc_full, number[("xz", q - 2, 2 * G - 1)] + 1)
                sp.dma_start(xT[:, q % 2], dram["xT"][:, q * QT:(q + 1) * QT].rearrange("(c p) t -> p c t", p=P)
                             ).then_inc(xT_loaded[q % 2], 16)

            def load_xrow(q):
                if q >= 1:
                    sp.wait_ge(x1_ready, QS * q)
                sp.dma_start(xrow[:], dram["x"][q * QS:(q + 1) * QS].rearrange("s t d -> t s d")
                             ).then_inc(xrow_loaded, 16)

            def store_q(q):
                for o in range(DC):
                    last = number[("q", q, o)]
                    sp.wait_ge(misc_free[last % 2], last // 2 + 1)
                for part in range(2):
                    sp.dma_start(q_parts[part, :, q * QT:(q + 1) * QT].rearrange("(c p) t -> p c t", p=P),
                                 q_sb[:, part].bitcast(F32)).then_inc(q_stored, 16)

            load_xT(0)
            sp.dma_start(w_out[:], dram["w_outT"].rearrange("(g p) n -> p g n", p=P)).then_inc(w_loaded, 16)
            sp.dma_start(wq[:], dram["L0_xattn_wq"].rearrange("(c p) n -> p c n", p=P)).then_inc(w_loaded, 16)
            sp.dma_start(bq[:], dram["bq"]).then_inc(w_loaded, 16)
            load_xT(1)
            load_xrow(0)
            sp.wait_ge(consts, 1)
            sp.dma_start(xe[0:SLOTS + P].rearrange("(n p) d -> p n d", p=P),
                         zeros[:].unsqueeze(1).to_broadcast([P, TILES + 1, D])).then_inc(xe_cleared, 16)
            for q in range(1, QUADS):
                if q + 1 < QUADS:
                    load_xT(q + 1)
                load_xrow(q)
                store_q(q - 1)
            store_q(QUADS - 1)
            sp.wait_ge(q_stored, 32 * QUADS)

        @block.gpsimd
        def _(pool):
            pool.memset(ident[:], 0.0).then_inc(zeroed, 1)
            pool.memset(zeros[:], 0.0).then_inc(consts, 1)
            pool.memset(dtT[:], 0.0).then_inc(consts, 1)
            pool.wait_ge(consts, 2)
            pool.memset(w_dt[RANK:, :], 0.0).then_inc(consts, 1)
            pool.wait_ge(consts, 3)
            pool.memset(xpad[:, :, :, 0:TAPS - 1], 0.0).then_inc(consts, 1)
            pool.memset(dA[:, :, :, :, 0:1], 0.0).then_inc(consts, 1)
            pool.memset(eps[:], EPS).then_inc(consts, 1)
            pool.wait_ge(zeroed, 1)
            pool.affine_select(out=ident[:], in_=ident[:], compare_op=ALU.not_equal, fill=1.0, base=0,
                               pattern=[[-1, P]], channel_multiplier=1).then_inc(zeroed, 1)

            def make_du(q):
                pool.wait_ge(delta_ready, q + 1)
                pool.tensor_tensor(du[:, q % 2], delta[:, q % 2], u[:, q % 2], ALU.mult).then_inc(du_ready, 1)

            pool.wait_ge(fold_full, len(folds))
            make_du(0)
            for q in range(QUADS):
                for n in range(STATES):
                    U = q * STATES + n
                    if n == 0:
                        pool.wait_ge(du_ready, q + 1)
                    pool.wait_ge(b_copied, U + 1)
                    if U >= HB_RING:
                        pool.wait_ge(added, U - HB_RING + 1)
                    pool.tensor_tensor(hb[:, U % HB_RING], du[:, q % 2],
                                       Bs[:, U % 3].unsqueeze(1).to_broadcast([P, G, QT]),
                                       ALU.mult).then_inc(dbu_ready, 1)
                    if n == STATES - 1 and q + 1 < QUADS:
                        make_du(q + 1)

        @block.scalar
        def _(act):
            act.dma_start(conv_w[:], dram["conv_w"]).then_inc(small_loaded, 16)
            act.dma_start(conv_b[:], dram["conv_b"]).then_inc(small_loaded, 16)
            act.dma_start(b_dt[:], dram["b_dt"]).then_inc(small_loaded, 16)
            act.dma_start(skip[:], dram["Dp"]).then_inc(small_loaded, 16)
            act.dma_start(decay[:], dram["A_log"]).then_inc(small_loaded, 16)
            wx = dram["w_xprojT"].rearrange("(g p) n -> p g n", p=P)
            act.dma_start(w_x[:, :, 0:RANK + 2 * STATES], wx).then_inc(small_loaded, 16)
            act.dma_start(w_x[:, :, RANK + 2 * STATES:], wx[:, :, RANK:]).then_inc(small_loaded, 16)
            act.dma_start(w_dt[0:RANK, :], dram["w_dtT"]).then_inc(small_loaded, 16)
            act.wait_ge(small_loaded, 16 * NUM_SMALL)
            act.activation(decay[:], decay[:], ACT.Exp).then_inc(decay_exp, 1)

            def copy_xz(q, j):
                task = ("xz", q, j)
                wait_full(act, task)
                if j < G:
                    if q >= 1:
                        act.wait_ge(conv_done, G * (q - 1) + j + 1)
                    act.copy(xpad[:, j, :, TAPS - 1:],
                             misc_bank(task)[:, 0:QT].rearrange("p (s t) -> p s t", s=QS)).then_inc(xs_copied, 1)
                    if q >= 2:
                        act.wait_ge(y_taken, G * (q - 1))
                    free_bank(act.activation(u[:, q % 2, j], misc_bank(task)[:, 0:QT], ACT.Identity,
                                             scale=conv_w[:, j, TAPS - 1:TAPS], bias=conv_b[:, j:j + 1]), task)
                else:
                    if q >= 2 and j == G:
                        act.wait_ge(yz_ready, q - 1)
                    free_bank(act.copy(zs[:, q % 2, j - G], misc_bank(task)[:, 0:QT]), task)

            def silu_u(q):
                act.wait_ge(conv_done, G * (q + 1))
                act.activation(u[:, q % 2], u[:, q % 2], ACT.Silu).then_inc(u_ready, 1)

            def silu_z(q):
                for j in (2 * G - 2, 2 * G - 1):
                    last = number[("xz", q, j)]
                    act.wait_ge(misc_free[last % 2], last // 2 + 1)
                act.activation(zs[:, q % 2], zs[:, q % 2], ACT.Silu).then_inc(zs_ready, 1)

            def exp_table():
                act.preload_act_table_set("natural_log_exp_and_others")

            def split_bc(q):
                task = ("bcdt", q)
                wait_full(act, task)
                act.copy(bcs[RANK:, q % 2], misc_bank(task)[RANK:, 0:QT]).then_inc(bc_high, 1)
                act.copy(dtT[0:RANK, :], misc_bank(task)[0:RANK, 0:QT]).then_inc(dt_ready, 1)

            def copy_v(q, g):
                task = ("delta", q, g)
                wait_full(act, task)
                free_bank(act.activation(delta[:, q % 2, g], misc_bank(task)[:, 0:QT], ACT.Identity,
                                         bias=b_dt[:, g:g + 1]), task)

            def softplus_abs(q):
                for g in range(2):
                    last = number[("delta", q, G - 1 - g)]
                    act.wait_ge(misc_free[last % 2], last // 2 + 1)
                if q >= 1:
                    act.wait_ge(delta_ready, q)
                act.activation(tmp[:], delta[:, q % 2], ACT.Abs).then_inc(sp_step, 1)

            def softplus_exp(q):
                act.wait_ge(sp_step, 2 * q + 1)
                act.activation(tmp[:], tmp[:], ACT.Exp, scale=-1.0).then_inc(sp_step, 1)

            def softplus_log(q):
                act.wait_ge(sp_step, 2 * q + 2)
                act.activation(logs[:], tmp[:], ACT.Ln, bias=1.0).then_inc(log_ready, 1)

            def inverse_deviation(q):
                act.wait_ge(mv_ready, QS * (q + 1))
                if q >= 1:
                    act.wait_ge(x1_ready, QS * q)
                act.activation(lnv[:], mv[:, :, 1], ACT.Ln, bias=eps[0:STEPS, :]).then_inc(ln_ready, 1)
                act.wait_ge(ln_ready, q + 1)
                act.activation(rstd[:], lnv[:], ACT.Exp, scale=-0.5).then_inc(rstd_ready, 1)

            def copy_q(q):
                for o in range(DC):
                    task = ("q", q, o)
                    wait_full(act, task)
                    if q >= 1 and o == 0:
                        act.wait_ge(q_stored, 32 * q)
                    act.activation(q_sb[:, 0, o], misc_bank(task)[:, 0:QT], ACT.Identity, bias=bq[:, o:o + 1]
                                   ).then_inc(q_high, 1)

            def copy_b(U):
                act.wait_ge(b_full, U + 1)
                if U >= 3:
                    act.wait_ge(dbu_ready, U - 2)
                act.copy(Bs[:, U % 3], b_ps[:, 0:QT]).then_inc(b_copied, 1)

            def copy_c(U):
                act.wait_ge(c_full, U + 1)
                if U >= 3:
                    act.wait_ge(hc_done, U - 2)
                act.copy(Cs[:, U % 3], c_ps[:, 0:QT]).then_inc(c_copied, 1)

            def exps(U):
                q, n = divmod(U, STATES)
                if n == 0:
                    act.wait_ge(delta_ready, q + 1)
                if U >= DA_RING:
                    act.wait_ge(scan_done, U - DA_RING + 1)
                for g in range(G):
                    ins = act.activation(dA[:, U % DA_RING, g, :, 1:],
                                         delta[:, q % 2, g].rearrange("p (s t) -> p s t", s=QS)[:, :, 1:],
                                         ACT.Exp, scale=decay[:, g, n:n + 1])
                ins.then_inc(dA_ready, 1)

            act.wait_ge(consts, 6)
            for j in range(G):
                copy_xz(0, j)
            silu_u(0)
            exp_table()
            split_bc(0)
            for g in range(G):
                copy_v(0, g)
            softplus_abs(0)
            softplus_exp(0)
            softplus_log(0)
            act.wait_ge(decay_ready, 1)
            for U in range(2):
                copy_b(U)
                copy_c(U)
                exps(U)
            copy_b(2)
            for q in range(QUADS + 1):
                for n in range(STATES):
                    if q == QUADS and n > 9:
                        break
                    U = q * STATES + n
                    if U + 2 < UNITS:
                        exps(U + 2)
                    if U + 3 < UNITS:
                        copy_b(U + 3)
                    if U + 2 < UNITS:
                        copy_c(U + 2)
                    if q >= 1:
                        if n == 5:
                            inverse_deviation(q - 1)
                        if n == 8:
                            copy_q(q - 1)
                    for task in slots.get((q, n), ()):
                        if task[0] == "xz":
                            copy_xz(*task[1:])
                        if task[0] == "delta":
                            copy_v(*task[1:])
                    if n == 4 and q < QUADS:
                        if q + 1 < QUADS:
                            silu_u(q + 1)
                        silu_z(q)
                        exp_table()
                    if q + 1 < QUADS:
                        if n == 5:
                            split_bc(q + 1)
                        if n == 7:
                            softplus_abs(q + 1)
                            softplus_exp(q + 1)
                        if n == 8:
                            softplus_log(q + 1)

        @block.vector
        def _(dve):
            dve.wait_ge(lora_loaded, 16 * 6)
            dve.scalar_tensor_tensor(out=lora_b, in0=lora_b, scalar=LORA_SCALING, in1=lora_m,
                                     op0=ALU.mult, op1=ALU.mult).then_inc(lora_scaled, 1)
            dve.wait_ge(zeroed, 2)
            for part in range(2):
                r = RANK + 2 * STATES * part
                dve.tensor_copy(sel[r:r + 2 * STATES, :], ident[r:r + 2 * STATES, r:r + 2 * STATES]).then_inc(consts, 1)
            dve.wait_ge(w_in_loaded, 16)

            def fold(i):
                w = folds[i][0]
                dve.wait_ge(fold_full, i + 1)
                dve.tensor_tensor(w, w, y_ps[i % G][:, 0:w.shape[-1]], ALU.add).then_inc(w_folded, 1)

            for i in range(2 * DC):
                fold(i)
            dve.wait_ge(decay_exp, 1)
            dve.tensor_scalar(decay[:], decay[:], -1.0, None, ALU.mult).then_inc(decay_ready, 1)

            def conv(q, g):
                last = number[("xz", q, g)]
                dve.wait_ge(misc_free[last % 2], last // 2 + 1)
                out = u[:, q % 2, g].rearrange("p (s t) -> p s t", s=QS)
                step = (TAPS - 2) * (G * q + g)
                for k in range(TAPS - 1):
                    if k:
                        dve.wait_ge(conv_step, step + k)
                    ins = dve.scalar_tensor_tensor(out=out, in0=xpad[:, g, :, k:k + STEPS],
                                                   scalar=conv_w[:, g, k:k + 1], in1=out,
                                                   op0=ALU.mult, op1=ALU.add)
                    ins.then_inc(conv_step if k < TAPS - 2 else conv_done, 1)

            def low_bc(q):
                task = ("bcdt", q)
                dve.wait_ge(bc_high, q + 1)
                dve.wait_ge(dt_ready, q + 1)
                rows = slice(RANK + 2 * STATES, P)
                ins = dve.tensor_tensor(bcs[rows, q % 2], misc_bank(task)[rows, 0:QT],
                                        bcs[rows, q % 2].bitcast(F32), ALU.subtract)
                free_bank(ins, task)

            def softplus(q, parts):
                series = du[:, q % 2]
                steps = len(SERIES) + 1
                for k in parts:
                    if k == 0:
                        dve.wait_ge(sp_step, 2 * q + 2)
                        dve.tensor_scalar(small[:], tmp[:], SERIES_BELOW, None, ALU.is_lt).then_inc(series_step, 1)
                        dve.tensor_scalar(series, tmp[:], SERIES[0], None, ALU.mult).then_inc(series_step, 1)
                    elif k < len(SERIES):
                        dve.wait_ge(series_step, steps * q + k + 1)
                        dve.scalar_tensor_tensor(out=series, in0=series, scalar=SERIES[k], in1=tmp[:],
                                                 op0=ALU.add, op1=ALU.mult).then_inc(series_step, 1)
                    elif k == len(SERIES):
                        dve.wait_ge(series_step, steps * (q + 1))
                        dve.wait_ge(log_ready, q + 1)
                        dve.copy_predicated(logs[:], small[:], series).then_inc(log_patched, 1)
                    else:
                        dve.wait_ge(log_patched, q + 1)
                        dve.scalar_tensor_tensor(out=delta[:, q % 2], in0=delta[:, q % 2], scalar=0.0, in1=logs[:],
                                                 op0=ALU.max, op1=ALU.add).then_inc(delta_ready, 1)

            def scan(U):
                dve.wait_ge(dA_ready, U + 1)
                dve.wait_ge(dbu_ready, U + 1)
                flat = hb[:, U % HB_RING].rearrange("p g t -> p (g t)")
                dve.tensor_tensor_scan(flat, dA[:, U % DA_RING].rearrange("p g s t -> p (g s t)"), flat, 0.0,
                                       ALU.mult, ALU.add).then_inc(scan_done, 1)

            def times_c(U):
                dve.wait_ge(scan_done, U + 1)
                dve.wait_ge(c_copied, U + 1)
                dve.tensor_tensor(hb[:, U % HB_RING], hb[:, U % HB_RING],
                                  Cs[:, U % 3].unsqueeze(1).to_broadcast([P, G, QT]), ALU.mult).then_inc(hc_done, 1)

            def take_y(q):
                dve.wait_ge(added, STATES * (q + 1))
                if q >= 1:
                    dve.wait_ge(misc_full, number[("proj", q - 1, QS - 1)] + 1)
                for g in range(G):
                    ins = dve.scalar_tensor_tensor(out=yz[:, g], in0=u[:, q % 2, g], scalar=skip[:, g:g + 1],
                                                   in1=y_ps[g][:, 0:QT], op0=ALU.mult, op1=ALU.add)
                    ins.then_inc(y_taken, 1)
                dve.wait_ge(y_taken, G * (q + 1))
                dve.wait_ge(zs_ready, q + 1)
                dve.tensor_tensor(yz[:], yz[:], zs[:, q % 2], ALU.mult).then_inc(yz_ready, 1)

            def residual(q, part):
                dve.wait_ge(xrow_loaded, 16 * (q + 1))
                for s in range(2 * part, 2 * part + 2):
                    task = ("proj", q, s)
                    wait_full(dve, task)
                    ins = dve.tensor_tensor(xrow[:, s], misc_bank(task)[0:STEPS, 0:D], xrow[:, s],
                                            ALU.add)
                    free_bank(ins, task)
                for s in range(2 * part, 2 * part + 2):
                    last = number[("proj", q, s)]
                    dve.wait_ge(misc_free[last % 2], last // 2 + 1)
                    dve.bn_stats(stat[:, s], xrow[:, s]).then_inc(stat_ready, 1)
                for s in range(2 * part, 2 * part + 2):
                    dve.wait_ge(stat_ready, QS * q + s + 1)
                    dve.bn_aggr(mv[:, s], stat[:, s]).then_inc(mv_ready, 1)

            def normalise(q):
                dve.wait_ge(rstd_ready, q + 1)
                for s in range(QS):
                    dve.tensor_scalar(x1[:, QS * q + s], xrow[:, s], mv[:, s, 0:1], rstd[:, s:s + 1],
                                      ALU.subtract, ALU.mult).then_inc(x1_ready, 1)

            def copy_x1T(q):
                for c in range(DC):
                    task = ("x1T", q, c)
                    wait_full(dve, task)
                    free_bank(dve.tensor_copy(x1T[:, c], misc_bank(task)[:, 0:QT]), task)

            convs = {1: (0,), 2: (1, 2), 3: (3,)}
            softplus_parts = {8: (0,), 9: (1,), 10: (2, 3), 11: (4,), 12: (5,)}
            def low_q(q):
                for o in range(DC):
                    task = ("q", q, o)
                    dve.wait_ge(q_high, DC * q + o + 1)
                    ins = dve.scalar_tensor_tensor(out=q_sb[:, 1, o], in0=misc_bank(task)[:, 0:QT],
                                                   scalar=bq[:, o:o + 1], in1=q_sb[:, 0, o].bitcast(F32),
                                                   op0=ALU.add, op1=ALU.subtract)
                    free_bank(ins, task)

            for g in range(G):
                conv(0, g)
            low_bc(0)
            dve.wait_ge(w_loaded, 16 * NUM_W)
            for i in range(2 * DC, len(folds)):
                fold(i)
            dve.tensor_scalar(bq[:], bq[:], 0.25, None, ALU.mult).then_inc(q_scaled, 1)
            dve.tensor_scalar(wq[:], wq[:], 0.25, None, ALU.mult).then_inc(q_scaled, 1)
            softplus(0, range(len(SERIES) + 2))
            scan(0)
            for q in range(QUADS + 1):
                for n in range(STATES):
                    if q == QUADS and n > 9:
                        break
                    U = q * STATES + n
                    if U + 1 < UNITS:
                        scan(U + 1)
                    if U < UNITS:
                        times_c(U)
                    if q >= 1:
                        if n == 0:
                            take_y(q - 1)
                        if n in (3, 4):
                            residual(q - 1, n - 3)
                        if n == 6:
                            normalise(q - 1)
                        if n == 7:
                            copy_x1T(q - 1)
                    if q + 1 < QUADS:
                        for g in convs.get(n, ()):
                            conv(q + 1, g)
                        if n == 5:
                            low_bc(q + 1)
                        softplus(q + 1, softplus_parts.get(n, ()))
                    if q >= 1 and n == 8:
                        low_q(q - 1)

        @block.tensor
        def _(pe):
            pe.wait_ge(lora_scaled, 1)

            def fold(i):
                w, left, right = folds[i]
                if i >= G:
                    pe.wait_ge(w_folded, i - G + 1)
                pe.matmul(y_ps[i % G][:, 0:w.shape[-1]], left, right, start=True, stop=True).then_inc(fold_full, 1)

            for i in range(2 * DC):
                fold(i)

            def run(task):
                name, q = task[0], task[1]
                m = number[task]
                if m >= 2:
                    pe.wait_ge(misc_free[m % 2], m // 2)
                bank = misc_bank(task)
                if name == "xz":
                    j = task[2]
                    if j == 0:
                        pe.wait_ge(xT_loaded[q % 2], 16 * (q // 2 + 1))
                    if q == 0:
                        pe.wait_ge(w_folded, DC * (1 + j // G))
                    for c in range(DC):
                        ins = pe.matmul(bank[:, 0:QT], w_in[:, c, j * P:(j + 1) * P], xT[:, q % 2, c],
                                        start=(c == 0), stop=(c == DC - 1))
                elif name == "bcdt":
                    pe.wait_ge(u_ready, q + 1)
                    for g in range(G):
                        ins = pe.matmul(bank[:, 0:QT], w_x[:, g], u[:, q % 2, g],
                                        start=(g == 0), stop=(g == G - 1))
                elif name == "delta":
                    pe.wait_ge(dt_ready, q + 1)
                    g = task[2]
                    ins = pe.matmul(bank[:, 0:QT], w_dt[:, g * P:(g + 1) * P], dtT[:], start=True, stop=True)
                elif name == "proj":
                    pe.wait_ge(yz_ready, q + 1)
                    s = task[2]
                    for g in range(G):
                        ins = pe.matmul(bank[0:STEPS, 0:D], yz[:, g, s * STEPS:(s + 1) * STEPS], w_out[:, g],
                                        start=(g == 0), stop=(g == G - 1))
                elif name == "x1T":
                    c = task[2]
                    pe.wait_ge(x1_ready, QS * (q + 1))
                    for s in range(QS):
                        ins = pe.transpose(bank[:, s * STEPS:(s + 1) * STEPS], x1[:, QS * q + s, c * P:(c + 1) * P],
                                           ident[0:STEPS, 0:STEPS])
                elif name == "q":
                    for c in range(DC):
                        last = number[("x1T", q, c)]
                        pe.wait_ge(misc_free[last % 2], last // 2 + 1)
                    pe.wait_ge(q_scaled, 2)
                    o = task[2]
                    for c in range(DC):
                        ins = pe.matmul(bank[:, 0:QT], wq[:, c, o * P:(o + 1) * P], x1T[:, c],
                                        start=(c == 0), stop=(c == DC - 1))
                ins.then_inc(misc_full, 1)

            def spread(U, bank, row, full):
                q = U // STATES
                if U % STATES == 0:
                    last = number[("bcdt", q)]
                    pe.wait_ge(misc_free[last % 2], last // 2 + 1)
                n = row + U % STATES
                pe.matmul(bank[:, 0:QT], sel[RANK:, n:n + 1].to_broadcast([P - RANK, P]), bcs[RANK:, q % 2],
                          start=True, stop=True).then_inc(full, 1)

            def spread_b(U):
                if U >= 1:
                    pe.wait_ge(b_copied, U)
                spread(U, b_ps, 0, b_full)

            def spread_c(U):
                if U >= 1:
                    pe.wait_ge(c_copied, U)
                spread(U, c_ps, STATES, c_full)

            pe.wait_ge(consts, 8)
            for task in slots[(-1, 0)]:
                run(task)
            for i in range(2 * DC, len(folds)):
                fold(i)
            for U in range(2):
                spread_b(U)
                spread_c(U)
            spread_b(2)
            for q in range(QUADS + 1):
                for n in range(STATES):
                    U = q * STATES + n
                    if U + 3 < UNITS:
                        spread_b(U + 3)
                    if U + 2 < UNITS:
                        spread_c(U + 2)
                    for task in slots.get((q, n), ()):
                        run(task)
                    if U < UNITS:
                        pe.wait_ge(hc_done, U + 1)
                        if U == 0:
                            pe.wait_ge(w_folded, len(folds))
                        for g in range(G):
                            if n == 0 and q >= 1:
                                pe.wait_ge(y_taken, G * (q - 1) + g + 1)
                            ins = pe.matmul(y_ps[g][:, 0:QT], ident[:], hb[:, U % HB_RING, g],
                                            start=(n == 0), stop=(n == STATES - 1))
                        ins.then_inc(added, 1)


HEADS = 16
HD = D // HEADS
KEYS = 361
KEYS_EVEN = KEYS + KEYS % 2
KCH = [(0, 128), (128, 128), (256, KEYS - 256)]
PAIR = 2 * HD
PAIRS = D // PAIR
HG = 4
SPS = HEADS // HG
MASKED = -1e9


def wait(eng, semaphore, value):
    if not isinstance(value, int) or value > 0:
        eng.wait_ge(semaphore, value)


def stage_b(pr, x1, q_parts, q_stored, k_parts, ident, lg, w1, w1_loaded):
    nc, dram = pr.nc, pr.dram
    with ExitStack() as ctx:
        def sb(*a):
            return pr.sb(ctx, *a)

        def sem(name):
            return pr.sem(ctx, name)

        wk = sb("wk", [P, DC, D])
        wv = sb("wv", [P, DC, D])
        wo = sb("wo", [P, HG, D])
        bk = sb("bk", [P, DC])
        bv = sb("bv", [P, D])
        bo = sb("bo", [P, D])
        wg = sb("wg", [P, DC, 8])
        mask = sb("mask", [STEPS, KEYS])
        head_rows = sb("head_rows", [P, PAIR // HD])
        eps = sb("eps_b", [P, 1])
        ctxT = sb("ctxT", [P, 2, DC, KEYS])
        k_sb = sb("k_sb", [P, 2, DC, KEYS], F32R)
        k4 = sb("k4", [P, 2, PAIRS, KEYS_EVEN], F32R)
        q4 = sb("q4", [P, PAIRS, STEPS], F32R)
        v = sb("v", [P, 2, len(KCH), D + HD])
        qm = sb("qm", [P, 2, HEADS, STEPS], F32R)
        prob = sb("prob", [STEPS, 2, HG, KEYS])
        pT = sb("pT", [P, 2, len(KCH), HG * STEPS])
        mx = sb("mx", [STEPS, 2, HG])
        nmx = sb("nmx", [STEPS, 2, HG])
        rsum = sb("rsum", [STEPS, 2, HEADS])
        inv = sb("inv", [STEPS, HEADS])
        inv_wide = sb("inv_wide", [STEPS, HEADS, 32])
        inv_sb = sb("inv_sb", [P, HG * STEPS])
        oT = sb("oT", [P, HG, STEPS])
        x1b = sb("x1b", [STEPS, D])
        res = sb("res", [STEPS, D])
        stat = sb("stat_b", [STEPS, 6])
        mv = sb("mv_b", [STEPS, 2])
        lnv = sb("lnv_b", [STEPS, 1])
        rstd = sb("rstd_b", [STEPS, 1])
        x2 = sb("x2_b", [STEPS, D])
        x2T = sb("x2T_b", [P, DC, STEPS])

        s_ps = [pr.psum(ctx, f"s_ps{i}", [P, 512]) for i in range(2)]
        t_ps = [pr.psum(ctx, f"t_ps{i}", [P, 512]) for i in range(3)]
        o_ps = pr.psum(ctx, "o_ps", [P, 512])
        misc = [pr.psum(ctx, f"misc_b{i}", [P, 512]) for i in range(2)]

        w_loaded, wo_zero, consts = sem("wb_loaded"), sem("wo_zero"), sem("consts_b")
        mask_ready = sem("mask_ready")
        ctx_loaded = [sem(f"ctx_loaded{i}") for i in range(2)]
        k_high, k_stored = sem("k_high"), sem("k_stored")
        k_loaded = [sem(f"k_loaded{i}") for i in range(2)]
        q_loaded, qm_ready = sem("q_loaded"), sem("qm_ready")
        misc_full = sem("misc_b_full")
        misc_free = [sem(f"misc_b_free{i}") for i in range(2)]
        s_full, s_taken, nmx_ready, p_ready = sem("s_full"), sem("s_taken"), sem("nmx_ready"), sem("p_ready")
        t_full, pt_vector, pt_scalar, pv_done = sem("t_full"), sem("pt_vector"), sem("pt_scalar"), sem("pv_done")
        inv_ready, wide_ready, o_ready = sem("inv_ready"), sem("wide_ready"), sem("o_ready")
        x1b_ready, stat_ready, mv_ready = sem("x1b_ready"), sem("stat_b_ready"), sem("mv_b_ready")
        ln_ready, rstd_ready, x2_ready, x2_kept = (
            sem("ln_b_ready"), sem("rstd_b_ready"), sem("x2_ready"), sem("x2_kept"))

        ORDER = ["R", "K0", "K1", "proj", "V0", "V1", "V2", "xT", "lg"]
        FIRST = ["K0", "K1", "V0", "V1", "V2"]
        LAST = ["R", "proj", "xT", "lg"]
        SHIFT = 2 * len(FIRST) - len(ORDER)

        class Seq:

            def __init__(self, it, s):
                self.it, self.s = it, s

            def count(self, per_seq, more=0):
                return self.it * (2 * per_seq) + (self.s * per_seq + more)

            def use(self, name):
                b = 2 * self.it + self.s if isinstance(self.it, int) else None
                if b is not None and (b <= 0 or b == SEQS):
                    m = (len(FIRST) * (b + 1) + FIRST.index(name) if b <= 0 else
                         SEQS * len(ORDER) + SHIFT + LAST.index(name))
                    return m, m % 2, m // 2
                n = self.s * len(ORDER) + SHIFT + ORDER.index(name)
                return self.it * (2 * len(ORDER)) + n, n % 2, self.it * len(ORDER) + n // 2

            def bank(self, name):
                return misc[self.use(name)[1]]

            def wait_full(self, eng, name):
                eng.wait_ge(misc_full, self.use(name)[0] + 1)

            def free(self, ins, name):
                return ins.then_inc(misc_free[self.use(name)[1]], 1)

            def wait_freed(self, eng, name):
                _, i, before = self.use(name)
                eng.wait_ge(misc_free[i], before + 1)

        def sequences(eng, lead, body, tail):
            lead(Seq(0, -1))
            for s in range(2):
                body(Seq(0, s), s)
            with eng.Fori(1, SEQS // 2) as it:
                for s in range(2):
                    body(Seq(it, s), s)
            tail(Seq(SEQS // 2, 0))

        def first(seq):
            return isinstance(seq.it, int) and 2 * seq.it + seq.s == 0

        def alone(eng):
            eng.sem_inc(met[eng.engine], 1)

        STORES = DC * 2 * 16
        SPREADS = DC * 4 * 16

        def half_spreads(seq):
            return seq.it * SPREADS + SPREADS * ((seq.s + 1) // 2 + 1)

        NUM_W = 12
        met = {e.engine: sem(f"waits_met_{i}") for i, e in enumerate((nc.vector, nc.gpsimd, nc.sync))}
        block = ctx.enter_context(nc.Block())

        @block.sync
        def _(sp):
            def load(q, s):
                sp.dma_start(ctxT[:, s], dram["ctxT"][q].rearrange("(c p) t -> p c t", p=P)).then_inc(ctx_loaded[s], 16)

            load(0, 0)
            sp.dma_start(wk[:], dram["L0_xattn_wk"].rearrange("(c p) n -> p c n", p=P)).then_inc(w_loaded, 16)
            sp.dma_start(wv[:], dram["L0_xattn_wv"].rearrange("(c p) n -> p c n", p=P)).then_inc(w_loaded, 16)
            sp.dma_start(bk[:], dram["bk"]).then_inc(w_loaded, 16)
            for row, name in ((bv, "L0_xattn_bv"), (bo, "L0_xattn_bo")):
                sp.dma_start(row[:], dram[name].rearrange("(a n) -> a n", a=1).partition_broadcast(P)
                             ).then_inc(w_loaded, 16)
            sp.dma_start(mask[:], dram["mask_1x1xSxS2_fk1"].rearrange("a b q k -> (a b q) k")).then_inc(w_loaded, 16)
            sp.dma_start(wg[:], dram["L0_ffn_Wg"].rearrange("(c p) n -> p c n", p=P)).then_inc(w_loaded, 16)
            sp.dma_start(head_rows[:], dram["head_rows"]).then_inc(w_loaded, 16)
            sp.wait_ge(consts, 1)
            for h in range(HG):
                sp.dma_start(wo[32 * h:32 * h + HD], dram["L0_xattn_wo"].rearrange("(j h r) n -> h r j n", h=HG, r=HD)[h]
                             ).then_inc(w_loaded, 16)
            load(1, 1)
            for e in range(EXPERTS):
                sp.dma_start(w1[:, e], dram["L0_ffn_W1"][e].rearrange("(c p) f -> p c f", p=P)).then_inc(w1_loaded, 16)

            def load_q(seq, b):
                wait(sp, qm_ready, seq.count(1, 1))
                alone(sp)
                for m, part in enumerate((0, 0, 1, 1)):
                    sp.dma_start(q4[m * PAIR:(m + 1) * PAIR].bitcast(F32),
                                 q_parts[part, :, bass.ds(b * STEPS, STEPS)].rearrange("(t r) n -> r t n", r=PAIR)
                                 ).then_inc(q_loaded, 16)

            def spread_k(seq, s, o):
                rows, pairs = slice(o * P, (o + 1) * P), slice(o * P // PAIR, (o + 1) * P // PAIR)
                seq.wait_freed(sp, f"K{o}")
                alone(sp)
                if o == 0:
                    wait(sp, k_loaded[s], half_spreads(seq) - SPREADS)
                for part in range(2):
                    sp.dma_start(k_parts[s, part, rows], k_sb[:, part, o].bitcast(F32)).then_inc(k_stored, 16)
                sp.wait_ge(k_stored, seq.count(STORES, STORES + 32 * (o + 1)))
                alone(sp)
                if o == 0:
                    wait(sp, s_full, seq.count(HEADS))
                for m, part in enumerate((0, 1, 0, 1)):
                    sp.dma_start(k4[m * PAIR:(m + 1) * PAIR, s, pairs, 0:KEYS].bitcast(F32),
                                 k_parts[s, part, rows].rearrange("(t r) k -> r t k", r=PAIR)
                                 ).then_inc(k_loaded[s], 16)

            def lead(seq):
                load_q(seq, 0)
                for o in range(DC):
                    spread_k(seq, 0, o)

            def body(seq, s):
                sp.wait_ge(misc_full, Seq(seq.it, seq.s - 1).use("V2")[0] + 1)
                load(seq.count(1, 2) % SEQS, s)
                load_q(seq, seq.count(1, 1) % SEQS)
                for o in range(DC):
                    spread_k(seq, 1 - s, o)

            sequences(sp, lead, body, lambda seq: None)
            for s in range(2):
                sp.wait_ge(ctx_loaded[s], 16 * (SEQS // 2 + 1))
                sp.wait_ge(k_loaded[s], SPREADS * (SEQS // 2 + 1 - s))
            sp.wait_ge(q_loaded, 16 * 4 * (SEQS + 1))

        @block.gpsimd
        def _(pool):
            pool.memset(wo[:], 0.0).then_inc(consts, 1)
            pool.memset(v[:, :, :, D:], 0.0).then_inc(consts, 1)
            pool.memset(eps[:], EPS).then_inc(consts, 1)
            pool.memset(k4[:, :, :, KEYS:].bitcast(F32), 0.0).then_inc(consts, 1)
            pool.wait_ge(w_loaded, 16 * NUM_W)

            def masked_q(seq, s):
                wait(pool, s_full, seq.count(HEADS))
                pool.wait_ge(q_loaded, seq.count(16 * 4, 2 * 16 * 4))
                alone(pool)
                for i in range(PAIR // HD):
                    ins = pool.tensor_scalar(
                        qm[:, s].rearrange("p (t i) n -> p i t n", i=PAIR // HD)[:, i], q4[:].bitcast(F32),
                        head_rows[:, i:i + 1], None, ALU.mult)
                ins.then_inc(qm_ready, 1)

            def after(seq):
                pool.wait_ge(inv_ready, seq.count(1))
                wait(pool, o_ready, seq.count(1, -1))
                alone(pool)
                pool.tensor_copy(inv_wide[:], inv[:].unsqueeze(2).to_broadcast([STEPS, HEADS, 32])).then_inc(wide_ready, 1)
                wait(pool, mv_ready, seq.count(1, -1))
                pool.tensor_tensor(x1b[:], x1[:, bass.ds(seq.count(1, -1), 1), :].rearrange("p a d -> p (a d)"),
                                   bo[0:STEPS], ALU.add).then_inc(x1b_ready, 1)

            def body(seq, s):
                if not first(seq):
                    after(seq)
                masked_q(seq, 1 - s)

            sequences(pool, lambda seq: masked_q(seq, 0), body, after)

        @block.scalar
        def _(act):
            act.preload_act_table_set("natural_log_exp_and_others")
            act.wait_ge(w_loaded, 16 * NUM_W)
            act.wait_ge(consts, 3)

            def copy_k(seq, o):
                seq.wait_full(act, f"K{o}")
                if o == 0:
                    wait(act, k_stored, seq.count(STORES, STORES))
                act.activation(k_sb[:, 0, o], seq.bank(f"K{o}")[:, 0:KEYS], ACT.Identity, bias=bk[:, o:o + 1]
                               ).then_inc(k_high, 1)

            def copy_pT(seq, j):
                n, rows = len(KCH) - 1, KCH[-1][1]
                act.wait_ge(t_full, seq.count(3 * SPS, 3 * j))
                wait(act, pv_done, seq.count(SPS, j - 2))
                act.copy(pT[0:rows, (j + 1) % 2, n], t_ps[n][0:rows, 0:HG * STEPS]).then_inc(pt_scalar, 1)

            def exps(seq, s, j, with_copy):
                act.wait_ge(nmx_ready, seq.count(SPS, j + 1))
                for h in range(HG):
                    if h == HG // 2 and with_copy:
                        copy_pT(seq, j)
                    ins = act.activation(prob[:, j % 2, h], prob[:, j % 2, h], ACT.Exp, bias=nmx[:, j % 2, h:h + 1],
                                         accum_out=rsum[:, s, HG * j + h:HG * j + h + 1])
                ins.then_inc(p_ready, 1)

            def copy_inv(seq):
                seq.wait_full(act, "R")
                wait(act, o_ready, seq.count(1, -1))
                seq.free(act.copy(inv_sb[:], seq.bank("R")[:, 0:HG * STEPS]), "R")

            def deviation(seq):
                act.wait_ge(mv_ready, seq.count(1))
                act.activation(lnv[:], mv[:, 1:2], ACT.Ln, bias=eps[0:STEPS, :]).then_inc(ln_ready, 1)
                act.wait_ge(ln_ready, seq.count(1))
                act.activation(rstd[:], lnv[:], ACT.Exp, scale=-0.5).then_inc(rstd_ready, 1)

            def body(seq, s):
                before = not first(seq)
                for j in range(SPS):
                    if j == 2 and before:
                        deviation(seq)
                    exps(seq, s, j, j or before)
                    if j == 0 and before:
                        copy_inv(seq)
                    if j < DC:
                        copy_k(seq, j)

            def tail(seq):
                copy_pT(seq, 0)
                copy_inv(seq)
                deviation(seq)

            def lead(seq):
                for o in range(DC):
                    copy_k(seq, o)

            sequences(act, lead, body, tail)

        @block.vector
        def _(dve):
            dve.wait_ge(w_loaded, 16 * NUM_W)
            dve.wait_ge(consts, 3)
            dve.tensor_scalar(mask[:], mask[:], MASKED, None, ALU.mult).then_inc(mask_ready, 1)
            dve.wait_ge(mask_ready, 1)

            def copy_v(seq, s, n):
                name, rows = f"V{n}", KCH[n][1]
                seq.wait_full(dve, name)
                wait(dve, pv_done, seq.count(SPS))
                seq.free(dve.tensor_tensor(v[0:rows, s, n, 0:D], seq.bank(name)[0:rows, 0:D], bv[0:rows], ALU.add), name)

            def mask_and_max(seq, j, h):
                dve.wait_ge(s_full, seq.count(HEADS, HG * j + h + 1))
                if h == 0:
                    wait(dve, t_full, seq.count(3 * SPS, 3 * (j - 1)))
                alone(dve)
                dve.tensor_tensor_reduce(prob[:, j % 2, h], s_ps[h % 2][0:STEPS, 0:KEYS], mask[:], 1.0, -3.0e38,
                                         ALU.add, ALU.max, mx[:, j % 2, h:h + 1]).then_inc(s_taken, 1)

            def copy_pT(seq, j, n):
                dve.wait_ge(t_full, seq.count(3 * SPS, 3 * (j - 1) + n + 1))
                if n == 0:
                    wait(dve, pv_done, seq.count(SPS, j - 2))
                rows = KCH[n][1]
                dve.tensor_copy(pT[0:rows, (j + 1) % 2, n], t_ps[n][0:rows, 0:HG * STEPS]).then_inc(pt_vector, 1)

            def finish_step(seq, j, before):
                dve.wait_ge(s_taken, seq.count(HEADS, HG * (j + 1)))
                wait(dve, p_ready, seq.count(SPS, j - 1))
                dve.tensor_scalar(nmx[:, j % 2], mx[:, j % 2], -1.0, None, ALU.mult).then_inc(nmx_ready, 1)
                if j or before:
                    for n in range(2):
                        copy_pT(seq, j, n)

            def inverse_sums(seq, s):
                dve.wait_ge(p_ready, seq.count(SPS))
                wait(dve, wide_ready, seq.count(1, -1))
                dve.reciprocal(inv[:], rsum[:, s]).then_inc(inv_ready, 1)

            def normalise_o(seq):
                dve.wait_ge(pv_done, seq.count(SPS))
                seq.wait_freed(dve, "R")
                dve.tensor_tensor(oT[:].rearrange("p j t -> p (j t)"), o_ps[:, 0:HG * STEPS], inv_sb[:], ALU.mult
                                  ).then_inc(o_ready, 1)

            def residual(seq):
                seq.wait_full(dve, "proj")
                dve.wait_ge(x1b_ready, seq.count(1))
                ins = dve.tensor_tensor(res[:], seq.bank("proj")[0:STEPS, 0:D], x1b[:], ALU.add)
                seq.free(ins, "proj")
                seq.wait_freed(dve, "proj")
                dve.bn_stats(stat[:], res[:]).then_inc(stat_ready, 1)
                dve.wait_ge(stat_ready, seq.count(1))
                alone(dve)
                dve.bn_aggr(mv[:], stat[:]).then_inc(mv_ready, 1)

            def normalise(seq):
                dve.wait_ge(rstd_ready, seq.count(1))
                dve.tensor_scalar(x1[:, bass.ds(seq.count(1, -1), 1), :].rearrange("p a d -> p (a d)"), res[:],
                                  mv[:, 0:1], rstd[:], ALU.subtract, ALU.mult).then_inc(x2_kept, 1)
                dve.tensor_scalar(x2[:], res[:], mv[:, 0:1], rstd[:], ALU.subtract, ALU.mult).then_inc(x2_ready, 1)

            def copy_x2T(seq):
                seq.wait_full(dve, "xT")
                seq.free(dve.tensor_copy(x2T[:].rearrange("p c t -> p (c t)"), seq.bank("xT")[:, 0:DC * STEPS]), "xT")

            def copy_logits(seq):
                seq.wait_full(dve, "lg")
                seq.free(dve.tensor_copy(lg[:, bass.ds(seq.count(1, -1), 1), :].rearrange("p a e -> p (a e)"),
                                         seq.bank("lg")[0:STEPS, 0:8]), "lg")

            def low_k(seq, o):
                dve.wait_ge(k_high, seq.count(DC, DC + o + 1))
                ins = dve.scalar_tensor_tensor(out=k_sb[:, 1, o], in0=seq.bank(f"K{o}")[:, 0:KEYS],
                                               scalar=bk[:, o:o + 1], in1=k_sb[:, 0, o].bitcast(F32),
                                               op0=ALU.add, op1=ALU.subtract)
                seq.free(ins, f"K{o}")

            def lead(seq):
                for o in range(DC):
                    low_k(seq, o)
                for n in range(len(KCH)):
                    copy_v(seq, 0, n)

            def body(seq, s):
                before = not first(seq)
                for j in range(SPS):
                    mask_and_max(seq, j, 0)
                    mask_and_max(seq, j, 1)
                    if j == 0 and before:
                        inverse_sums(seq, 1 - s)
                    if j in (1, 2):
                        low_k(seq, j - 1)
                    if j == 2 and before:
                        residual(seq)
                    if j == 3:
                        copy_v(seq, 1 - s, 0)
                        copy_v(seq, 1 - s, 1)
                    mask_and_max(seq, j, 2)
                    mask_and_max(seq, j, 3)
                    finish_step(seq, j, before)
                    if j == 1 and before:
                        normalise_o(seq)
                    if j == 2 and before:
                        normalise(seq)
                    if j == 3:
                        copy_v(seq, 1 - s, 2)
                        if before:
                            copy_x2T(seq)
                            copy_logits(seq)

            def tail(seq):
                for n in range(2):
                    copy_pT(seq, 0, n)
                inverse_sums(seq, 1)
                normalise_o(seq)
                residual(seq)
                normalise(seq)
                copy_x2T(seq)
                copy_logits(seq)

            sequences(dve, lead, body, tail)

        @block.tensor
        def _(pe):
            pe.wait_ge(w_loaded, 16 * NUM_W)
            pe.wait_ge(consts, 4)

            def acquire(seq, name):
                _, i, before = seq.use(name)
                wait(pe, misc_free[i], before)
                return seq.bank(name)

            def keys(seq, s, o):
                if o == 0:
                    pe.wait_ge(ctx_loaded[s], half_loads(seq, s))
                bank = acquire(seq, f"K{o}")
                for c in range(DC):
                    ins = pe.matmul(bank[:, 0:KEYS], wk[:, c, o * P:(o + 1) * P], ctxT[:, s, c],
                                    start=(c == 0), stop=(c == DC - 1))
                ins.then_inc(misc_full, 1)

            def half_loads(seq, s):
                return seq.it * 16 + 16 * ((seq.s + 1) // 2 + 1)

            def values(seq, s, n):
                at, rows = KCH[n]
                bank = acquire(seq, f"V{n}")
                for c in range(DC):
                    ins = pe.matmul(bank[0:rows, 0:D], ctxT[:, s, c, at:at + rows], wv[:, c],
                                    start=(c == 0), stop=(c == DC - 1))
                ins.then_inc(misc_full, 1)

            def scores(seq, s, j, h):
                wait(pe, s_taken, seq.count(HEADS, HG * j + h - 1))
                head = HG * j + h
                pe.matmul(s_ps[h % 2][0:STEPS, 0:KEYS_EVEN], qm[:, s, head], k4[:, s, head * HD // PAIR],
                          start=True, stop=True).then_inc(s_full, 1)

            def turn(seq, j, n):
                if n == 0:
                    pe.wait_ge(p_ready, seq.count(SPS, j))
                if n < len(KCH) - 1:
                    wait(pe, pt_vector, seq.count(2 * SPS, 2 * (j - 2) + n + 1))
                else:
                    wait(pe, pt_scalar, seq.count(SPS, j - 1))
                at, rows = KCH[n]
                for h in range(HG):
                    ins = pe.transpose(t_ps[n][0:rows, h * STEPS:(h + 1) * STEPS], prob[:, (j + 1) % 2, h, at:at + rows],
                                       ident[0:STEPS, 0:STEPS])
                ins.then_inc(t_full, 1)

            def times_v(seq, s, j):
                pe.wait_ge(pt_vector, seq.count(2 * SPS, 2 * (j - 1)))
                pe.wait_ge(pt_scalar, seq.count(SPS, j - 1))
                jj = (j - 2) % SPS
                if jj == 0:
                    wait(pe, o_ready, seq.count(1))
                for h in range(HG):
                    head = HG * jj + h
                    for n, (_, rows) in enumerate(KCH):
                        ins = pe.matmul(o_ps[32 * h:32 * h + 32, jj * STEPS:(jj + 1) * STEPS],
                                        v[0:rows, s, n, head * HD:head * HD + 32],
                                        pT[0:rows, j % 2, n, h * STEPS:(h + 1) * STEPS],
                                        start=(n == 0), stop=(n == len(KCH) - 1))
                ins.then_inc(pv_done, 1)

            def spread_inv(seq):
                pe.wait_ge(wide_ready, seq.count(1))
                bank = acquire(seq, "R")
                for j in range(HG):
                    ins = pe.matmul(bank[:, j * STEPS:(j + 1) * STEPS],
                                    inv_wide[:, HG * j:HG * (j + 1)].rearrange("p h r -> p (h r)"),
                                    ident[0:STEPS, 0:STEPS], start=True, stop=True)
                ins.then_inc(misc_full, 1)

            def project(seq):
                pe.wait_ge(o_ready, seq.count(1))
                bank = acquire(seq, "proj")
                for j in range(HG):
                    ins = pe.matmul(bank[0:STEPS, 0:D], oT[:, j], wo[:, j], start=(j == 0), stop=(j == HG - 1))
                ins.then_inc(misc_full, 1)

            def turn_x2(seq):
                pe.wait_ge(x2_ready, seq.count(1))
                bank = acquire(seq, "xT")
                for c in range(DC):
                    ins = pe.transpose(bank[:, c * STEPS:(c + 1) * STEPS], x2[:, c * P:(c + 1) * P],
                                       ident[0:STEPS, 0:STEPS])
                ins.then_inc(misc_full, 1)

            def logits(seq):
                seq.wait_freed(pe, "xT")
                bank = acquire(seq, "lg")
                for c in range(DC):
                    ins = pe.matmul(bank[0:STEPS, 0:8], x2T[:, c], wg[:, c], start=(c == 0), stop=(c == DC - 1))
                ins.then_inc(misc_full, 1)

            def first_scores(seq, s):
                pe.wait_ge(k_loaded[s], half_spreads(seq))
                pe.wait_ge(qm_ready, seq.count(1, 2))
                for h in range(2):
                    scores(Seq(seq.it, seq.s + 1), s, 0, h)

            def lead(seq):
                for o in range(DC):
                    keys(seq, 0, o)
                for n in range(len(KCH)):
                    values(seq, 0, n)
                first_scores(seq, 0)

            def body(seq, s):
                before = not first(seq)
                Seq(seq.it, seq.s - 1).wait_freed(pe, "V2")
                for j in range(SPS):
                    if j >= 2:
                        times_v(seq, s, j)
                    elif before:
                        times_v(seq, 1 - s, j)
                    scores(seq, s, j, 2)
                    scores(seq, s, j, 3)
                    if j or before:
                        for n in range(len(KCH)):
                            turn(seq, j, n)
                    if j < SPS - 1:
                        scores(seq, s, j + 1, 0)
                        scores(seq, s, j + 1, 1)
                    if j == 0:
                        if before:
                            spread_inv(seq)
                        keys(seq, 1 - s, 0)
                    if j == 1:
                        keys(seq, 1 - s, 1)
                        if before:
                            project(seq)
                    if j == 2:
                        values(seq, 1 - s, 0)
                        values(seq, 1 - s, 1)
                    if j == 3:
                        values(seq, 1 - s, 2)
                        first_scores(seq, 1 - s)
                        if before:
                            turn_x2(seq)
                            logits(seq)

            def tail(seq):
                for n in range(len(KCH)):
                    turn(seq, 0, n)
                times_v(seq, 1, 0)
                times_v(seq, 1, 1)
                spread_inv(seq)
                project(seq)
                turn_x2(seq)
                logits(seq)

            sequences(pe, lead, body, tail)


EXPERTS, WIDTH = 8, 1024
FC = WIDTH // P
CAPACITY = 2 * 2 * TOKENS // EXPERTS
TILES = (2 * TOKENS + EXPERTS * (P - 1)) // P
TILES_PER_EXPERT = -(-CAPACITY // P)
SLOTS = TILES * P
TRASH = SLOTS + P
XE_ROWS = TRASH + 2 * TOKENS


def stage_c(pr, x, lg, ident, w1, w1_loaded, scratch, xe, xe_cleared, ye, out):
    nc, dram = pr.nc, pr.dram
    with ExitStack() as ctx:
        def sb(*a):
            return pr.sb(ctx, *a)

        def sem(name):
            return pr.sem(ctx, name)

        w2 = sb("w2", [P, EXPERTS, FC, D])
        b1 = sb("b1", [P, FC, EXPERTS])
        b2 = sb("b2", [P, EXPERTS, D])
        R = [STEPS, SEQS, EXPERTS]
        tri = sb("tri", [STEPS, STEPS])
        ones = sb("ones", [STEPS, STEPS])
        rev = sb("rev", [STEPS, EXPERTS])
        tile_no = sb("tile_no", [STEPS, TILES + 1])
        token_no = sb("token_no", [STEPS, 2, SEQS])
        cont = sb("cont", [STEPS, EXPERTS, SEQS])
        gates = sb("gates", R)
        work = sb("work", R)
        mask = [sb(f"mask{i}", R) for i in range(2)]
        pos_all = [sb(f"pos_all{i}", R) for i in range(2)]
        total = [sb(f"total{i}", [STEPS, EXPERTS, SEQS]) for i in range(2)]
        running = [sb(f"running{i}", [STEPS, EXPERTS, SEQS]) for i in range(2)]
        top = sb("top", [STEPS, SEQS])
        row = sb("row", [STEPS, SEQS])
        gate = [sb(f"gate{i}", [STEPS, SEQS]) for i in range(2)]
        pos = sb("pos", [STEPS, 2, SEQS])
        base_of = sb("base_of", [STEPS, 2, SEQS])
        keep = sb("keep", [STEPS, 2, SEQS])
        weight = sb("weight", [STEPS, 2, SEQS])
        count = sb("count", [STEPS, EXPERTS])
        tiles = sb("tiles", [STEPS, EXPERTS])
        tile_end = sb("tile_end", [STEPS, EXPERTS])
        base = sb("base", [STEPS, EXPERTS])
        steps7 = sb("steps7", [STEPS, EXPERTS, TILES_PER_EXPERT])
        past = sb("past", [STEPS, TILES + 1, EXPERTS])
        expert_f = sb("expert_f", [STEPS, TILES + 1])
        expert = sb("expert", [STEPS, TILES + 1], I32)
        to_slot = sb("to_slot", [STEPS, 2, SEQS], U32)
        from_slot = sb("from_slot", [STEPS, 2, SEQS], U32)
        eps = sb("eps_c", [P, 1])
        b1c = sb("b1c", [P, 2, FC])
        hT = sb("hT", [P, 2, FC, P])
        flat = scratch.rearrange("p c t -> p (c t)")
        h_sb = flat[:, 0:2 * WIDTH].rearrange("p (i f) -> p i f", i=2)
        xs = flat[:, 2 * WIDTH:2 * WIDTH + 2 * D].rearrange("p (i d) -> p i d", i=2)
        xTt = flat[:, 2 * WIDTH + 2 * D:2 * WIDTH + 4 * D].rearrange("p (i c t) -> p i c t", i=2, c=DC)
        y_sb = sb("y_sb", [P, 2, D])
        picked = hT[0:STEPS].rearrange("p i c t -> p (i c t)").rearrange("p (s k d) -> p s k d", s=4, k=2)
        NPICK = 4

        x_ps = pr.psum(ctx, "x_ps", [P, 512])
        h_ps = [pr.psum(ctx, f"h_ps{i}", [P, 512]) for i in range(2)]
        hT_ps = [pr.psum(ctx, f"hT_ps{i}", [P, 512]) for i in range(2)]
        y_ps = pr.psum(ctx, "y_ps_c", [P, 512])

        w2_loaded, b_loaded, consts = sem("w2_loaded"), sem("b_loaded"), sem("consts_c")
        route_step, logit_max, gate_exp = sem("route_step"), sem("logit_max"), sem("gate_exp")
        masks_ready, prefix_full, routed = sem("masks_ready"), sem("prefix_full"), sem("routed")
        dispatched = sem("dispatched")
        xs_loaded = [sem(f"xs_loaded{i}") for i in range(2)]
        xt_full, xt_copied = sem("xt_full"), sem("xt_copied")
        h_full, h_scalar, h_vector = sem("h_full"), sem("h_scalar"), sem("h_vector")
        ht_full, bias_ready, gelu_done = sem("ht_full"), sem("bias_ready"), sem("gelu_done")
        y_full, y_ready = sem("y_full"), sem("y_ready")
        y_stored = [sem(f"y_stored{i}") for i in range(2)]
        picked_in = [sem(f"picked_in{i}") for i in range(NPICK)]
        mix_step, mixed, stat_ready, mv_ready = sem("mix_step"), sem("mixed"), sem("stat_c_ready"), sem("mv_c_ready")
        ln_ready, rstd_ready, out_ready, stored = sem("ln_c_ready"), sem("rstd_c_ready"), sem("out_ready"), sem("stored")

        class Tile:

            def __init__(self, it, s):
                self.it, self.s = it, s

            def count(self, per_tile, more=0):
                return self.it * (2 * per_tile) + (self.s * per_tile + more)

            def at(self, before=0):
                return self.count(1, -before)

        def tile_steps(eng, body):
            for s in range(2):
                body(Tile(0, s), s, (True, s == 1, False))
            with eng.Fori(1, TILES // 2) as it:
                for s in range(2):
                    body(Tile(it, s), s, (True, True, True))
            body(Tile(TILES // 2, 0), 0, (False, True, True))
            body(Tile(TILES // 2, 1), 1, (False, False, True))

        const_count = 9

        def finish(dve, s):
            dve.wait_ge(rstd_ready, s + 1)
            dve.tensor_scalar(x[:, s], x[:, s], pos_all[0][:, s, 0:1], row[:, s:s + 1],
                              ALU.subtract, ALU.mult).then_inc(out_ready, 1)

        block = ctx.enter_context(nc.Block())

        @block.sync
        def _(sp):
            sp.dma_start(b1[:], dram["b1T"]).then_inc(b_loaded, 16)
            sp.dma_start(b2[:].rearrange("p e d -> p (e d)"), dram["L0_ffn_b2"].rearrange("(a e) d -> a (e d)", a=1)
                         .partition_broadcast(P)).then_inc(b_loaded, 16)
            for e in range(EXPERTS):
                sp.dma_start(w2[:, e], dram["L0_ffn_W2"][e].rearrange("(c p) d -> p c d", p=P)).then_inc(w2_loaded, 16)

            def load(t, s):
                sp.dma_start(xs[:, s], xe[bass.ds(t * P, P), :]).then_inc(xs_loaded[s], 16)

            sp.wait_ge(dispatched, 16 * 2 * SEQS)
            load(0, 0)

            def body(tile, s, parts):
                first, _, last = parts
                if first:
                    wait(sp, xt_full, tile.count(1))
                    load(tile.at(-1), 1 - s)
                if last:
                    sp.wait_ge(y_ready, tile.count(1, -1))
                    sp.dma_start(ye[bass.ds(tile.at(2) * P, P), :], y_sb[:, s]).then_inc(y_stored[s], 16)

            tile_steps(sp, body)
            for s in range(2):
                sp.wait_ge(y_stored[s], 16 * (TILES // 2 + 1))
            sp.wait_ge(xs_loaded[TILES % 2], 16 * (TILES // 2 + 1))
            for s in range(SEQS):
                sp.wait_ge(out_ready, s + 1)
                sp.dma_start(out[s], x[:, s]).then_inc(stored, 16)
            sp.wait_ge(stored, 16 * SEQS)

        @block.gpsimd
        def _(pool):
            def const(ins):
                const.made += 1
                ins.then_inc(consts, 1)
                pool.wait_ge(consts, const.made)

            const.made = 0
            const(pool.memset(ones[:], 1.0))
            const(pool.affine_select(out=tri[:], in_=ones[:], compare_op=ALU.is_gt, fill=0.0, base=0,
                                     pattern=[[1, STEPS]], channel_multiplier=-1))
            const(pool.iota(rev[:], pattern=[[-1, EXPERTS]], base=EXPERTS, channel_multiplier=0,
                            allow_small_or_imprecise_dtypes=True))
            const(pool.iota(tile_no[:], pattern=[[1, TILES + 1]], base=0, channel_multiplier=0,
                            allow_small_or_imprecise_dtypes=True))
            const(pool.iota(token_no[:], pattern=[[TOKENS, 2], [STEPS, SEQS]], base=TRASH, channel_multiplier=1,
                            allow_small_or_imprecise_dtypes=True))
            const(pool.iota(steps7[:], pattern=[[0, EXPERTS], [P, TILES_PER_EXPERT]], base=0, channel_multiplier=0,
                            allow_small_or_imprecise_dtypes=True))
            const(pool.memset(cont[:], 1.0))
            const(pool.memset(cont[:, :, 0:1], 0.0))
            const(pool.memset(eps[:], EPS))
            for s in range(2):
                pool.sem_inc(y_stored[s], 16)
            pool.wait_ge(xe_cleared, 16)
            pool.wait_ge(routed, 2)
            for k in range(2):
                for s in range(SEQS):
                    pool.indirect_dma_start(
                        out=xe[:], out_offset=bass.IndirectOffsetOnAxis(ap=to_slot[:, k, s:s + 1], axis=0),
                        in_=x[:, s], in_offset=None).then_inc(dispatched, 16)
            for s in range(2):
                pool.wait_ge(y_stored[s], 16 * (TILES // 2 + 1))
            for s in range(SEQS):
                if s >= NPICK:
                    pool.wait_ge(mixed, s - NPICK + 1)
                for k in range(2):
                    pool.indirect_dma_start(
                        out=picked[:, s % NPICK, k], out_offset=None, in_=ye[:],
                        in_offset=bass.IndirectOffsetOnAxis(ap=from_slot[:, k, s:s + 1], axis=0)
                    ).then_inc(picked_in[s % NPICK], 16)

        @block.scalar
        def _(act):
            act.wait_ge(logit_max, 1)
            act.activation(gates[:], gates[:], ACT.Exp).then_inc(gate_exp, 1)

            def body(tile, s, parts):
                first, middle, _ = parts
                if first:
                    act.wait_ge(h_full, tile.count(2, 1))
                    wait(act, ht_full, tile.count(1, -1))
                    act.copy(h_sb[:, s, 0:512], h_ps[0][:]).then_inc(h_scalar, 1)
                if middle:
                    act.wait_ge(ht_full, tile.count(1))
                    act.wait_ge(bias_ready, tile.count(1))
                    wait(act, y_full, tile.count(1, -2))
                    for c in range(FC):
                        ins = act.activation(hT[:, 1 - s, c], hT_ps[c // 4][:, (c % 4) * P:(c % 4 + 1) * P], ACT.Gelu,
                                             bias=b1c[:, 1 - s, c:c + 1])
                    ins.then_inc(gelu_done, 1)

            tile_steps(act, body)
            act.preload_act_table_set("natural_log_exp_and_others")
            act.wait_ge(consts, const_count)
            for s in range(SEQS):
                act.wait_ge(mv_ready, s + 1)
                act.activation(top[:, s:s + 1], pos_all[0][:, s, 1:2], ACT.Ln, bias=eps[0:STEPS, :]).then_inc(ln_ready, 1)
                act.wait_ge(ln_ready, s + 1)
                act.activation(row[:, s:s + 1], top[:, s:s + 1], ACT.Exp, scale=-0.5).then_inc(rstd_ready, 1)

        @block.vector
        def _(dve):
            done = [0]

            def link(ins):
                done[0] += 1
                ins.then_inc(route_step, 1)
                dve.wait_ge(route_step, done[0])

            def over_e(a):
                return a.unsqueeze(2).to_broadcast(R)

            def over_s(a):
                return a.unsqueeze(1).to_broadcast(R)

            def by_seq(a):
                return a.rearrange("p e s -> p s e")

            def first_hot(values, largest, onehot):
                link(dve.tensor_tensor(work[:], values[:], over_e(largest[:]), ALU.is_equal))
                link(dve.tensor_tensor(work[:], work[:], over_s(rev[:]), ALU.mult))
                link(dve.tensor_reduce(row[:], work[:], AX_X, ALU.max))
                link(dve.tensor_tensor(onehot[:], over_s(rev[:]), over_e(row[:]), ALU.is_equal))

            def pick(result, onehot, values):
                link(dve.tensor_tensor(work[:], onehot[:], values, ALU.mult))
                link(dve.tensor_reduce(result, work[:], AX_X, ALU.add))

            dve.wait_ge(consts, const_count)
            link(dve.tensor_reduce(top[:], lg[:], AX_X, ALU.max))
            dve.tensor_tensor(gates[:], lg[:], over_e(top[:]), ALU.subtract).then_inc(logit_max, 1)
            dve.wait_ge(gate_exp, 1)
            link(dve.tensor_reduce(top[:], gates[:], AX_X, ALU.add))
            link(dve.reciprocal(top[:], top[:]))
            link(dve.tensor_tensor(gates[:], gates[:], over_e(top[:]), ALU.mult))
            link(dve.tensor_reduce(gate[0][:], gates[:], AX_X, ALU.max))
            first_hot(gates, gate[0], mask[0])
            link(dve.scalar_tensor_tensor(out=lg[:], in0=mask[0][:], scalar=-3.0e38, in1=lg[:],
                                          op0=ALU.mult, op1=ALU.add))
            link(dve.tensor_reduce(top[:], lg[:], AX_X, ALU.max))
            first_hot(lg, top, mask[1])
            dve.sem_inc(masks_ready, 1)
            pick(gate[1][:], mask[1], gates[:])
            link(dve.scalar_tensor_tensor(out=top[:], in0=gate[0][:], scalar=1e-9, in1=gate[1][:],
                                          op0=ALU.add, op1=ALU.add))
            link(dve.reciprocal(top[:], top[:]))
            for k in range(2):
                link(dve.tensor_tensor(weight[:, k], gate[k][:], top[:], ALU.mult))
            dve.wait_ge(prefix_full, 1)
            for k in range(2):
                tot = h_ps[k][0:STEPS, SEQS * EXPERTS:2 * SEQS * EXPERTS].rearrange("p (s e) -> p e s", e=EXPERTS)
                link(dve.tensor_copy(total[k][:], tot))
                link(dve.tensor_tensor_scan(running[k][:].rearrange("p e s -> p (e s)"),
                                            cont[:].rearrange("p e s -> p (e s)"),
                                            total[k][:].rearrange("p e s -> p (e s)"), 0.0, ALU.mult, ALU.add))
                within = h_ps[k][0:STEPS, 0:SEQS * EXPERTS].rearrange("p (s e) -> p s e", e=EXPERTS)
                link(dve.tensor_tensor(pos_all[k][:], within, by_seq(running[k][:]), ALU.add))
                link(dve.tensor_tensor(pos_all[k][:], pos_all[k][:], by_seq(total[k][:]), ALU.subtract))
            all_first = running[0][:, :, SEQS - 1]
            link(dve.tensor_tensor(pos_all[1][:], pos_all[1][:], over_s(all_first), ALU.add))
            link(dve.tensor_tensor(count[:], all_first, running[1][:, :, SEQS - 1], ALU.add))
            link(dve.tensor_scalar(count[:], count[:], float(CAPACITY), None, ALU.min))
            link(dve.tensor_tensor(steps7[:], count[:].unsqueeze(2).to_broadcast([STEPS, EXPERTS, TILES_PER_EXPERT]),
                                   steps7[:], ALU.is_gt))
            link(dve.tensor_reduce(tiles[:], steps7[:], AX_X, ALU.add))
            link(dve.tensor_tensor_scan(tile_end[:], ones[:, 0:EXPERTS], tiles[:], 0.0, ALU.mult, ALU.add))
            link(dve.tensor_tensor(base[:], tile_end[:], tiles[:], ALU.subtract))
            link(dve.tensor_scalar(base[:], base[:], float(P), None, ALU.mult))
            for k in range(2):
                pick(pos[:, k], mask[k], pos_all[k][:])
                pick(base_of[:, k], mask[k], over_s(base[:]))
            link(dve.tensor_scalar(keep[:], pos[:], float(CAPACITY), None, ALU.is_lt))
            link(dve.tensor_tensor(weight[:], weight[:], keep[:], ALU.mult))
            link(dve.tensor_tensor(pos[:], pos[:], base_of[:], ALU.add))
            link(dve.tensor_tensor(pos[:], pos[:], token_no[:], ALU.subtract))
            link(dve.tensor_tensor(base_of[:], pos[:], keep[:], ALU.mult))
            link(dve.tensor_tensor(base_of[:], base_of[:], token_no[:], ALU.add))
            dve.tensor_copy(to_slot[:], base_of[:]).then_inc(routed, 1)
            link(dve.tensor_tensor(pos[:], pos[:], token_no[:], ALU.add))
            link(dve.tensor_tensor(pos[:], pos[:], keep[:], ALU.mult))
            dve.tensor_copy(from_slot[:], pos[:]).then_inc(routed, 1)
            shape = [STEPS, TILES + 1, EXPERTS]
            link(dve.tensor_tensor(past[:], tile_end[:].unsqueeze(1).to_broadcast(shape),
                                   tile_no[:].unsqueeze(2).to_broadcast(shape), ALU.is_le))
            link(dve.tensor_reduce(expert_f[:], past[:], AX_X, ALU.add))
            link(dve.tensor_scalar(expert_f[:], expert_f[:], float(EXPERTS - 1), None, ALU.min))
            dve.tensor_copy(expert[:], expert_f[:]).then_inc(routed, 1)
            dve.wait_ge(routed, 3)
            dve.wait_ge(b_loaded, 32)

            def copy_xT(tile, s):
                dve.wait_ge(xt_full, tile.count(1, 1))
                wait(dve, h_full, tile.count(2, -2))
                dve.tensor_copy(xTt[:, s].rearrange("p c t -> p (c t)"), x_ps[:, 0:DC * P]).then_inc(xt_copied, 1)

            copy_xT(Tile(0, 0), 0)

            def body(tile, s, parts):
                first, _, last = parts
                if first:
                    e = dve.value_load(expert[0:1, bass.ds(tile.at(), 1)], min_val=0, max_val=EXPERTS - 1)
                    wait(dve, gelu_done, tile.count(1, -1))
                    dve.tensor_copy(b1c[:, s], b1[:, :, bass.ds(e, 1)].rearrange("p c a -> p (c a)")
                                    ).then_inc(bias_ready, 1)
                    dve.wait_ge(h_full, tile.count(2, 2))
                    wait(dve, ht_full, tile.count(1, -1))
                    dve.tensor_copy(h_sb[:, s, 512:], h_ps[1][:]).then_inc(h_vector, 1)
                    copy_xT(Tile(tile.it, tile.s + 1), 1 - s)
                if last:
                    e = dve.value_load(expert[0:1, bass.ds(tile.at(2), 1)], min_val=0, max_val=EXPERTS - 1)
                    dve.wait_ge(y_full, tile.count(1, -1))
                    dve.wait_ge(y_stored[s], (tile.it + tile.s // 2) * 16)
                    dve.tensor_tensor(y_sb[:, s], y_ps[:, 0:D], b2[:, bass.ds(e, 1)].rearrange("p a d -> p (a d)"),
                                      ALU.add).then_inc(y_ready, 1)

            tile_steps(dve, body)

            for s in range(SEQS):
                dve.wait_ge(picked_in[s % NPICK], 32 * (s // NPICK + 1))
                dve.scalar_tensor_tensor(out=x[:, s], in0=picked[:, s % NPICK, 0], scalar=weight[:, 0, s:s + 1],
                                         in1=x[:, s], op0=ALU.mult, op1=ALU.add).then_inc(mix_step, 1)
                dve.wait_ge(mix_step, s + 1)
                dve.scalar_tensor_tensor(out=x[:, s], in0=picked[:, s % NPICK, 1], scalar=weight[:, 1, s:s + 1],
                                         in1=x[:, s], op0=ALU.mult, op1=ALU.add).then_inc(mixed, 1)
                dve.wait_ge(mixed, s + 1)
                dve.bn_stats(gates[:, s, 0:6], x[:, s]).then_inc(stat_ready, 1)
                dve.wait_ge(stat_ready, s + 1)
                dve.bn_aggr(pos_all[0][:, s, 0:2], gates[:, s, 0:6]).then_inc(mv_ready, 1)
                if s:
                    finish(dve, s - 1)
            finish(dve, SEQS - 1)

        @block.tensor
        def _(pe):
            pe.wait_ge(masks_ready, 1)
            for k in range(2):
                flat_mask = mask[k][:].rearrange("p s e -> p (s e)")
                pe.matmul(h_ps[k][0:STEPS, 0:SEQS * EXPERTS], tri[:], flat_mask, start=True, stop=True)
                ins = pe.matmul(h_ps[k][0:STEPS, SEQS * EXPERTS:2 * SEQS * EXPERTS], ones[:], flat_mask,
                                start=True, stop=True)
            ins.then_inc(prefix_full, 1)
            pe.wait_ge(routed, 3)
            pe.wait_ge(w1_loaded, 16 * EXPERTS)

            def turn_x(tile, s):
                pe.wait_ge(xs_loaded[s], tile.it * 16 + 16 * (tile.s // 2 + 1))
                wait(pe, xt_copied, tile.count(1))
                for c in range(DC):
                    ins = pe.transpose(x_ps[:, c * P:(c + 1) * P], xs[:, s, c * P:(c + 1) * P], ident[:])
                ins.then_inc(xt_full, 1)

            turn_x(Tile(0, 0), 0)

            def body(tile, s, parts):
                first, middle, last = parts
                if first:
                    e = pe.value_load(expert[0:1, bass.ds(tile.at(), 1)], min_val=0, max_val=EXPERTS - 1)
                    pe.wait_ge(xt_copied, tile.count(1, 1))
                    wait(pe, h_scalar, tile.count(1))
                    wait(pe, h_vector, tile.count(1))
                    for half in range(2):
                        for c in range(DC):
                            ins = pe.matmul(h_ps[half][:], xTt[:, s, c],
                                            w1[:, bass.ds(e, 1), c, half * 512:(half + 1) * 512].rearrange("p a f -> p (a f)"),
                                            start=(c == 0), stop=(c == DC - 1))
                        ins.then_inc(h_full, 1)
                    turn_x(Tile(tile.it, tile.s + 1), 1 - s)
                if middle:
                    pe.wait_ge(h_scalar, tile.count(1))
                    pe.wait_ge(h_vector, tile.count(1))
                    wait(pe, gelu_done, tile.count(1, -1))
                    for c in range(FC):
                        ins = pe.transpose(hT_ps[c // 4][:, (c % 4) * P:(c % 4 + 1) * P],
                                           h_sb[:, 1 - s, c * P:(c + 1) * P], ident[:])
                    ins.then_inc(ht_full, 1)
                if last:
                    e = pe.value_load(expert[0:1, bass.ds(tile.at(2), 1)], min_val=0, max_val=EXPERTS - 1)
                    pe.wait_ge(gelu_done, tile.count(1, -1))
                    wait(pe, y_ready, tile.count(1, -2))
                    for c in range(FC):
                        ins = pe.matmul(y_ps[:, 0:D], hT[:, s, c],
                                        w2[:, bass.ds(e, 1), c, :].rearrange("p a d -> p (a d)"),
                                        start=(c == 0), stop=(c == FC - 1))
                    ins.then_inc(y_full, 1)

            pe.wait_ge(w2_loaded, 16 * EXPERTS)
            tile_steps(pe, body)


def program(nc, dram, out):
    pr = Program(nc, dram)
    with ExitStack() as ctx:
        ident = pr.sb(ctx, "ident", [P, P])
        x1 = pr.sb(ctx, "x1", [STEPS, SEQS, D])
        lg = pr.sb(ctx, "lg", [STEPS, SEQS, EXPERTS])
        xe = nc.dram_tensor("xe", (XE_ROWS, D), F32, kind="Internal").ap()
        ye = nc.dram_tensor("ye", (SLOTS, D), F32, kind="Internal").ap()
        q_parts = nc.dram_tensor("q_parts", (2, D, TOKENS), F32, kind="Internal").ap()
        k_parts = nc.dram_tensor("k_parts", (2, 2, D, KEYS), F32, kind="Internal").ap()
        q_stored = pr.sem(ctx, "q_stored")
        xe_cleared, w1_loaded = pr.sem(ctx, "xe_cleared"), pr.sem(ctx, "w1_loaded")
        stage_a(pr, x1, q_parts, q_stored, ident, xe, xe_cleared)
        w1 = pr.sb(ctx, "w1", [P, EXPERTS, DC, WIDTH])
        stage_b(pr, x1, q_parts, q_stored, k_parts, ident, lg, w1, w1_loaded)
        scratch = pr.sb(ctx, "scratch", [P, DC, TOKENS])
        stage_c(pr, x1, lg, ident, w1, w1_loaded, scratch[:], xe, xe_cleared, ye, out)


def kernel(**inputs):
    import numpy as np
    import concourse.bacc as bacc
    from concourse.bass_utils import run_bass_kernel_spmd

    a = {k: np.asarray(v) for k, v in inputs.items()}

    def columns(v):
        return v.reshape(-1, P, *v.shape[1:]).swapaxes(0, 1)

    laid = dict(
        xT=a["x"].reshape(TOKENS, D).T,
        ctxT=a["ctx_1024"].transpose(0, 2, 1),
        w_inT=a["L0_attn_w_in"].T,
        lora_B_inT=a["L0_attn_lora_B_in"].T,
        lora_B_outT=a["L0_attn_lora_B_out"].T,
        w_xprojT=a["L0_attn_w_xproj"].T,
        w_dtT=a["L0_attn_w_dt"].T,
        w_outT=a["L0_attn_w_out"].T,
        conv_w=columns(a["L0_attn_conv_w"].reshape(INNER, TAPS)),
        conv_b=columns(a["L0_attn_conv_b"]),
        b_dt=columns(a["L0_attn_b_dt"]),
        Dp=columns(a["L0_attn_Dp"]),
        A_log=columns(a["L0_attn_A_log"]),
        bq=columns(a["L0_xattn_bq"]),
        bk=columns(a["L0_xattn_bk"]),
        head_rows=(np.arange(P)[:, None] % PAIR // HD == np.arange(PAIR // HD)).astype(np.float32),
        b1T=columns(a["L0_ffn_b1"].T),
    )
    for name in ("x", "mask_1x1xSxS2_fk1", "L0_attn_lora_A_in", "L0_attn_lora_A_out", "L0_attn_mask_in",
                 "L0_attn_mask_out", "L0_xattn_wq", "L0_xattn_wk", "L0_xattn_wv", "L0_xattn_wo",
                 "L0_xattn_bv", "L0_xattn_bo", "L0_ffn_Wg", "L0_ffn_W1", "L0_ffn_W2", "L0_ffn_b2"):
        laid[name] = a[name]
    laid = {k: np.ascontiguousarray(v) for k, v in laid.items()}
    nc = bacc.Bacc("TRN2", target_bir_lowering=False, num_devices=1)
    dram = {k: nc.dram_tensor(f"in_{k}", v.shape, mybir.dt.from_np(v.dtype), kind="ExternalInput").ap()
            for k, v in laid.items()}
    out = nc.dram_tensor("out_0", (SEQS, STEPS, D), F32, kind="ExternalOutput").ap()
    program(nc, dram, out)
    r = run_bass_kernel_spmd(nc, [{f"in_{k}": v for k, v in laid.items()}], core_ids=[0])
    return r.results[0]["out_0"]
```

```python
from contextlib import ExitStack

import concourse.bass as bass
from concourse import mybir

F32 = mybir.dt.float32
F32R = mybir.dt.float32r
I32 = mybir.dt.int32
U32 = mybir.dt.uint32
ALU = mybir.AluOpType
ACT = mybir.ActivationFunctionType
AX_X = mybir.AxisListType.X

P = 128
SEQS, STEPS, D = 16, 100, 256
TOKENS = SEQS * STEPS
DC = D // P
INNER, STATES, TAPS, RANK, LORA = 512, 16, 4, 64, 16
G = INNER // P
QS = 4
QUADS = SEQS // QS
QT = QS * STEPS
PAD = STEPS + TAPS - 1
LORA_SCALING = 2.0
EPS = 1e-5
UNITS = QUADS * STATES
HB_RING, DA_RING = 4, 3
SERIES = [(-1.0) ** (k + 1) / k for k in range(3, 0, -1)]
SERIES_BELOW = 2.0 ** -7


class Program:

    def __init__(self, nc, dram):
        self.nc, self.dram = nc, dram

    def sb(self, ctx, name, shape, dt=F32):
        return ctx.enter_context(self.nc.sbuf_tensor(name, shape, dt))

    def psum(self, ctx, name, shape, dt=F32):
        return ctx.enter_context(self.nc.psum_tensor(name, shape, dt))

    def sem(self, ctx, name):
        return ctx.enter_context(self.nc.semaphore(name))


def misc_schedule():
    slots = {}

    def put(q, n, *task):
        slots.setdefault((q, n), []).append(task)

    for j in range(G):
        put(-1, 0, "xz", 0, j)
    put(-1, 0, "bcdt", 0)
    for g in range(G):
        put(-1, 0, "delta", 0, g)
        put(0, g, "xz", 0, G + g)
    for q in range(QUADS):
        if q:
            for s in range(QS):
                put(q, 3 + s // 2, "proj", q - 1, s)
            for c in range(DC):
                put(q, 7, "x1T", q - 1, c)
            for o in range(DC):
                put(q, 8, "q", q - 1, o)
        if q + 1 < QUADS:
            for j, n in enumerate((1, 1, 2, 2, 9, 10, 11, 12)):
                put(q, n, "xz", q + 1, j)
            put(q, 5, "bcdt", q + 1)
            for g in range(G):
                put(q, 6, "delta", q + 1, g)
    order = sorted(slots)
    number, m = {}, 0
    for key in order:
        for task in slots[key]:
            number[task] = m
            m += 1
    return slots, number


def view(flat, at, *dims):
    names = "abc"[:len(dims)]
    size = 1
    for d in dims:
        size *= d
    return flat[:, at:at + size].rearrange(f"p ({' '.join(names)}) -> p {' '.join(names)}", **dict(zip(names, dims)))


class Shared:

    def __init__(self, late, early):
        self.u, self.zs, self.delta, self.du = (view(late, i * 2 * G * QT, 2, G, QT) for i in range(4))
        at = 8 * G * QT
        self.tmp = view(late, at, G, QT)
        self.w_out = view(late, at + G * QT, G, D)
        self.wq = view(late, at + G * QT + G * D, DC, D)
        self.bq = view(late, at + G * QT + G * D + DC * D, DC)
        self.last_q_sb = view(late, 2 * 2 * G * QT, 2, DC, QT).bitcast(F32R)
        self.last_x1T = view(late, 3 * 2 * G * QT, DC, QT)

        self.w_in = view(early, 0, DC, 2 * INNER)
        at = DC * 2 * INNER
        self.xT = view(early, at, 2, DC, QT)
        at += 2 * DC * QT
        self.xpad = view(early, at, G, QS * PAD).rearrange("p g (s t) -> p g s t", s=QS)
        self.wo = view(early, at, HG, D)
        sizes = (DC * D, DC * D, 2 * DC * KEYS, D, D, KEYS, DC * EXPERTS, DC, PAIR // HD)
        at = [sum(sizes[:i]) for i in range(len(sizes))]
        self.wk, self.wv = view(early, at[0], DC, D), view(early, at[1], DC, D)
        self.ctxT = view(early, at[2], 2, DC * KEYS).rearrange("p s (c k) -> p s c k", c=DC)
        self.bv, self.bo = view(early, at[3], D), view(early, at[4], D)
        self.mask = view(early, at[5], KEYS)[0:STEPS]
        self.wg, self.bk = view(early, at[6], DC, EXPERTS), view(early, at[7], DC)
        self.head_rows = view(early, at[8], PAIR // HD)


EARLY = DC * 2 * INNER + 2 * DC * QT + G * QS * PAD


class QuadEnd:

    def __init__(self, pr, ctx, tag, first, shared, x1, x1T, q_sb, q_parts, q_stored, ident, eps, uses):
        self.first, self.x1, self.x1T, self.q_sb, self.ident, self.eps, self.uses = (
            first, x1, x1T, q_sb, ident, eps, uses)
        self.yz, self.w_out, self.wq, self.bq = shared.tmp, shared.w_out, shared.wq, shared.bq
        self.q_parts, self.q_stored = q_parts, q_stored
        self.stat = pr.sb(ctx, "stat_" + tag, [STEPS, QS, 6])
        self.mv = pr.sb(ctx, "mv_" + tag, [STEPS, QS, 2])
        self.lnv = pr.sb(ctx, "lnv_" + tag, [STEPS, QS])
        self.rstd = pr.sb(ctx, "rstd_" + tag, [STEPS, QS])
        self.summed, self.stat_ready, self.mv_ready, self.ln_ready, self.rstd_ready, self.x1_ready, self.q_high = (
            pr.sem(ctx, name + "_" + tag) for name in
            ("summed", "stat_ready", "mv_ready", "ln_ready", "rstd_ready", "x1_ready", "q_high"))

    def project(self, pe, q, s):
        bank = self.uses.bank(("proj", q, s))
        for g in range(G):
            ins = pe.matmul(bank[0:STEPS, 0:D], self.yz[:, g, s * STEPS:(s + 1) * STEPS], self.w_out[:, g],
                            start=(g == 0), stop=(g == G - 1))
        return ins

    def turn_x1(self, pe, q, c):
        pe.wait_ge(self.x1_ready, QS * (q - self.first + 1))
        bank = self.uses.bank(("x1T", q, c))
        for s in range(QS):
            ins = pe.transpose(bank[:, s * STEPS:(s + 1) * STEPS], self.x1[:, QS * q + s, c * P:(c + 1) * P],
                               self.ident[0:STEPS, 0:STEPS])
        return ins

    def queries(self, pe, q, o):
        for c in range(DC):
            self.uses.wait_freed(pe, ("x1T", q, c))
        bank = self.uses.bank(("q", q, o))
        for c in range(DC):
            ins = pe.matmul(bank[:, 0:QT], self.wq[:, c, o * P:(o + 1) * P], self.x1T[:, c],
                            start=(c == 0), stop=(c == DC - 1))
        return ins

    def residual(self, dve, q, part):
        seqs = range(2 * part, 2 * part + 2)
        for s in seqs:
            task = ("proj", q, s)
            self.uses.wait_full(dve, task)
            x = self.x1[:, QS * q + s]
            self.uses.free(dve.tensor_tensor(x, self.uses.bank(task)[0:STEPS, 0:D], x, ALU.add), task)
        for s in seqs:
            self.uses.wait_freed(dve, ("proj", q, s))
            dve.bn_stats(self.stat[:, s], self.x1[:, QS * q + s]).then_inc(self.stat_ready, 1)
        for s in seqs:
            dve.wait_ge(self.stat_ready, QS * (q - self.first) + s + 1)
            dve.bn_aggr(self.mv[:, s], self.stat[:, s]).then_inc(self.mv_ready, 1)

    def normalise(self, dve, q):
        dve.wait_ge(self.rstd_ready, q - self.first + 1)
        for s in range(QS):
            x = self.x1[:, QS * q + s]
            dve.tensor_scalar(x, x, self.mv[:, s, 0:1], self.rstd[:, s:s + 1],
                              ALU.subtract, ALU.mult).then_inc(self.x1_ready, 1)

    def copy_x1T(self, dve, q):
        for c in range(DC):
            task = ("x1T", q, c)
            self.uses.wait_full(dve, task)
            self.uses.free(dve.tensor_copy(self.x1T[:, c], self.uses.bank(task)[:, 0:QT]), task)

    def low_q(self, dve, q):
        for o in range(DC):
            task = ("q", q, o)
            dve.wait_ge(self.q_high, DC * (q - self.first) + o + 1)
            ins = dve.scalar_tensor_tensor(out=self.q_sb[:, 1, o], in0=self.uses.bank(task)[:, 0:QT],
                                           scalar=self.bq[:, o:o + 1], in1=self.q_sb[:, 0, o].bitcast(F32),
                                           op0=ALU.add, op1=ALU.subtract)
            self.uses.free(ins, task)

    def inverse_deviation(self, act, q):
        k = q - self.first
        act.wait_ge(self.mv_ready, QS * (k + 1))
        if k >= 1:
            act.wait_ge(self.x1_ready, QS * k)
        act.activation(self.lnv[:], self.mv[:, :, 1], ACT.Ln, bias=self.eps[0:STEPS, :]).then_inc(self.ln_ready, 1)
        act.wait_ge(self.ln_ready, k + 1)
        act.activation(self.rstd[:], self.lnv[:], ACT.Exp, scale=-0.5).then_inc(self.rstd_ready, 1)

    def copy_q(self, act, q):
        k = q - self.first
        if k >= 1:
            act.wait_ge(self.q_stored, 32 * k)
        for o in range(DC):
            task = ("q", q, o)
            self.uses.wait_full(act, task)
            act.activation(self.q_sb[:, 0, o], self.uses.bank(task)[:, 0:QT], ACT.Identity, bias=self.bq[:, o:o + 1]
                           ).then_inc(self.q_high, 1)

    def store_q(self, sp, q):
        for o in range(DC):
            self.uses.wait_freed(sp, ("q", q, o))
        for part in range(2):
            sp.dma_start(self.q_parts[part, :, q * QT:(q + 1) * QT].rearrange("(c p) t -> p c t", p=P),
                         self.q_sb[:, part].bitcast(F32)).then_inc(self.q_stored, 16)


class Uses:

    def __init__(self, banks, full, free, number):
        self.banks, self.full, self.freed, self.number = banks, full, free, number

    def bank(self, task):
        return self.banks[self.number[task] % len(self.banks)]

    def acquire(self, pe, task):
        m = self.number[task]
        if m >= len(self.banks):
            pe.wait_ge(self.freed[m % len(self.banks)], m // len(self.banks))

    def wait_full(self, eng, task):
        eng.wait_ge(self.full, self.number[task] + 1)

    def free(self, ins, task):
        return ins.then_inc(self.freed[self.number[task] % len(self.banks)], 1)

    def wait_freed(self, eng, task):
        m = self.number[task]
        eng.wait_ge(self.freed[m % len(self.banks)], m // len(self.banks) + 1)


def stage_a(pr, x1, shared, q_parts, q_stored, ident, xe, xe_cleared, wb_loaded, ctx_loaded):
    nc, dram = pr.nc, pr.dram
    slots, number = misc_schedule()
    u, zs, delta, du, tmp = shared.u, shared.zs, shared.delta, shared.du, shared.tmp
    w_in, xT, xpad, w_out, wq, bq = shared.w_in, shared.xT, shared.xpad, shared.w_out, shared.wq, shared.bq
    with ExitStack() as ctx:
        def sb(*a):
            return pr.sb(ctx, *a)

        def sem(name):
            return pr.sem(ctx, name)

        w_x = sb("w_x", [P, G, RANK + 4 * STATES])
        w_dt = sb("w_dt", [P, INNER])
        conv_w = sb("conv_w", [P, G, TAPS])
        conv_b = sb("conv_b", [P, G])
        b_dt = sb("b_dt", [P, G])
        skip = sb("skip", [P, G])
        decay = sb("decay", [P, G, STATES])
        eps = sb("eps", [P, 1])
        q_sb = sb("q_sb", [P, 2, DC, QT], F32R)
        sel = sb("sel", [P, 2 * STATES], F32R)

        zeros = sb("zeros", [P, D])
        logs = sb("logs", [P, G, QT])
        small = sb("small", [P, G, QT], mybir.dt.uint8)
        dtT = sb("dtT", [P, QT])
        bcs = sb("bcs", [P, 2, QT], F32R)
        Bs = sb("Bs", [P, 3, QT])
        Cs = sb("Cs", [P, 3, QT])
        dA = sb("dA", [P, DA_RING, G, QS, STEPS])
        hb = sb("hb", [P, HB_RING, G, QT])
        yz, x1T = tmp, logs[:, 0:DC]

        y_ps = [pr.psum(ctx, f"y_ps{g}", [P, 512]) for g in range(G)]
        b_ps = pr.psum(ctx, "b_ps", [P, 512])
        c_ps = pr.psum(ctx, "c_ps", [P, 512])
        misc = [pr.psum(ctx, f"misc{i}", [P, 512]) for i in range(2)]

        small_loaded = sem("small_loaded")
        w_in_loaded, w_loaded, lora_loaded = sem("w_in_loaded"), sem("w_loaded"), sem("lora_loaded")
        xT_loaded = [sem(f"xT_loaded{i}") for i in range(2)]
        x_loaded, wo_zero = sem("x_loaded"), sem("wo_zero")
        consts = sem("consts")
        zeroed = sem("zeroed")
        lora_scaled, fold_full, w_folded = sem("lora_scaled"), sem("fold_full"), sem("w_folded")
        decay_exp, decay_ready = sem("decay_exp"), sem("decay_ready")
        misc_full = sem("misc_full")
        misc_free = [sem(f"misc_free{i}") for i in range(2)]
        xs_copied, z_copied, conv_step, conv_done = sem("xs_copied"), sem("z_copied"), sem("conv_step"), sem("conv_done")
        u_ready, zs_ready, dt_ready = sem("u_ready"), sem("zs_ready"), sem("dt_ready")
        bc_high, bc_ready = sem("bc_high"), sem("bc_ready")
        v_ready, sp_step, log_ready, delta_ready, du_ready = (
            sem("v_ready"), sem("sp_step"), sem("log_ready"), sem("delta_ready"), sem("du_ready"))
        series_step, log_patched = sem("series_step"), sem("log_patched")
        b_full, b_copied, c_full, c_copied = sem("b_full"), sem("b_copied"), sem("c_full"), sem("c_copied")
        dA_ready, dbu_ready, scan_done, hc_done, added = (
            sem("dA_ready"), sem("dbu_ready"), sem("scan_done"), sem("hc_done"), sem("added"))
        y_taken, yz_ready = sem("y_taken"), sem("yz_ready")
        q_scaled = sem("q_scaled")

        lora_a = hb[0:LORA, 0, 0:2, :].rearrange("p g t -> p (g t)")[:, 0:D + INNER]
        lora_b = hb[0:LORA, 1, :, :].rearrange("p g t -> p (g t)")[:, 0:2 * INNER + D]
        lora_m = hb[0:LORA, 2, :, :].rearrange("p g t -> p (g t)")[:, 0:2 * INNER + D]
        A_IN, A_OUT = lora_a[:, 0:D], lora_a[:, D:]
        B_IN, B_OUT = lora_b[:, 0:2 * INNER], lora_b[:, 2 * INNER:]
        folds = [(w_in[:, c, f * 512:(f + 1) * 512], A_IN[:, c * P:(c + 1) * P], B_IN[:, f * 512:(f + 1) * 512])
                 for f in range(2) for c in range(DC)]
        folds += [(w_out[:, g, :], A_OUT[:, g * P:(g + 1) * P], B_OUT) for g in range(G)]
        NUM_SMALL, NUM_W = 8, 3

        def gate(eng, q):
            eng.wait_ge(y_taken, G * (q + 1))
            eng.wait_ge(zs_ready, q + 1)
            eng.tensor_tensor(yz[:], yz[:], zs[:, q % 2], ALU.mult).then_inc(yz_ready, 1)

        uses = Uses(misc, misc_full, misc_free, number)
        misc_bank, wait_full, free_bank = uses.bank, uses.wait_full, uses.free
        end = QuadEnd(pr, ctx, "quad", 0, shared, x1, x1T, q_sb, q_parts, q_stored, ident, eps, uses)

        block = ctx.enter_context(nc.Block())

        @block.sync
        def _(sp):
            sp.dma_start(lora_a[:, 0:D], dram["L0_attn_lora_A_in"]).then_inc(lora_loaded, 16)
            sp.dma_start(A_OUT, dram["L0_attn_lora_A_out"]).then_inc(lora_loaded, 16)
            sp.dma_start(B_IN, dram["lora_B_inT"]).then_inc(lora_loaded, 16)
            sp.dma_start(B_OUT, dram["lora_B_outT"]).then_inc(lora_loaded, 16)
            sp.dma_start(lora_m[:, 0:2 * INNER], dram["L0_attn_mask_in"].rearrange("(a n) -> a n", a=1)
                         .partition_broadcast(LORA)).then_inc(lora_loaded, 16)
            sp.dma_start(lora_m[:, 2 * INNER:], dram["L0_attn_mask_out"].rearrange("(a n) -> a n", a=1)
                         .partition_broadcast(LORA)).then_inc(lora_loaded, 16)
            sp.dma_start(w_in[:], dram["w_inT"].rearrange("(c p) n -> p c n", p=P)).then_inc(w_in_loaded, 16)

            def load_xT(q):
                if q >= 2:
                    sp.wait_ge(misc_full, number[("xz", q - 2, 2 * G - 1)] + 1)
                sp.dma_start(xT[:, q % 2], dram["xT"][:, q * QT:(q + 1) * QT].rearrange("(c p) t -> p c t", p=P)
                             ).then_inc(xT_loaded[q % 2], 16)

            load_xT(0)
            sp.dma_start(w_out[:], dram["w_outT"].rearrange("(g p) n -> p g n", p=P)).then_inc(w_loaded, 16)
            sp.dma_start(wq[:], dram["L0_xattn_wq"].rearrange("(c p) n -> p c n", p=P)).then_inc(w_loaded, 16)
            sp.dma_start(bq[:], dram["bq"]).then_inc(w_loaded, 16)
            load_xT(1)
            sp.dma_start(x1[:], dram["x"].rearrange("s t d -> t s d")).then_inc(x_loaded, 16)
            sp.wait_ge(consts, 1)
            sp.dma_start(xe[0:SLOTS + P].rearrange("(n p) d -> p n d", p=P),
                         zeros[:].unsqueeze(1).to_broadcast([P, TILES + 1, D])).then_inc(xe_cleared, 16)
            for q in range(2, QUADS):
                load_xT(q)
                end.store_q(sp, q - 2)
            uses.wait_full(sp, ("xz", QUADS - 1, 2 * G - 1))
            load_stage_b(sp, dram, shared, wb_loaded, ctx_loaded)
            sp.wait_ge(wo_zero, 1)
            for h in range(HG):
                sp.dma_start(shared.wo[32 * h:32 * h + HD],
                             dram["L0_xattn_wo"].rearrange("(j h r) n -> h r j n", h=HG, r=HD)[h]
                             ).then_inc(wb_loaded, 16)
            end.store_q(sp, QUADS - 2)
            sp.wait_ge(q_stored, 32 * (QUADS - 1))
            sp.wait_ge(wb_loaded, 16 * NUM_WB)

        @block.gpsimd
        def _(pool):
            pool.memset(ident[:], 0.0).then_inc(zeroed, 1)
            pool.memset(zeros[:], 0.0).then_inc(consts, 1)
            pool.memset(dtT[:], 0.0).then_inc(consts, 1)
            pool.wait_ge(consts, 2)
            pool.memset(w_dt[RANK:, :], 0.0).then_inc(consts, 1)
            pool.wait_ge(consts, 3)
            pool.memset(xpad[:, :, :, 0:TAPS - 1], 0.0).then_inc(consts, 1)
            pool.memset(dA[:, :, :, :, 0:1], 0.0).then_inc(consts, 1)
            pool.memset(eps[:], EPS).then_inc(consts, 1)
            pool.wait_ge(zeroed, 1)
            pool.affine_select(out=ident[:], in_=ident[:], compare_op=ALU.not_equal, fill=1.0, base=0,
                               pattern=[[-1, P]], channel_multiplier=1).then_inc(zeroed, 1)

            def make_du(q):
                pool.wait_ge(delta_ready, q + 1)
                pool.tensor_tensor(du[:, q % 2], delta[:, q % 2], u[:, q % 2], ALU.mult).then_inc(du_ready, 1)

            pool.wait_ge(fold_full, len(folds))
            for q in range(QUADS):
                for n in range(STATES):
                    U = q * STATES + n
                    if q == QUADS - 1 and n == 0:
                        pool.wait_ge(conv_done, G * QUADS)
                        pool.memset(shared.wo, 0.0).then_inc(wo_zero, 1)
                    if n == 0:
                        pool.wait_ge(du_ready, q + 1)
                    pool.wait_ge(b_copied, U + 1)
                    if U >= HB_RING:
                        pool.wait_ge(added, U - HB_RING + 1)
                    pool.tensor_tensor(hb[:, U % HB_RING], du[:, q % 2],
                                       Bs[:, U % 3].unsqueeze(1).to_broadcast([P, G, QT]),
                                       ALU.mult).then_inc(dbu_ready, 1)
                    if n == 4 and q >= 1:
                        gate(pool, q - 1)
                    if n == STATES - 1 and q + 1 < QUADS:
                        make_du(q + 1)

        @block.scalar
        def _(act):
            act.dma_start(conv_w[:], dram["conv_w"]).then_inc(small_loaded, 16)
            act.dma_start(conv_b[:], dram["conv_b"]).then_inc(small_loaded, 16)
            act.dma_start(b_dt[:], dram["b_dt"]).then_inc(small_loaded, 16)
            act.dma_start(skip[:], dram["Dp"]).then_inc(small_loaded, 16)
            act.dma_start(decay[:], dram["A_log"]).then_inc(small_loaded, 16)
            wx = dram["w_xprojT"].rearrange("(g p) n -> p g n", p=P)
            act.dma_start(w_x[:, :, 0:RANK + 2 * STATES], wx).then_inc(small_loaded, 16)
            act.dma_start(w_x[:, :, RANK + 2 * STATES:], wx[:, :, RANK:]).then_inc(small_loaded, 16)
            act.dma_start(w_dt[0:RANK, :], dram["w_dtT"]).then_inc(small_loaded, 16)
            act.wait_ge(small_loaded, 16 * NUM_SMALL)
            act.activation(decay[:], decay[:], ACT.Exp).then_inc(decay_exp, 1)

            def copy_xz(q, j):
                task = ("xz", q, j)
                wait_full(act, task)
                if j < G:
                    if q >= 1:
                        act.wait_ge(conv_done, G * (q - 1) + j + 1)
                    act.copy(xpad[:, j, :, TAPS - 1:],
                             misc_bank(task)[:, 0:QT].rearrange("p (s t) -> p s t", s=QS)).then_inc(xs_copied, 1)
                    if q >= 2:
                        act.wait_ge(y_taken, G * (q - 1))
                    free_bank(act.activation(u[:, q % 2, j], misc_bank(task)[:, 0:QT], ACT.Identity,
                                             scale=conv_w[:, j, TAPS - 1:TAPS], bias=conv_b[:, j:j + 1]), task)
                else:
                    if q >= 2 and j == G:
                        act.wait_ge(yz_ready, q - 1)
                    free_bank(act.copy(zs[:, q % 2, j - G], misc_bank(task)[:, 0:QT]), task)

            def silu_u(q):
                act.wait_ge(conv_done, G * (q + 1))
                act.activation(u[:, q % 2], u[:, q % 2], ACT.Silu).then_inc(u_ready, 1)

            def silu_z(q):
                for j in (2 * G - 2, 2 * G - 1):
                    last = number[("xz", q, j)]
                    act.wait_ge(misc_free[last % 2], last // 2 + 1)
                act.activation(zs[:, q % 2], zs[:, q % 2], ACT.Silu).then_inc(zs_ready, 1)

            def exp_table():
                act.preload_act_table_set("natural_log_exp_and_others")

            def split_bc(q):
                task = ("bcdt", q)
                wait_full(act, task)
                act.copy(bcs[RANK:, q % 2], misc_bank(task)[RANK:, 0:QT]).then_inc(bc_high, 1)
                act.copy(dtT[0:RANK, :], misc_bank(task)[0:RANK, 0:QT]).then_inc(dt_ready, 1)

            def copy_v(q, g):
                task = ("delta", q, g)
                wait_full(act, task)
                free_bank(act.activation(delta[:, q % 2, g], misc_bank(task)[:, 0:QT], ACT.Identity,
                                         bias=b_dt[:, g:g + 1]), task)

            def softplus_abs(q):
                for g in range(2):
                    last = number[("delta", q, G - 1 - g)]
                    act.wait_ge(misc_free[last % 2], last // 2 + 1)
                if q >= 1:
                    act.wait_ge(delta_ready, q)
                act.activation(tmp[:], delta[:, q % 2], ACT.Abs).then_inc(sp_step, 1)

            def softplus_exp(q):
                act.wait_ge(sp_step, 2 * q + 1)
                act.activation(tmp[:], tmp[:], ACT.Exp, scale=-1.0).then_inc(sp_step, 1)

            def softplus_log(q):
                act.wait_ge(sp_step, 2 * q + 2)
                act.activation(logs[:], tmp[:], ACT.Ln, bias=1.0).then_inc(log_ready, 1)

            def copy_b(U):
                act.wait_ge(b_full, U + 1)
                if U >= 3:
                    act.wait_ge(dbu_ready, U - 2)
                act.copy(Bs[:, U % 3], b_ps[:, 0:QT]).then_inc(b_copied, 1)

            def copy_c(U):
                act.wait_ge(c_full, U + 1)
                if U >= 3:
                    act.wait_ge(hc_done, U - 2)
                act.copy(Cs[:, U % 3], c_ps[:, 0:QT]).then_inc(c_copied, 1)

            def exps(U):
                q, n = divmod(U, STATES)
                if n == 0:
                    act.wait_ge(delta_ready, q + 1)
                if U >= DA_RING:
                    act.wait_ge(scan_done, U - DA_RING + 1)
                for g in range(G):
                    ins = act.activation(dA[:, U % DA_RING, g, :, 1:],
                                         delta[:, q % 2, g].rearrange("p (s t) -> p s t", s=QS)[:, :, 1:],
                                         ACT.Exp, scale=decay[:, g, n:n + 1])
                ins.then_inc(dA_ready, 1)

            act.preload_act_table_set("silu_and_others")
            act.wait_ge(consts, 6)
            for j in range(G):
                copy_xz(0, j)
            for g in range(G):
                act.wait_ge(conv_done, g + 1)
                act.activation(u[:, 0, g], u[:, 0, g], ACT.Silu).then_inc(u_ready, 1)
            exp_table()
            split_bc(0)
            for g in range(G):
                copy_v(0, g)
            softplus_abs(0)
            softplus_exp(0)
            softplus_log(0)
            act.wait_ge(decay_ready, 1)
            for U in range(2):
                copy_b(U)
                copy_c(U)
                exps(U)
            copy_b(2)
            for q in range(QUADS):
                for n in range(STATES):
                    U = q * STATES + n
                    if U + 2 < UNITS:
                        exps(U + 2)
                    if U + 3 < UNITS:
                        copy_b(U + 3)
                    if U + 2 < UNITS:
                        copy_c(U + 2)
                    if q >= 1:
                        if n == 5:
                            end.inverse_deviation(act, q - 1)
                        if n == 8:
                            end.copy_q(act, q - 1)
                    for task in slots.get((q, n), ()):
                        if task[0] == "xz":
                            copy_xz(*task[1:])
                        if task[0] == "delta":
                            copy_v(*task[1:])
                    if n == 4:
                        if q + 1 < QUADS:
                            silu_u(q + 1)
                        silu_z(q)
                        exp_table()
                    if q + 1 < QUADS:
                        if n == 5:
                            split_bc(q + 1)
                        if n == 7:
                            softplus_abs(q + 1)
                            softplus_exp(q + 1)
                        if n == 8:
                            softplus_log(q + 1)

        @block.vector
        def _(dve):
            dve.wait_ge(lora_loaded, 16 * 6)
            dve.scalar_tensor_tensor(out=lora_b, in0=lora_b, scalar=LORA_SCALING, in1=lora_m,
                                     op0=ALU.mult, op1=ALU.mult).then_inc(lora_scaled, 1)
            dve.wait_ge(zeroed, 2)
            for part in range(2):
                r = RANK + 2 * STATES * part
                dve.tensor_copy(sel[r:r + 2 * STATES, :], ident[r:r + 2 * STATES, r:r + 2 * STATES]).then_inc(consts, 1)
            dve.wait_ge(w_in_loaded, 16)

            def fold(i):
                w = folds[i][0]
                dve.wait_ge(fold_full, i + 1)
                dve.tensor_tensor(w, w, y_ps[i % G][:, 0:w.shape[-1]], ALU.add).then_inc(w_folded, 1)

            for i in range(2 * DC):
                fold(i)
            dve.wait_ge(decay_exp, 1)
            dve.tensor_scalar(decay[:], decay[:], -1.0, None, ALU.mult).then_inc(decay_ready, 1)

            def conv(q, g):
                last = number[("xz", q, g)]
                dve.wait_ge(misc_free[last % 2], last // 2 + 1)
                out = u[:, q % 2, g].rearrange("p (s t) -> p s t", s=QS)
                step = (TAPS - 2) * (G * q + g)
                for k in range(TAPS - 1):
                    if k:
                        dve.wait_ge(conv_step, step + k)
                    ins = dve.scalar_tensor_tensor(out=out, in0=xpad[:, g, :, k:k + STEPS],
                                                   scalar=conv_w[:, g, k:k + 1], in1=out,
                                                   op0=ALU.mult, op1=ALU.add)
                    ins.then_inc(conv_step if k < TAPS - 2 else conv_done, 1)

            def low_bc(q):
                task = ("bcdt", q)
                dve.wait_ge(bc_high, q + 1)
                dve.wait_ge(dt_ready, q + 1)
                rows = slice(RANK + 2 * STATES, P)
                ins = dve.tensor_tensor(bcs[rows, q % 2], misc_bank(task)[rows, 0:QT],
                                        bcs[rows, q % 2].bitcast(F32), ALU.subtract)
                free_bank(ins, task)

            def softplus(q, parts):
                series = du[:, q % 2]
                steps = len(SERIES) + 1
                for k in parts:
                    if k == 0:
                        dve.wait_ge(sp_step, 2 * q + 2)
                        dve.tensor_scalar(small[:], tmp[:], SERIES_BELOW, None, ALU.is_lt).then_inc(series_step, 1)
                        dve.tensor_scalar(series, tmp[:], SERIES[0], None, ALU.mult).then_inc(series_step, 1)
                    elif k < len(SERIES):
                        dve.wait_ge(series_step, steps * q + k + 1)
                        dve.scalar_tensor_tensor(out=series, in0=series, scalar=SERIES[k], in1=tmp[:],
                                                 op0=ALU.add, op1=ALU.mult).then_inc(series_step, 1)
                    elif k == len(SERIES):
                        dve.wait_ge(series_step, steps * (q + 1))
                        dve.wait_ge(log_ready, q + 1)
                        dve.copy_predicated(logs[:], small[:], series).then_inc(log_patched, 1)
                    else:
                        dve.wait_ge(log_patched, q + 1)
                        dve.scalar_tensor_tensor(out=delta[:, q % 2], in0=delta[:, q % 2], scalar=0.0, in1=logs[:],
                                                 op0=ALU.max, op1=ALU.add).then_inc(delta_ready, 1)

            def scan(U):
                dve.wait_ge(dA_ready, U + 1)
                dve.wait_ge(dbu_ready, U + 1)
                flat = hb[:, U % HB_RING].rearrange("p g t -> p (g t)")
                dve.tensor_tensor_scan(flat, dA[:, U % DA_RING].rearrange("p g s t -> p (g s t)"), flat, 0.0,
                                       ALU.mult, ALU.add).then_inc(scan_done, 1)

            def times_c(U):
                dve.wait_ge(scan_done, U + 1)
                dve.wait_ge(c_copied, U + 1)
                dve.tensor_tensor(hb[:, U % HB_RING], hb[:, U % HB_RING],
                                  Cs[:, U % 3].unsqueeze(1).to_broadcast([P, G, QT]), ALU.mult).then_inc(hc_done, 1)

            def take_y(q):
                dve.wait_ge(added, STATES * (q + 1))
                if q >= 1:
                    dve.wait_ge(misc_full, number[("proj", q - 1, QS - 1)] + 1)
                for g in range(G):
                    ins = dve.scalar_tensor_tensor(out=yz[:, g], in0=u[:, q % 2, g], scalar=skip[:, g:g + 1],
                                                   in1=y_ps[g][:, 0:QT], op0=ALU.mult, op1=ALU.add)
                    ins.then_inc(y_taken, 1)

            convs = {1: (0,), 2: (1, 2), 3: (3,)}
            softplus_parts = {8: (0,), 9: (1,), 10: (2,), 11: (3,), 12: (4,)}

            for g in range(G):
                conv(0, g)
            low_bc(0)
            dve.wait_ge(w_loaded, 16 * NUM_W)
            for i in range(2 * DC, len(folds)):
                fold(i)
            dve.tensor_scalar(bq[:], bq[:], 0.25, None, ALU.mult).then_inc(q_scaled, 1)
            dve.tensor_scalar(wq[:], wq[:], 0.25, None, ALU.mult).then_inc(q_scaled, 1)
            softplus(0, range(len(SERIES) + 2))
            dve.wait_ge(delta_ready, 1)
            dve.tensor_tensor(du[:, 0], delta[:, 0], u[:, 0], ALU.mult).then_inc(du_ready, 1)
            scan(0)
            for q in range(QUADS):
                for n in range(STATES):
                    U = q * STATES + n
                    if U + 1 < UNITS:
                        scan(U + 1)
                    if U < UNITS:
                        times_c(U)
                    if q >= 1:
                        if n == 0:
                            take_y(q - 1)
                        if n in (3, 4):
                            if q == 1 and n == 3:
                                dve.wait_ge(x_loaded, 16)
                            end.residual(dve, q - 1, n - 3)
                        if n == 6:
                            end.normalise(dve, q - 1)
                        if n == 7:
                            end.copy_x1T(dve, q - 1)
                    if q + 1 < QUADS:
                        for g in convs.get(n, ()):
                            conv(q + 1, g)
                        if n == 5:
                            low_bc(q + 1)
                        softplus(q + 1, softplus_parts.get(n, ()))
                    if q >= 1 and n == 8:
                        end.low_q(dve, q - 1)
            take_y(QUADS - 1)
            gate(dve, QUADS - 1)

        @block.tensor
        def _(pe):
            pe.wait_ge(lora_scaled, 1)

            def fold(i):
                w, left, right = folds[i]
                if i >= G:
                    pe.wait_ge(w_folded, i - G + 1)
                pe.matmul(y_ps[i % G][:, 0:w.shape[-1]], left, right, start=True, stop=True).then_inc(fold_full, 1)

            for i in range(2 * DC):
                fold(i)

            def run(task):
                name, q = task[0], task[1]
                uses.acquire(pe, task)
                bank = misc_bank(task)
                if name == "xz":
                    j = task[2]
                    if j == 0:
                        pe.wait_ge(xT_loaded[q % 2], 16 * (q // 2 + 1))
                    if q == 0:
                        pe.wait_ge(w_folded, DC * (1 + j // G))
                    for c in range(DC):
                        ins = pe.matmul(bank[:, 0:QT], w_in[:, c, j * P:(j + 1) * P], xT[:, q % 2, c],
                                        start=(c == 0), stop=(c == DC - 1))
                elif name == "bcdt":
                    pe.wait_ge(u_ready, G + q if q else 1)
                    for g in range(G):
                        if q == 0 and g:
                            pe.wait_ge(u_ready, g + 1)
                        ins = pe.matmul(bank[:, 0:QT], w_x[:, g], u[:, q % 2, g],
                                        start=(g == 0), stop=(g == G - 1))
                elif name == "delta":
                    pe.wait_ge(dt_ready, q + 1)
                    g = task[2]
                    ins = pe.matmul(bank[:, 0:QT], w_dt[:, g * P:(g + 1) * P], dtT[:], start=True, stop=True)
                elif name == "proj":
                    pe.wait_ge(yz_ready, q + 1)
                    ins = end.project(pe, q, task[2])
                elif name == "x1T":
                    ins = end.turn_x1(pe, q, task[2])
                elif name == "q":
                    pe.wait_ge(q_scaled, 2)
                    ins = end.queries(pe, q, task[2])
                ins.then_inc(misc_full, 1)

            def spread(U, bank, row, full):
                q = U // STATES
                if U % STATES == 0:
                    last = number[("bcdt", q)]
                    pe.wait_ge(misc_free[last % 2], last // 2 + 1)
                n = row + U % STATES
                pe.matmul(bank[:, 0:QT], sel[RANK:, n:n + 1].to_broadcast([P - RANK, P]), bcs[RANK:, q % 2],
                          start=True, stop=True).then_inc(full, 1)

            def spread_b(U):
                if U >= 1:
                    pe.wait_ge(b_copied, U)
                spread(U, b_ps, 0, b_full)

            def spread_c(U):
                if U >= 1:
                    pe.wait_ge(c_copied, U)
                spread(U, c_ps, STATES, c_full)

            pe.wait_ge(consts, 8)
            for task in slots[(-1, 0)]:
                run(task)
            for i in range(2 * DC, len(folds)):
                fold(i)
            for U in range(2):
                spread_b(U)
                spread_c(U)
            spread_b(2)
            for q in range(QUADS):
                for n in range(STATES):
                    U = q * STATES + n
                    if U + 3 < UNITS:
                        spread_b(U + 3)
                    if U + 2 < UNITS:
                        spread_c(U + 2)
                    for task in slots.get((q, n), ()):
                        run(task)
                    if U < UNITS:
                        pe.wait_ge(hc_done, U + 1)
                        if U == 0:
                            pe.wait_ge(w_folded, len(folds))
                        for g in range(G):
                            if n == 0 and q >= 1:
                                pe.wait_ge(y_taken, G * (q - 1) + g + 1)
                            ins = pe.matmul(y_ps[g][:, 0:QT], ident[:], hb[:, U % HB_RING, g],
                                            start=(n == 0), stop=(n == STATES - 1))
                        ins.then_inc(added, 1)


HEADS = 16
HD = D // HEADS
KEYS = 361
KEYS_EVEN = KEYS + KEYS % 2
KCH = [(0, 128), (128, 128), (256, KEYS - 256)]
PAIR = 2 * HD
PAIRS = D // PAIR
HG = 4
SPS = HEADS // HG
MASKED = -1e9


def wait(eng, semaphore, value):
    if not isinstance(value, int) or value > 0:
        eng.wait_ge(semaphore, value)


NUM_WB = 8 + HG


def load_contexts(sp, dram, shared, ctx_loaded, b, s):
    sp.dma_start(shared.ctxT[:, s], dram["ctxT"][b].rearrange("(c p) t -> p c t", p=P)).then_inc(ctx_loaded[s], 16)


def load_stage_b(sp, dram, shared, wb_loaded, ctx_loaded):
    load_contexts(sp, dram, shared, ctx_loaded, 0, 0)
    sp.dma_start(shared.wk, dram["L0_xattn_wk"].rearrange("(c p) n -> p c n", p=P)).then_inc(wb_loaded, 16)
    sp.dma_start(shared.wv, dram["L0_xattn_wv"].rearrange("(c p) n -> p c n", p=P)).then_inc(wb_loaded, 16)
    sp.dma_start(shared.bk, dram["bk"]).then_inc(wb_loaded, 16)
    for row, name in ((shared.bv, "L0_xattn_bv"), (shared.bo, "L0_xattn_bo")):
        sp.dma_start(row, dram[name].rearrange("(a n) -> a n", a=1).partition_broadcast(P)).then_inc(wb_loaded, 16)
    sp.dma_start(shared.mask, dram["mask_1x1xSxS2_fk1"].rearrange("a b q k -> (a b q) k")).then_inc(wb_loaded, 16)
    sp.dma_start(shared.wg, dram["L0_ffn_Wg"].rearrange("(c p) n -> p c n", p=P)).then_inc(wb_loaded, 16)
    sp.dma_start(shared.head_rows, dram["head_rows"]).then_inc(wb_loaded, 16)
    load_contexts(sp, dram, shared, ctx_loaded, 1, 1)


def stage_b(pr, x1, shared, q_parts, q_stored, k_parts, ident, lg, w1, w1_loaded, w_loaded, ctx_loaded):
    nc, dram = pr.nc, pr.dram
    with ExitStack() as ctx:
        def sb(*a):
            return pr.sb(ctx, *a)

        def sem(name):
            return pr.sem(ctx, name)

        wk, wv, wo, bk, bv, bo = shared.wk, shared.wv, shared.wo, shared.bk, shared.bv, shared.bo
        wg, mask, head_rows, ctxT = shared.wg, shared.mask, shared.head_rows, shared.ctxT
        eps = sb("eps_b", [P, 1])
        k_sb = sb("k_sb", [P, 2, DC, KEYS], F32R)
        k4 = sb("k4", [P, 2, PAIRS, KEYS_EVEN], F32R)
        q4 = sb("q4", [P, PAIRS, STEPS], F32R)
        v = sb("v", [P, 2, len(KCH), D + HD])
        qm = sb("qm", [P, 2, HEADS, STEPS], F32R)
        prob = sb("prob", [STEPS, 2, HG, KEYS])
        pT = sb("pT", [P, 2, len(KCH), HG * STEPS])
        mx = sb("mx", [STEPS, 2, HG])
        nmx = sb("nmx", [STEPS, 2, HG])
        rsum = sb("rsum", [STEPS, 2, HEADS])
        inv = sb("inv", [STEPS, HEADS])
        inv_wide = sb("inv_wide", [STEPS, HEADS, 32])
        inv_sb = sb("inv_sb", [P, HG * STEPS])
        oT = sb("oT", [P, HG, STEPS])
        x1b = sb("x1b", [STEPS, D])
        res = sb("res", [STEPS, D])
        stat = sb("stat_b", [STEPS, 6])
        mv = sb("mv_b", [STEPS, 2])
        lnv = sb("lnv_b", [STEPS, 1])
        rstd = sb("rstd_b", [STEPS, 1])
        x2 = sb("x2_b", [STEPS, D])
        x2T = sb("x2T_b", [P, DC, STEPS])

        s_ps = [pr.psum(ctx, f"s_ps{i}", [P, 512]) for i in range(2)]
        t_ps = [pr.psum(ctx, f"t_ps{i}", [P, 512]) for i in range(3)]
        o_ps = pr.psum(ctx, "o_ps", [P, 512])
        misc = [pr.psum(ctx, f"misc_b{i}", [P, 512]) for i in range(2)]

        consts = sem("consts_b")
        mask_ready = sem("mask_ready")
        k_high, k_stored = sem("k_high"), sem("k_stored")
        k_loaded = [sem(f"k_loaded{i}") for i in range(2)]
        q_loaded, qm_ready = sem("q_loaded"), sem("qm_ready")
        misc_full = sem("misc_b_full")
        misc_free = [sem(f"misc_b_free{i}") for i in range(2)]
        s_full, s_taken, nmx_ready, p_ready = sem("s_full"), sem("s_taken"), sem("nmx_ready"), sem("p_ready")
        t_full, pt_vector, pt_scalar, pv_done = sem("t_full"), sem("pt_vector"), sem("pt_scalar"), sem("pv_done")
        inv_ready, wide_ready, o_ready = sem("inv_ready"), sem("wide_ready"), sem("o_ready")
        x1b_ready, stat_ready, mv_ready = sem("x1b_ready"), sem("stat_b_ready"), sem("mv_b_ready")
        ln_ready, rstd_ready, x2_ready, x2_kept = (
            sem("ln_b_ready"), sem("rstd_b_ready"), sem("x2_ready"), sem("x2_kept"))

        ORDER = ["K0", "R", "K1", "proj", "V0", "V1", "V2", "xT", "lg"]
        FIRST = ["K0", "K1", "V0", "V1", "V2"]
        LAST = ["R", "proj", "xT", "lg"]
        SHIFT = 2 * len(FIRST) - len(ORDER)

        class Seq:

            def __init__(self, it, s):
                self.it, self.s = it, s

            def count(self, per_seq, more=0):
                return self.it * (2 * per_seq) + (self.s * per_seq + more)

            def use(self, name):
                b = 2 * self.it + self.s if isinstance(self.it, int) else None
                if b is not None and (b <= 0 or b == SEQS):
                    m = (len(FIRST) * (b + 1) + FIRST.index(name) if b <= 0 else
                         SEQS * len(ORDER) + SHIFT + LAST.index(name))
                    return m, m % 2, m // 2
                n = self.s * len(ORDER) + SHIFT + ORDER.index(name)
                return self.it * (2 * len(ORDER)) + n, n % 2, self.it * len(ORDER) + n // 2

            def bank(self, name):
                return misc[self.use(name)[1]]

            def wait_full(self, eng, name):
                eng.wait_ge(misc_full, self.use(name)[0] + 1)

            def free(self, ins, name):
                return ins.then_inc(misc_free[self.use(name)[1]], 1)

            def wait_freed(self, eng, name):
                _, i, before = self.use(name)
                eng.wait_ge(misc_free[i], before + 1)

        last_tasks = ([("proj", QUADS - 1, i) for i in range(QS)] + [("x1T", QUADS - 1, c) for c in range(DC)]
                      + [("q", QUADS - 1, o) for o in range(DC)])
        last_full, last_free = sem("last_full"), [sem(f"last_free{i}") for i in range(2)]
        uses = Uses(t_ps[0:2], last_full, last_free, {task: i for i, task in enumerate(last_tasks)})
        end = QuadEnd(pr, ctx, "last", QUADS - 1, shared, x1, shared.last_x1T, shared.last_q_sb, q_parts, q_stored,
                      ident, eps, uses)

        def sequences(eng, lead, body, tail):
            lead(Seq(0, -1))
            for s in range(2):
                body(Seq(0, s), s)
            with eng.Fori(1, SEQS // 2) as it:
                for s in range(2):
                    body(Seq(it, s), s)
            tail(Seq(SEQS // 2, 0))

        def first(seq):
            return isinstance(seq.it, int) and 2 * seq.it + seq.s == 0

        def alone(eng):
            eng.sem_inc(met[eng.engine], 1)

        STORES = DC * 2 * 16
        SPREADS = DC * 4 * 16

        def half_spreads(seq):
            return seq.it * SPREADS + SPREADS * ((seq.s + 1) // 2 + 1)

        met = {e.engine: sem(f"waits_met_{i}") for i, e in enumerate((nc.vector, nc.gpsimd, nc.sync))}
        block = ctx.enter_context(nc.Block())

        @block.sync
        def _(sp):
            def load_q(seq, b):
                wait(sp, qm_ready, seq.count(1, 1))
                alone(sp)
                for m, part in enumerate((0, 0, 1, 1)):
                    sp.dma_start(q4[m * PAIR:(m + 1) * PAIR].bitcast(F32),
                                 q_parts[part, :, bass.ds(b * STEPS, STEPS)].rearrange("(t r) n -> r t n", r=PAIR)
                                 ).then_inc(q_loaded, 16)

            def spread_k(seq, s, o):
                rows, pairs = slice(o * P, (o + 1) * P), slice(o * P // PAIR, (o + 1) * P // PAIR)
                seq.wait_freed(sp, f"K{o}")
                alone(sp)
                if o == 0:
                    wait(sp, k_loaded[s], half_spreads(seq) - SPREADS)
                for part in range(2):
                    sp.dma_start(k_parts[s, part, rows], k_sb[:, part, o].bitcast(F32)).then_inc(k_stored, 16)
                sp.wait_ge(k_stored, seq.count(STORES, STORES + 32 * (o + 1)))
                alone(sp)
                if o == 0:
                    wait(sp, s_full, seq.count(HEADS))
                for m, part in enumerate((0, 1, 0, 1)):
                    sp.dma_start(k4[m * PAIR:(m + 1) * PAIR, s, pairs, 0:KEYS].bitcast(F32),
                                 k_parts[s, part, rows].rearrange("(t r) k -> r t k", r=PAIR)
                                 ).then_inc(k_loaded[s], 16)

            def lead(seq):
                load_q(seq, 0)
                for o in range(DC):
                    spread_k(seq, 0, o)
                end.store_q(sp, QUADS - 1)
                sp.wait_ge(q_stored, 32 * QUADS)

            def body(seq, s):
                sp.wait_ge(misc_full, Seq(seq.it, seq.s - 1).use("V2")[0] + 1)
                load_contexts(sp, dram, shared, ctx_loaded, seq.count(1, 2) % SEQS, s)
                load_q(seq, seq.count(1, 1) % SEQS)
                for o in range(DC):
                    spread_k(seq, 1 - s, o)
                expert = slice(seq.it, seq.it + 1) if isinstance(seq.it, int) else bass.ds(seq.it, 1)
                sp.dma_start(w1[:, expert, s], dram["L0_ffn_W1"][expert, s * P:(s + 1) * P].rearrange("e p f -> p e f")
                             ).then_inc(w1_loaded, 16)

            sequences(sp, lead, body, lambda seq: None)
            for s in range(2):
                sp.wait_ge(ctx_loaded[s], 16 * (SEQS // 2 + 1))
                sp.wait_ge(k_loaded[s], SPREADS * (SEQS // 2 + 1 - s))
            sp.wait_ge(q_loaded, 16 * 4 * (SEQS + 1))

        @block.gpsimd
        def _(pool):
            pool.memset(v[:, :, :, D:], 0.0).then_inc(consts, 1)
            pool.memset(eps[:], EPS).then_inc(consts, 1)
            pool.memset(k4[:, :, :, KEYS:].bitcast(F32), 0.0).then_inc(consts, 1)
            pool.wait_ge(w_loaded, 16 * NUM_WB)

            def masked_q(seq, s):
                wait(pool, s_full, seq.count(HEADS))
                pool.wait_ge(q_loaded, seq.count(16 * 4, 2 * 16 * 4))
                alone(pool)
                for i in range(PAIR // HD):
                    ins = pool.tensor_scalar(
                        qm[:, s].rearrange("p (t i) n -> p i t n", i=PAIR // HD)[:, i], q4[:].bitcast(F32),
                        head_rows[:, i:i + 1], None, ALU.mult)
                ins.then_inc(qm_ready, 1)

            def after(seq):
                pool.wait_ge(inv_ready, seq.count(1))
                wait(pool, o_ready, seq.count(1, -1))
                alone(pool)
                pool.tensor_copy(inv_wide[:], inv[:].unsqueeze(2).to_broadcast([STEPS, HEADS, 32])).then_inc(wide_ready, 1)
                wait(pool, mv_ready, seq.count(1, -1))
                pool.tensor_tensor(x1b[:], x1[:, bass.ds(seq.count(1, -1), 1), :].rearrange("p a d -> p (a d)"),
                                   bo[0:STEPS], ALU.add).then_inc(x1b_ready, 1)

            def body(seq, s):
                if not first(seq):
                    after(seq)
                masked_q(seq, 1 - s)

            sequences(pool, lambda seq: masked_q(seq, 0), body, after)

        @block.scalar
        def _(act):
            act.preload_act_table_set("natural_log_exp_and_others")
            act.wait_ge(w_loaded, 16 * NUM_WB)
            act.wait_ge(consts, 2)

            def copy_k(seq, o):
                seq.wait_full(act, f"K{o}")
                if o == 0:
                    wait(act, k_stored, seq.count(STORES, STORES))
                act.activation(k_sb[:, 0, o], seq.bank(f"K{o}")[:, 0:KEYS], ACT.Identity, bias=bk[:, o:o + 1]
                               ).then_inc(k_high, 1)

            def copy_pT(seq, j):
                n, rows = len(KCH) - 1, KCH[-1][1]
                act.wait_ge(t_full, seq.count(3 * SPS, 3 * j))
                wait(act, pv_done, seq.count(SPS, j - 2))
                act.copy(pT[0:rows, (j + 1) % 2, n], t_ps[n][0:rows, 0:HG * STEPS]).then_inc(pt_scalar, 1)

            def exps(seq, s, j, with_copy):
                act.wait_ge(nmx_ready, seq.count(SPS, j + 1))
                for h in range(HG):
                    if h == HG // 2 and with_copy:
                        copy_pT(seq, j)
                    if h == HG - 1 and j < DC:
                        copy_k(seq, j)
                    ins = act.activation(prob[:, j % 2, h], prob[:, j % 2, h], ACT.Exp, bias=nmx[:, j % 2, h:h + 1],
                                         accum_out=rsum[:, s, HG * j + h:HG * j + h + 1])
                ins.then_inc(p_ready, 1)

            def copy_inv(seq):
                seq.wait_full(act, "R")
                wait(act, o_ready, seq.count(1, -1))
                seq.free(act.copy(inv_sb[:], seq.bank("R")[:, 0:HG * STEPS]), "R")

            def copy_logits(seq):
                seq.wait_full(act, "lg")
                seq.free(act.copy(lg[:, bass.ds(seq.count(1, -1), 1), :].rearrange("p a e -> p (a e)"),
                                         seq.bank("lg")[0:STEPS, 0:8]), "lg")

            def deviation(seq):
                act.wait_ge(mv_ready, seq.count(1))
                act.activation(lnv[:], mv[:, 1:2], ACT.Ln, bias=eps[0:STEPS, :]).then_inc(ln_ready, 1)
                act.wait_ge(ln_ready, seq.count(1))
                act.activation(rstd[:], lnv[:], ACT.Exp, scale=-0.5).then_inc(rstd_ready, 1)

            def body(seq, s):
                before = not first(seq)
                for j in range(SPS):
                    if j == 2 and before:
                        deviation(seq)
                    exps(seq, s, j, j or before)
                    if j == 0 and before:
                        copy_inv(seq)
                    if j == 3 and before:
                        copy_logits(seq)

            def tail(seq):
                copy_pT(seq, 0)
                copy_inv(seq)
                deviation(seq)
                copy_logits(seq)

            def lead(seq):
                for o in range(DC):
                    copy_k(seq, o)
                end.inverse_deviation(act, QUADS - 1)
                end.copy_q(act, QUADS - 1)

            sequences(act, lead, body, tail)

        @block.vector
        def _(dve):
            dve.wait_ge(w_loaded, 16 * NUM_WB)
            dve.wait_ge(consts, 2)
            dve.tensor_scalar(mask[:], mask[:], MASKED, None, ALU.mult).then_inc(mask_ready, 1)
            dve.wait_ge(mask_ready, 1)

            def copy_v(seq, s, n):
                name, rows = f"V{n}", KCH[n][1]
                seq.wait_full(dve, name)
                wait(dve, pv_done, seq.count(SPS))
                seq.free(dve.tensor_tensor(v[0:rows, s, n, 0:D], seq.bank(name)[0:rows, 0:D], bv[0:rows], ALU.add), name)

            def mask_and_max(seq, j, h):
                dve.wait_ge(s_full, seq.count(HEADS, HG * j + h + 1))
                if h == 0:
                    wait(dve, t_full, seq.count(3 * SPS, 3 * (j - 1)))
                alone(dve)
                dve.tensor_tensor_reduce(prob[:, j % 2, h], s_ps[h % 2][0:STEPS, 0:KEYS], mask[:], 1.0, -3.0e38,
                                         ALU.add, ALU.max, mx[:, j % 2, h:h + 1]).then_inc(s_taken, 1)

            def copy_pT(seq, j, n):
                dve.wait_ge(t_full, seq.count(3 * SPS, 3 * (j - 1) + n + 1))
                if n == 0:
                    wait(dve, pv_done, seq.count(SPS, j - 2))
                rows = KCH[n][1]
                dve.tensor_copy(pT[0:rows, (j + 1) % 2, n], t_ps[n][0:rows, 0:HG * STEPS]).then_inc(pt_vector, 1)

            def finish_step(seq, j, before):
                dve.wait_ge(s_taken, seq.count(HEADS, HG * (j + 1)))
                wait(dve, p_ready, seq.count(SPS, j - 1))
                dve.tensor_scalar(nmx[:, j % 2], mx[:, j % 2], -1.0, None, ALU.mult).then_inc(nmx_ready, 1)
                if j or before:
                    for n in range(2):
                        copy_pT(seq, j, n)

            def inverse_sums(seq, s):
                dve.wait_ge(p_ready, seq.count(SPS))
                wait(dve, wide_ready, seq.count(1, -1))
                dve.reciprocal(inv[:], rsum[:, s]).then_inc(inv_ready, 1)

            def normalise_o(seq):
                dve.wait_ge(pv_done, seq.count(SPS))
                seq.wait_freed(dve, "R")
                dve.tensor_tensor(oT[:].rearrange("p j t -> p (j t)"), o_ps[:, 0:HG * STEPS], inv_sb[:], ALU.mult
                                  ).then_inc(o_ready, 1)

            def residual(seq):
                seq.wait_full(dve, "proj")
                dve.wait_ge(x1b_ready, seq.count(1))
                ins = dve.tensor_tensor(res[:], seq.bank("proj")[0:STEPS, 0:D], x1b[:], ALU.add)
                seq.free(ins, "proj")
                seq.wait_freed(dve, "proj")
                dve.bn_stats(stat[:], res[:]).then_inc(stat_ready, 1)
                dve.wait_ge(stat_ready, seq.count(1))
                alone(dve)
                dve.bn_aggr(mv[:], stat[:]).then_inc(mv_ready, 1)

            def normalise(seq):
                dve.wait_ge(rstd_ready, seq.count(1))
                dve.tensor_scalar(x1[:, bass.ds(seq.count(1, -1), 1), :].rearrange("p a d -> p (a d)"), res[:],
                                  mv[:, 0:1], rstd[:], ALU.subtract, ALU.mult).then_inc(x2_kept, 1)
                dve.tensor_scalar(x2[:], res[:], mv[:, 0:1], rstd[:], ALU.subtract, ALU.mult).then_inc(x2_ready, 1)

            def copy_x2T(seq):
                seq.wait_full(dve, "xT")
                seq.free(dve.tensor_copy(x2T[:].rearrange("p c t -> p (c t)"), seq.bank("xT")[:, 0:DC * STEPS]), "xT")

            def low_k(seq, o):
                dve.wait_ge(k_high, seq.count(DC, DC + o + 1))
                ins = dve.scalar_tensor_tensor(out=k_sb[:, 1, o], in0=seq.bank(f"K{o}")[:, 0:KEYS],
                                               scalar=bk[:, o:o + 1], in1=k_sb[:, 0, o].bitcast(F32),
                                               op0=ALU.add, op1=ALU.subtract)
                seq.free(ins, f"K{o}")

            def lead(seq):
                for o in range(DC):
                    low_k(seq, o)
                for n in range(len(KCH)):
                    copy_v(seq, 0, n)
                for part in range(QS // 2):
                    end.residual(dve, QUADS - 1, part)
                end.normalise(dve, QUADS - 1)
                end.copy_x1T(dve, QUADS - 1)
                end.low_q(dve, QUADS - 1)

            def body(seq, s):
                before = not first(seq)
                for j in range(SPS):
                    mask_and_max(seq, j, 0)
                    mask_and_max(seq, j, 1)
                    if j == 0 and before:
                        inverse_sums(seq, 1 - s)
                    if j in (1, 2):
                        low_k(seq, j - 1)
                    if j == 2 and before:
                        residual(seq)
                    if j == 3:
                        copy_v(seq, 1 - s, 0)
                        copy_v(seq, 1 - s, 1)
                    mask_and_max(seq, j, 2)
                    mask_and_max(seq, j, 3)
                    finish_step(seq, j, before)
                    if j == 1 and before:
                        normalise_o(seq)
                    if j == 2 and before:
                        normalise(seq)
                    if j == 3:
                        copy_v(seq, 1 - s, 2)
                        if before:
                            copy_x2T(seq)

            def tail(seq):
                for n in range(2):
                    copy_pT(seq, 0, n)
                inverse_sums(seq, 1)
                normalise_o(seq)
                residual(seq)
                normalise(seq)
                copy_x2T(seq)

            sequences(dve, lead, body, tail)

        @block.tensor
        def _(pe):
            pe.wait_ge(w_loaded, 16 * NUM_WB)
            pe.wait_ge(consts, 3)

            def acquire(seq, name):
                _, i, before = seq.use(name)
                wait(pe, misc_free[i], before)
                return seq.bank(name)

            def keys(seq, s, o):
                if o == 0:
                    pe.wait_ge(ctx_loaded[s], half_loads(seq, s))
                bank = acquire(seq, f"K{o}")
                for c in range(DC):
                    ins = pe.matmul(bank[:, 0:KEYS], wk[:, c, o * P:(o + 1) * P], ctxT[:, s, c],
                                    start=(c == 0), stop=(c == DC - 1))
                ins.then_inc(misc_full, 1)

            def half_loads(seq, s):
                return seq.it * 16 + 16 * ((seq.s + 1) // 2 + 1)

            def values(seq, s, n):
                at, rows = KCH[n]
                bank = acquire(seq, f"V{n}")
                for c in range(DC):
                    ins = pe.matmul(bank[0:rows, 0:D], ctxT[:, s, c, at:at + rows], wv[:, c],
                                    start=(c == 0), stop=(c == DC - 1))
                ins.then_inc(misc_full, 1)

            def scores(seq, s, j, h):
                wait(pe, s_taken, seq.count(HEADS, HG * j + h - 1))
                head = HG * j + h
                pe.matmul(s_ps[h % 2][0:STEPS, 0:KEYS_EVEN], qm[:, s, head], k4[:, s, head * HD // PAIR],
                          start=True, stop=True).then_inc(s_full, 1)

            def turn(seq, j, n):
                if n == 0:
                    pe.wait_ge(p_ready, seq.count(SPS, j))
                if n < len(KCH) - 1:
                    wait(pe, pt_vector, seq.count(2 * SPS, 2 * (j - 2) + n + 1))
                else:
                    wait(pe, pt_scalar, seq.count(SPS, j - 1))
                at, rows = KCH[n]
                for h in range(HG):
                    ins = pe.transpose(t_ps[n][0:rows, h * STEPS:(h + 1) * STEPS], prob[:, (j + 1) % 2, h, at:at + rows],
                                       ident[0:STEPS, 0:STEPS])
                ins.then_inc(t_full, 1)

            def times_v(seq, s, j):
                pe.wait_ge(pt_vector, seq.count(2 * SPS, 2 * (j - 1)))
                pe.wait_ge(pt_scalar, seq.count(SPS, j - 1))
                jj = (j - 2) % SPS
                if jj == 0:
                    wait(pe, o_ready, seq.count(1))
                for h in range(HG):
                    head = HG * jj + h
                    for n, (_, rows) in enumerate(KCH):
                        ins = pe.matmul(o_ps[32 * h:32 * h + 32, jj * STEPS:(jj + 1) * STEPS],
                                        v[0:rows, s, n, head * HD:head * HD + 32],
                                        pT[0:rows, j % 2, n, h * STEPS:(h + 1) * STEPS],
                                        start=(n == 0), stop=(n == len(KCH) - 1))
                ins.then_inc(pv_done, 1)

            def spread_inv(seq):
                pe.wait_ge(wide_ready, seq.count(1))
                bank = acquire(seq, "R")
                for j in range(HG):
                    ins = pe.matmul(bank[:, j * STEPS:(j + 1) * STEPS],
                                    inv_wide[:, HG * j:HG * (j + 1)].rearrange("p h r -> p (h r)"),
                                    ident[0:STEPS, 0:STEPS], start=True, stop=True)
                ins.then_inc(misc_full, 1)

            def project(seq):
                pe.wait_ge(o_ready, seq.count(1))
                bank = acquire(seq, "proj")
                for j in range(HG):
                    ins = pe.matmul(bank[0:STEPS, 0:D], oT[:, j], wo[:, j], start=(j == 0), stop=(j == HG - 1))
                ins.then_inc(misc_full, 1)

            def turn_x2(seq):
                pe.wait_ge(x2_ready, seq.count(1))
                bank = acquire(seq, "xT")
                for c in range(DC):
                    ins = pe.transpose(bank[:, c * STEPS:(c + 1) * STEPS], x2[:, c * P:(c + 1) * P],
                                       ident[0:STEPS, 0:STEPS])
                ins.then_inc(misc_full, 1)

            def logits(seq):
                seq.wait_freed(pe, "xT")
                bank = acquire(seq, "lg")
                for c in range(DC):
                    ins = pe.matmul(bank[0:STEPS, 0:8], x2T[:, c], wg[:, c], start=(c == 0), stop=(c == DC - 1))
                ins.then_inc(misc_full, 1)

            def first_scores(seq, s):
                pe.wait_ge(k_loaded[s], half_spreads(seq))
                pe.wait_ge(qm_ready, seq.count(1, 2))
                for h in range(2):
                    scores(Seq(seq.it, seq.s + 1), s, 0, h)

            def lead(seq):
                for o in range(DC):
                    keys(seq, 0, o)
                for n in range(len(KCH)):
                    values(seq, 0, n)
                for task in last_tasks:
                    uses.acquire(pe, task)
                    ins = {"proj": end.project, "x1T": end.turn_x1, "q": end.queries}[task[0]](pe, *task[1:])
                    ins.then_inc(last_full, 1)
                first_scores(seq, 0)
                for o in range(DC):
                    uses.wait_freed(pe, ("q", QUADS - 1, o))

            def body(seq, s):
                before = not first(seq)
                Seq(seq.it, seq.s - 1).wait_freed(pe, "V2")
                for j in range(SPS):
                    if j >= 2:
                        times_v(seq, s, j)
                    elif before:
                        times_v(seq, 1 - s, j)
                    scores(seq, s, j, 2)
                    scores(seq, s, j, 3)
                    if j or before:
                        for n in range(len(KCH)):
                            turn(seq, j, n)
                    if j < SPS - 1:
                        scores(seq, s, j + 1, 0)
                        scores(seq, s, j + 1, 1)
                    if j == 0:
                        keys(seq, 1 - s, 0)
                        if before:
                            spread_inv(seq)
                    if j == 1:
                        keys(seq, 1 - s, 1)
                        if before:
                            project(seq)
                    if j == 2:
                        values(seq, 1 - s, 0)
                        values(seq, 1 - s, 1)
                    if j == 3:
                        values(seq, 1 - s, 2)
                        first_scores(seq, 1 - s)
                        if before:
                            turn_x2(seq)
                            logits(seq)

            def tail(seq):
                for n in range(len(KCH)):
                    turn(seq, 0, n)
                times_v(seq, 1, 0)
                times_v(seq, 1, 1)
                spread_inv(seq)
                project(seq)
                turn_x2(seq)
                logits(seq)

            sequences(pe, lead, body, tail)


EXPERTS, WIDTH = 8, 1024
assert SEQS == EXPERTS * DC
FC = WIDTH // P
CAPACITY = 2 * 2 * TOKENS // EXPERTS
TILES = (2 * TOKENS + EXPERTS * (P - 1)) // P
TILES_PER_EXPERT = -(-CAPACITY // P)
SLOTS = TILES * P
TRASH = SLOTS + P
XE_ROWS = TRASH + 2 * TOKENS


def stage_c(pr, x, lg, ident, w1, w1_loaded, scratch, xe, xe_cleared, ye, out):
    nc, dram = pr.nc, pr.dram
    with ExitStack() as ctx:
        def sb(*a):
            return pr.sb(ctx, *a)

        def sem(name):
            return pr.sem(ctx, name)

        w2 = sb("w2", [P, EXPERTS, FC, D])
        b1 = sb("b1", [P, FC, EXPERTS])
        b2 = sb("b2", [P, EXPERTS, D])
        R = [STEPS, SEQS, EXPERTS]
        tri = sb("tri", [STEPS, STEPS])
        ones = sb("ones", [STEPS, STEPS])
        rev = sb("rev", [STEPS, EXPERTS])
        tile_no = sb("tile_no", [STEPS, TILES + 1])
        token_no = sb("token_no", [STEPS, 2, SEQS])
        cont = sb("cont", [STEPS, EXPERTS, SEQS])
        gates = sb("gates", R)
        work = sb("work", R)
        mask = [sb(f"mask{i}", R) for i in range(2)]
        pos_all = [sb(f"pos_all{i}", R) for i in range(2)]
        total = [sb(f"total{i}", [STEPS, EXPERTS, SEQS]) for i in range(2)]
        running = [sb(f"running{i}", [STEPS, EXPERTS, SEQS]) for i in range(2)]
        top = sb("top", [STEPS, SEQS])
        row = sb("row", [STEPS, SEQS])
        gate = [sb(f"gate{i}", [STEPS, SEQS]) for i in range(2)]
        pos = sb("pos", [STEPS, 2, SEQS])
        base_of = sb("base_of", [STEPS, 2, SEQS])
        keep = sb("keep", [STEPS, 2, SEQS])
        weight = sb("weight", [STEPS, 2, SEQS])
        count = sb("count", [STEPS, EXPERTS])
        tiles = sb("tiles", [STEPS, EXPERTS])
        tile_end = sb("tile_end", [STEPS, EXPERTS])
        base = sb("base", [STEPS, EXPERTS])
        steps7 = sb("steps7", [STEPS, EXPERTS, TILES_PER_EXPERT])
        past = sb("past", [STEPS, TILES + 1, EXPERTS])
        expert_f = sb("expert_f", [STEPS, TILES + 1])
        expert = sb("expert", [STEPS, TILES + 1], I32)
        to_slot = sb("to_slot", [STEPS, 2, SEQS], U32)
        from_slot = sb("from_slot", [STEPS, 2, SEQS], U32)
        eps = sb("eps_c", [P, 1])
        b1c = sb("b1c", [P, 2, FC])
        hT = sb("hT", [P, 2, FC, P])
        flat = scratch.rearrange("p c t -> p (c t)")
        h_sb = flat[:, 0:2 * WIDTH].rearrange("p (i f) -> p i f", i=2)
        xs = flat[:, 2 * WIDTH:2 * WIDTH + 2 * D].rearrange("p (i d) -> p i d", i=2)
        xTt = flat[:, 2 * WIDTH + 2 * D:2 * WIDTH + 4 * D].rearrange("p (i c t) -> p i c t", i=2, c=DC)
        y_sb = sb("y_sb", [P, 2, D])
        picked = hT[0:STEPS].rearrange("p i c t -> p (i c t)").rearrange("p (s k d) -> p s k d", s=4, k=2)
        NPICK = 4

        x_ps = pr.psum(ctx, "x_ps", [P, 512])
        h_ps = [pr.psum(ctx, f"h_ps{i}", [P, 512]) for i in range(2)]
        hT_ps = [pr.psum(ctx, f"hT_ps{i}", [P, 512]) for i in range(2)]
        y_ps = pr.psum(ctx, "y_ps_c", [P, 512])

        w2_loaded, b_loaded, consts = sem("w2_loaded"), sem("b_loaded"), sem("consts_c")
        route_step, logit_max, gate_exp = sem("route_step"), sem("logit_max"), sem("gate_exp")
        masks_ready, prefix_full, routed = sem("masks_ready"), sem("prefix_full"), sem("routed")
        dispatched = sem("dispatched")
        xs_loaded = [sem(f"xs_loaded{i}") for i in range(2)]
        xt_full, xt_copied = sem("xt_full"), sem("xt_copied")
        h_full, h_scalar, h_vector = sem("h_full"), sem("h_scalar"), sem("h_vector")
        ht_full, bias_ready, gelu_done = sem("ht_full"), sem("bias_ready"), sem("gelu_done")
        y_full, y_ready = sem("y_full"), sem("y_ready")
        y_stored = [sem(f"y_stored{i}") for i in range(2)]
        picked_in = [sem(f"picked_in{i}") for i in range(NPICK)]
        mix_step, mixed, stat_ready, mv_ready = sem("mix_step"), sem("mixed"), sem("stat_c_ready"), sem("mv_c_ready")
        ln_ready, rstd_ready, out_ready, stored = sem("ln_c_ready"), sem("rstd_c_ready"), sem("out_ready"), sem("stored")

        class Tile:

            def __init__(self, it, s):
                self.it, self.s = it, s

            def count(self, per_tile, more=0):
                return self.it * (2 * per_tile) + (self.s * per_tile + more)

            def at(self, before=0):
                return self.count(1, -before)

        def tile_steps(eng, body):
            for s in range(2):
                body(Tile(0, s), s, (True, s == 1, False))
            with eng.Fori(1, TILES // 2) as it:
                for s in range(2):
                    body(Tile(it, s), s, (True, True, True))
            body(Tile(TILES // 2, 0), 0, (False, True, True))
            body(Tile(TILES // 2, 1), 1, (False, False, True))

        const_count = 9

        def finish(dve, s):
            dve.wait_ge(rstd_ready, s + 1)
            dve.tensor_scalar(x[:, s], x[:, s], pos_all[0][:, s, 0:1], row[:, s:s + 1],
                              ALU.subtract, ALU.mult).then_inc(out_ready, 1)

        block = ctx.enter_context(nc.Block())

        @block.sync
        def _(sp):
            sp.dma_start(b1[:], dram["b1T"]).then_inc(b_loaded, 16)
            sp.dma_start(b2[:].rearrange("p e d -> p (e d)"), dram["L0_ffn_b2"].rearrange("(a e) d -> a (e d)", a=1)
                         .partition_broadcast(P)).then_inc(b_loaded, 16)
            for e in range(EXPERTS):
                sp.dma_start(w2[:, e], dram["L0_ffn_W2"][e].rearrange("(c p) d -> p c d", p=P)).then_inc(w2_loaded, 16)

            def load(t, s):
                sp.dma_start(xs[:, s], xe[bass.ds(t * P, P), :]).then_inc(xs_loaded[s], 16)

            sp.wait_ge(dispatched, 16 * 2 * SEQS)
            load(0, 0)

            def body(tile, s, parts):
                if parts[0]:
                    wait(sp, xt_full, tile.count(1))
                    load(tile.at(-1), 1 - s)

            tile_steps(sp, body)
            for s in range(2):
                sp.wait_ge(y_stored[s], 16 * (TILES // 2 + 1))
            sp.wait_ge(xs_loaded[TILES % 2], 16 * (TILES // 2 + 1))
            for s in range(SEQS):
                sp.wait_ge(out_ready, s + 1)
                sp.dma_start(out[s], x[:, s]).then_inc(stored, 16)
            sp.wait_ge(stored, 16 * SEQS)

        @block.gpsimd
        def _(pool):
            def const(ins):
                const.made += 1
                ins.then_inc(consts, 1)
                pool.wait_ge(consts, const.made)

            const.made = 0
            const(pool.memset(ones[:], 1.0))
            const(pool.affine_select(out=tri[:], in_=ones[:], compare_op=ALU.is_gt, fill=0.0, base=0,
                                     pattern=[[1, STEPS]], channel_multiplier=-1))
            const(pool.iota(rev[:], pattern=[[-1, EXPERTS]], base=EXPERTS, channel_multiplier=0,
                            allow_small_or_imprecise_dtypes=True))
            const(pool.iota(tile_no[:], pattern=[[1, TILES + 1]], base=0, channel_multiplier=0,
                            allow_small_or_imprecise_dtypes=True))
            const(pool.iota(token_no[:], pattern=[[TOKENS, 2], [STEPS, SEQS]], base=TRASH, channel_multiplier=1,
                            allow_small_or_imprecise_dtypes=True))
            const(pool.iota(steps7[:], pattern=[[0, EXPERTS], [P, TILES_PER_EXPERT]], base=0, channel_multiplier=0,
                            allow_small_or_imprecise_dtypes=True))
            const(pool.memset(cont[:], 1.0))
            const(pool.memset(cont[:, :, 0:1], 0.0))
            const(pool.memset(eps[:], EPS))
            for s in range(2):
                pool.sem_inc(y_stored[s], 16)
            pool.wait_ge(xe_cleared, 16)
            pool.wait_ge(routed, 2)
            for k in range(2):
                for s in range(SEQS):
                    pool.indirect_dma_start(
                        out=xe[:], out_offset=bass.IndirectOffsetOnAxis(ap=to_slot[:, k, s:s + 1], axis=0),
                        in_=x[:, s], in_offset=None).then_inc(dispatched, 16)
            for s in range(2):
                pool.wait_ge(y_stored[s], 16 * (TILES // 2 + 1))
            for s in range(SEQS):
                if s >= NPICK:
                    pool.wait_ge(mixed, s - NPICK + 1)
                for k in range(2):
                    pool.indirect_dma_start(
                        out=picked[:, s % NPICK, k], out_offset=None, in_=ye[:],
                        in_offset=bass.IndirectOffsetOnAxis(ap=from_slot[:, k, s:s + 1], axis=0)
                    ).then_inc(picked_in[s % NPICK], 16)

        @block.scalar
        def _(act):
            act.wait_ge(logit_max, 1)
            act.activation(gates[:], gates[:], ACT.Exp).then_inc(gate_exp, 1)
            act.preload_act_table_set("gelu_and_others")

            def body(tile, s, parts):
                first, middle, last = parts
                if first:
                    act.wait_ge(h_full, tile.count(2, 1))
                    wait(act, ht_full, tile.count(1, -1))
                    act.copy(h_sb[:, s, 0:512], h_ps[0][:]).then_inc(h_scalar, 1)
                if middle:
                    act.wait_ge(ht_full, tile.count(1))
                    act.wait_ge(bias_ready, tile.count(1))
                    wait(act, y_full, tile.count(1, -2))
                    for c in range(FC):
                        ins = act.activation(hT[:, 1 - s, c], hT_ps[c // 4][:, (c % 4) * P:(c % 4 + 1) * P], ACT.Gelu,
                                             bias=b1c[:, 1 - s, c:c + 1])
                    ins.then_inc(gelu_done, 1)
                if last:
                    act.wait_ge(y_ready, tile.count(1, -1))
                    act.dma_start(ye[bass.ds(tile.at(2) * P, P), :], y_sb[:, s]).then_inc(y_stored[s], 16)

            tile_steps(act, body)
            act.preload_act_table_set("natural_log_exp_and_others")
            act.wait_ge(consts, const_count)
            for s in range(SEQS):
                act.wait_ge(mv_ready, s + 1)
                act.activation(top[:, s:s + 1], pos_all[0][:, s, 1:2], ACT.Ln, bias=eps[0:STEPS, :]).then_inc(ln_ready, 1)
                act.wait_ge(ln_ready, s + 1)
                act.activation(row[:, s:s + 1], top[:, s:s + 1], ACT.Exp, scale=-0.5).then_inc(rstd_ready, 1)

        @block.vector
        def _(dve):
            done = [0]

            def link(ins):
                done[0] += 1
                ins.then_inc(route_step, 1)
                dve.wait_ge(route_step, done[0])

            def over_e(a):
                return a.unsqueeze(2).to_broadcast(R)

            def over_s(a):
                return a.unsqueeze(1).to_broadcast(R)

            def by_seq(a):
                return a.rearrange("p e s -> p s e")

            def first_hot(values, largest, onehot):
                link(dve.tensor_tensor(work[:], values[:], over_e(largest[:]), ALU.is_equal))
                link(dve.tensor_tensor(work[:], work[:], over_s(rev[:]), ALU.mult))
                link(dve.tensor_reduce(row[:], work[:], AX_X, ALU.max))
                link(dve.tensor_tensor(onehot[:], over_s(rev[:]), over_e(row[:]), ALU.is_equal))

            def pick(result, onehot, values):
                link(dve.tensor_tensor(work[:], onehot[:], values, ALU.mult))
                link(dve.tensor_reduce(result, work[:], AX_X, ALU.add))

            dve.wait_ge(consts, const_count)
            link(dve.tensor_reduce(top[:], lg[:], AX_X, ALU.max))
            dve.tensor_tensor(gates[:], lg[:], over_e(top[:]), ALU.subtract).then_inc(logit_max, 1)
            dve.wait_ge(gate_exp, 1)
            link(dve.tensor_reduce(top[:], gates[:], AX_X, ALU.add))
            link(dve.reciprocal(top[:], top[:]))
            link(dve.tensor_tensor(gates[:], gates[:], over_e(top[:]), ALU.mult))
            link(dve.tensor_reduce(gate[0][:], gates[:], AX_X, ALU.max))
            first_hot(gates, gate[0], mask[0])
            link(dve.scalar_tensor_tensor(out=lg[:], in0=mask[0][:], scalar=-3.0e38, in1=lg[:],
                                          op0=ALU.mult, op1=ALU.add))
            link(dve.tensor_reduce(top[:], lg[:], AX_X, ALU.max))
            first_hot(lg, top, mask[1])
            dve.sem_inc(masks_ready, 1)
            pick(gate[1][:], mask[1], gates[:])
            link(dve.scalar_tensor_tensor(out=top[:], in0=gate[0][:], scalar=1e-9, in1=gate[1][:],
                                          op0=ALU.add, op1=ALU.add))
            link(dve.reciprocal(top[:], top[:]))
            for k in range(2):
                link(dve.tensor_tensor(weight[:, k], gate[k][:], top[:], ALU.mult))
            dve.wait_ge(prefix_full, 1)
            for k in range(2):
                tot = h_ps[k][0:STEPS, SEQS * EXPERTS:2 * SEQS * EXPERTS].rearrange("p (s e) -> p e s", e=EXPERTS)
                link(dve.tensor_copy(total[k][:], tot))
                link(dve.tensor_tensor_scan(running[k][:].rearrange("p e s -> p (e s)"),
                                            cont[:].rearrange("p e s -> p (e s)"),
                                            total[k][:].rearrange("p e s -> p (e s)"), 0.0, ALU.mult, ALU.add))
                within = h_ps[k][0:STEPS, 0:SEQS * EXPERTS].rearrange("p (s e) -> p s e", e=EXPERTS)
                link(dve.tensor_tensor(pos_all[k][:], within, by_seq(running[k][:]), ALU.add))
                link(dve.tensor_tensor(pos_all[k][:], pos_all[k][:], by_seq(total[k][:]), ALU.subtract))
            all_first = running[0][:, :, SEQS - 1]
            link(dve.tensor_tensor(pos_all[1][:], pos_all[1][:], over_s(all_first), ALU.add))
            link(dve.tensor_tensor(count[:], all_first, running[1][:, :, SEQS - 1], ALU.add))
            link(dve.tensor_scalar(count[:], count[:], float(CAPACITY), None, ALU.min))
            link(dve.tensor_tensor(steps7[:], count[:].unsqueeze(2).to_broadcast([STEPS, EXPERTS, TILES_PER_EXPERT]),
                                   steps7[:], ALU.is_gt))
            link(dve.tensor_reduce(tiles[:], steps7[:], AX_X, ALU.add))
            link(dve.tensor_tensor_scan(tile_end[:], ones[:, 0:EXPERTS], tiles[:], 0.0, ALU.mult, ALU.add))
            link(dve.tensor_tensor(base[:], tile_end[:], tiles[:], ALU.subtract))
            link(dve.tensor_scalar(base[:], base[:], float(P), None, ALU.mult))
            for k in range(2):
                pick(pos[:, k], mask[k], pos_all[k][:])
                pick(base_of[:, k], mask[k], over_s(base[:]))
            link(dve.tensor_scalar(keep[:], pos[:], float(CAPACITY), None, ALU.is_lt))
            link(dve.tensor_tensor(weight[:], weight[:], keep[:], ALU.mult))
            link(dve.tensor_tensor(pos[:], pos[:], base_of[:], ALU.add))
            link(dve.tensor_tensor(pos[:], pos[:], token_no[:], ALU.subtract))
            link(dve.tensor_tensor(base_of[:], pos[:], keep[:], ALU.mult))
            link(dve.tensor_tensor(base_of[:], base_of[:], token_no[:], ALU.add))
            dve.tensor_copy(to_slot[:], base_of[:]).then_inc(routed, 1)
            link(dve.tensor_tensor(pos[:], pos[:], token_no[:], ALU.add))
            link(dve.tensor_tensor(pos[:], pos[:], keep[:], ALU.mult))
            dve.tensor_copy(from_slot[:], pos[:]).then_inc(routed, 1)
            shape = [STEPS, TILES + 1, EXPERTS]
            link(dve.tensor_tensor(past[:], tile_end[:].unsqueeze(1).to_broadcast(shape),
                                   tile_no[:].unsqueeze(2).to_broadcast(shape), ALU.is_le))
            link(dve.tensor_reduce(expert_f[:], past[:], AX_X, ALU.add))
            link(dve.tensor_scalar(expert_f[:], expert_f[:], float(EXPERTS - 1), None, ALU.min))
            dve.tensor_copy(expert[:], expert_f[:]).then_inc(routed, 1)
            dve.wait_ge(routed, 3)
            dve.wait_ge(b_loaded, 32)

            def copy_xT(tile, s):
                dve.wait_ge(xt_full, tile.count(1, 1))
                wait(dve, h_full, tile.count(2, -2))
                dve.tensor_copy(xTt[:, s].rearrange("p c t -> p (c t)"), x_ps[:, 0:DC * P]).then_inc(xt_copied, 1)

            copy_xT(Tile(0, 0), 0)

            def body(tile, s, parts):
                first, _, last = parts
                if first:
                    e = dve.value_load(expert[0:1, bass.ds(tile.at(), 1)], min_val=0, max_val=EXPERTS - 1)
                    wait(dve, gelu_done, tile.count(1, -1))
                    dve.tensor_copy(b1c[:, s], b1[:, :, bass.ds(e, 1)].rearrange("p c a -> p (c a)")
                                    ).then_inc(bias_ready, 1)
                    dve.wait_ge(h_full, tile.count(2, 2))
                    wait(dve, ht_full, tile.count(1, -1))
                    dve.tensor_copy(h_sb[:, s, 512:], h_ps[1][:]).then_inc(h_vector, 1)
                    copy_xT(Tile(tile.it, tile.s + 1), 1 - s)
                if last:
                    e = dve.value_load(expert[0:1, bass.ds(tile.at(2), 1)], min_val=0, max_val=EXPERTS - 1)
                    dve.wait_ge(y_full, tile.count(1, -1))
                    dve.wait_ge(y_stored[s], (tile.it + tile.s // 2) * 16)
                    dve.tensor_tensor(y_sb[:, s], y_ps[:, 0:D], b2[:, bass.ds(e, 1)].rearrange("p a d -> p (a d)"),
                                      ALU.add).then_inc(y_ready, 1)

            tile_steps(dve, body)

            for s in range(SEQS):
                dve.wait_ge(picked_in[s % NPICK], 32 * (s // NPICK + 1))
                dve.scalar_tensor_tensor(out=x[:, s], in0=picked[:, s % NPICK, 0], scalar=weight[:, 0, s:s + 1],
                                         in1=x[:, s], op0=ALU.mult, op1=ALU.add).then_inc(mix_step, 1)
                dve.wait_ge(mix_step, s + 1)
                dve.scalar_tensor_tensor(out=x[:, s], in0=picked[:, s % NPICK, 1], scalar=weight[:, 1, s:s + 1],
                                         in1=x[:, s], op0=ALU.mult, op1=ALU.add).then_inc(mixed, 1)
                dve.wait_ge(mixed, s + 1)
                dve.bn_stats(gates[:, s, 0:6], x[:, s]).then_inc(stat_ready, 1)
                dve.wait_ge(stat_ready, s + 1)
                dve.bn_aggr(pos_all[0][:, s, 0:2], gates[:, s, 0:6]).then_inc(mv_ready, 1)
                if s:
                    finish(dve, s - 1)
            finish(dve, SEQS - 1)

        @block.tensor
        def _(pe):
            pe.wait_ge(masks_ready, 1)
            for k in range(2):
                flat_mask = mask[k][:].rearrange("p s e -> p (s e)")
                pe.matmul(h_ps[k][0:STEPS, 0:SEQS * EXPERTS], tri[:], flat_mask, start=True, stop=True)
                ins = pe.matmul(h_ps[k][0:STEPS, SEQS * EXPERTS:2 * SEQS * EXPERTS], ones[:], flat_mask,
                                start=True, stop=True)
            ins.then_inc(prefix_full, 1)
            pe.wait_ge(routed, 3)
            pe.wait_ge(w1_loaded, 16 * EXPERTS * DC)

            def turn_x(tile, s):
                pe.wait_ge(xs_loaded[s], tile.it * 16 + 16 * (tile.s // 2 + 1))
                wait(pe, xt_copied, tile.count(1))
                for c in range(DC):
                    ins = pe.transpose(x_ps[:, c * P:(c + 1) * P], xs[:, s, c * P:(c + 1) * P], ident[:])
                ins.then_inc(xt_full, 1)

            turn_x(Tile(0, 0), 0)

            def body(tile, s, parts):
                first, middle, last = parts
                if first:
                    e = pe.value_load(expert[0:1, bass.ds(tile.at(), 1)], min_val=0, max_val=EXPERTS - 1)
                    pe.wait_ge(xt_copied, tile.count(1, 1))
                    wait(pe, h_scalar, tile.count(1))
                    wait(pe, h_vector, tile.count(1))
                    for half in range(2):
                        for c in range(DC):
                            ins = pe.matmul(h_ps[half][:], xTt[:, s, c],
                                            w1[:, bass.ds(e, 1), c, half * 512:(half + 1) * 512].rearrange("p a f -> p (a f)"),
                                            start=(c == 0), stop=(c == DC - 1))
                        ins.then_inc(h_full, 1)
                    turn_x(Tile(tile.it, tile.s + 1), 1 - s)
                if middle:
                    pe.wait_ge(h_scalar, tile.count(1))
                    pe.wait_ge(h_vector, tile.count(1))
                    wait(pe, gelu_done, tile.count(1, -1))
                    for c in range(FC):
                        ins = pe.transpose(hT_ps[c // 4][:, (c % 4) * P:(c % 4 + 1) * P],
                                           h_sb[:, 1 - s, c * P:(c + 1) * P], ident[:])
                    ins.then_inc(ht_full, 1)
                if last:
                    e = pe.value_load(expert[0:1, bass.ds(tile.at(2), 1)], min_val=0, max_val=EXPERTS - 1)
                    pe.wait_ge(gelu_done, tile.count(1, -1))
                    wait(pe, y_ready, tile.count(1, -2))
                    for c in range(FC):
                        ins = pe.matmul(y_ps[:, 0:D], hT[:, s, c],
                                        w2[:, bass.ds(e, 1), c, :].rearrange("p a d -> p (a d)"),
                                        start=(c == 0), stop=(c == FC - 1))
                    ins.then_inc(y_full, 1)

            pe.wait_ge(w2_loaded, 16 * EXPERTS)
            tile_steps(pe, body)


def program(nc, dram, out):
    pr = Program(nc, dram)
    with ExitStack() as ctx:
        ident = pr.sb(ctx, "ident", [P, P])
        x1 = pr.sb(ctx, "x1", [STEPS, SEQS, D])
        w1 = pr.sb(ctx, "w1", [P, EXPERTS, DC, WIDTH])
        early = pr.sb(ctx, "early", [P, EARLY])
        shared = Shared(w1[:].rearrange("p e c f -> p (e c f)"), early[:])
        lg = pr.sb(ctx, "lg", [STEPS, SEQS, EXPERTS])
        xe = nc.dram_tensor("xe", (XE_ROWS, D), F32, kind="Internal").ap()
        ye = nc.dram_tensor("ye", (SLOTS, D), F32, kind="Internal").ap()
        q_parts = nc.dram_tensor("q_parts", (2, D, TOKENS), F32, kind="Internal").ap()
        k_parts = nc.dram_tensor("k_parts", (2, 2, D, KEYS), F32, kind="Internal").ap()
        q_stored = pr.sem(ctx, "q_stored")
        xe_cleared, w1_loaded = pr.sem(ctx, "xe_cleared"), pr.sem(ctx, "w1_loaded")
        wb_loaded, ctx_loaded = pr.sem(ctx, "wb_loaded"), [pr.sem(ctx, f"ctx_loaded{i}") for i in range(2)]
        stage_a(pr, x1, shared, q_parts, q_stored, ident, xe, xe_cleared, wb_loaded, ctx_loaded)
        stage_b(pr, x1, shared, q_parts, q_stored, k_parts, ident, lg, w1, w1_loaded, wb_loaded, ctx_loaded)
        scratch = pr.sb(ctx, "scratch", [P, DC, TOKENS])
        stage_c(pr, x1, lg, ident, w1, w1_loaded, scratch[:], xe, xe_cleared, ye, out)


def kernel(**inputs):
    import numpy as np
    import concourse.bacc as bacc
    from concourse.bass_utils import run_bass_kernel_spmd

    a = {k: np.asarray(v) for k, v in inputs.items()}

    def columns(v):
        return v.reshape(-1, P, *v.shape[1:]).swapaxes(0, 1)

    laid = dict(
        xT=a["x"].reshape(TOKENS, D).T,
        ctxT=a["ctx_1024"].transpose(0, 2, 1),
        w_inT=a["L0_attn_w_in"].T,
        lora_B_inT=a["L0_attn_lora_B_in"].T,
        lora_B_outT=a["L0_attn_lora_B_out"].T,
        w_xprojT=a["L0_attn_w_xproj"].T,
        w_dtT=a["L0_attn_w_dt"].T,
        w_outT=a["L0_attn_w_out"].T,
        conv_w=columns(a["L0_attn_conv_w"].reshape(INNER, TAPS)),
        conv_b=columns(a["L0_attn_conv_b"]),
        b_dt=columns(a["L0_attn_b_dt"]),
        Dp=columns(a["L0_attn_Dp"]),
        A_log=columns(a["L0_attn_A_log"]),
        bq=columns(a["L0_xattn_bq"]),
        bk=columns(a["L0_xattn_bk"]),
        head_rows=(np.arange(P)[:, None] % PAIR // HD == np.arange(PAIR // HD)).astype(np.float32),
        b1T=columns(a["L0_ffn_b1"].T),
    )
    for name in ("x", "mask_1x1xSxS2_fk1", "L0_attn_lora_A_in", "L0_attn_lora_A_out", "L0_attn_mask_in",
                 "L0_attn_mask_out", "L0_xattn_wq", "L0_xattn_wk", "L0_xattn_wv", "L0_xattn_wo",
                 "L0_xattn_bv", "L0_xattn_bo", "L0_ffn_Wg", "L0_ffn_W1", "L0_ffn_W2", "L0_ffn_b2"):
        laid[name] = a[name]
    laid = {k: np.ascontiguousarray(v) for k, v in laid.items()}
    nc = bacc.Bacc("TRN2", target_bir_lowering=False, num_devices=1)
    dram = {k: nc.dram_tensor(f"in_{k}", v.shape, mybir.dt.from_np(v.dtype), kind="ExternalInput").ap()
            for k, v in laid.items()}
    out = nc.dram_tensor("out_0", (SEQS, STEPS, D), F32, kind="ExternalOutput").ap()
    program(nc, dram, out)
    r = run_bass_kernel_spmd(nc, [{f"in_{k}": v for k, v in laid.items()}], core_ids=[0])
    return r.results[0]["out_0"]
```
